# Optimizing a Trainium2 kernel written in Bass

```python
import numpy as np
import jax
import jax.numpy as jnp

def _softmax(x, axis=-1):
    return jax.nn.softmax(x, axis=axis)

def _gelu(x):
    return jax.nn.gelu(x, approximate=True)

def _silu(x):
    return jax.nn.silu(x)

def _sigmoid(x):
    return jax.nn.sigmoid(x)

def _layernorm(x, axis=-1, eps=1e-05):
    m = jnp.mean(x, axis=axis, keepdims=True)
    v = jnp.var(x, axis=axis, keepdims=True)
    return (x - m) / jnp.sqrt(v + eps)

def _scatter_add(tgt, idx, src, axis=0):
    return tgt.at[idx].add(src)

def _segment_sum(src, seg, n):
    return jax.ops.segment_sum(src, seg, n)
kernel_name = 'mk_seq_postln_d1_jaxref_r4_b9f589'

def setup_inputs(seed: int=0):
    np.random.seed(seed)
    _w = jnp.asarray

    def _L0_attn_setup():
        import jax, jax.numpy as jnp
        import numpy as np
        DIM = 256
        D_STATE = 16
        D_CONV = 4
        EXPAND = 2
        D_INNER = EXPAND * DIM

        def _mamba_forward(x, W_in, conv_w, conv_b, W_x, W_dt, b_dt, A_log, D, W_out):
            b, seq_len, _ = x.shape
            x_and_res = x @ W_in.T
            xp, res = jnp.split(x_and_res, 2, axis=-1)
            xc = jnp.swapaxes(xp, 1, 2)
            xc = jax.lax.conv_general_dilated(xc, conv_w, window_strides=(1,), padding=[(D_CONV - 1, 0)], dimension_numbers=('NCH', 'OIH', 'NCH'), feature_group_count=D_INNER)
            xc = xc + conv_b[None, :, None]
            xc = jnp.swapaxes(xc, 1, 2)
            xc = jax.nn.silu(xc)
            ssm = xc @ W_x.T
            B = ssm[..., :D_STATE]
            C = ssm[..., D_STATE:2 * D_STATE]
            dt = ssm[..., 2 * D_STATE:]
            dt = jax.nn.softplus(dt @ W_dt.T + b_dt)
            A = -jnp.exp(A_log)

            def step(h, inp):
                xt, dt_t, B_t, C_t = inp
                A_disc = jnp.exp(A[None, None, :] * dt_t[:, :, None])
                h = A_disc * h + dt_t[:, :, None] * B_t[:, None, :] * xt[:, :, None]
                y_t = jnp.einsum('bed,bd->be', h, C_t) + D * xt
                return (h, y_t)
            h0 = jnp.zeros((b, D_INNER, D_STATE), dtype=x.dtype)
            xs = (jnp.swapaxes(xc, 0, 1), jnp.swapaxes(dt, 0, 1), jnp.swapaxes(B, 0, 1), jnp.swapaxes(C, 0, 1))
            _, ys = jax.lax.scan(step, h0, xs)
            y = jnp.swapaxes(ys, 0, 1)
            y = jax.nn.silu(y + res)
            return y @ W_out.T
        key = jax.random.key(seed)
        ks = jax.random.split(key, 9)
        b, seq = (2, 512)
        s = lambda k, shape, fan: jax.random.normal(k, shape, dtype=jnp.float32) * (1.0 / np.sqrt(fan))
        x = jax.random.normal(ks[0], (b, seq, DIM), dtype=jnp.float32)
        W_in = s(ks[1], (2 * D_INNER, DIM), DIM)
        conv_w = s(ks[2], (D_INNER, 1, D_CONV), D_CONV)
        conv_b = jnp.zeros((D_INNER,), dtype=jnp.float32)
        W_x = s(ks[3], (2 * D_STATE + 1, D_INNER), D_INNER)
        W_dt = s(ks[4], (D_INNER, 1), 1)
        b_dt = jnp.zeros((D_INNER,), dtype=jnp.float32)
        A_log = jnp.log(jnp.arange(1, D_STATE + 1, dtype=jnp.float32))
        D = jnp.ones((D_INNER,), dtype=jnp.float32)
        W_out = s(ks[5], (DIM, D_INNER), D_INNER)
        return {'x': x, 'W_in': W_in, 'conv_w': conv_w, 'conv_b': conv_b, 'W_x': W_x, 'W_dt': W_dt, 'b_dt': b_dt, 'A_log': A_log, 'D': D, 'W_out': W_out}
    _L0_attn_in = _L0_attn_setup()

    def _L0_ffn_setup():
        import jax, jax.numpy as jnp
        import numpy as np
        TOP_K = 2
        key = jax.random.key(seed)
        ks = jax.random.split(key, 5)
        B, N, C, FF, E = (2, 512, 256, 1024, 8)
        x = jax.random.normal(ks[0], (B, N, C), dtype=jnp.float32)
        router_w = jax.random.normal(ks[1], (E, C), dtype=jnp.float32) * 0.02
        lim1 = np.sqrt(6.0 / (FF + C))
        expert_w1 = jax.random.uniform(ks[2], (E, FF, C), dtype=jnp.float32, minval=-lim1, maxval=lim1)
        expert_b1 = jnp.zeros((E, FF), dtype=jnp.float32)
        expert_w2 = jax.random.uniform(ks[3], (E, C, FF), dtype=jnp.float32, minval=-lim1, maxval=lim1)
        expert_b2 = jnp.zeros((E, C), dtype=jnp.float32)
        return {'x': x, 'router_w': router_w, 'expert_w1': expert_w1, 'expert_b1': expert_b1, 'expert_w2': expert_w2, 'expert_b2': expert_b2}
    _L0_ffn_in = _L0_ffn_setup()
    _d = {'L0_attn_x': _L0_attn_in['x'], 'L0_attn_W_in': _L0_attn_in['W_in'], 'L0_attn_conv_w': _L0_attn_in['conv_w'], 'L0_attn_conv_b': _L0_attn_in['conv_b'], 'L0_attn_W_x': _L0_attn_in['W_x'], 'L0_attn_W_dt': _L0_attn_in['W_dt'], 'L0_attn_b_dt': _L0_attn_in['b_dt'], 'L0_attn_A_log': _L0_attn_in['A_log'], 'L0_attn_D': _L0_attn_in['D'], 'L0_attn_W_out': _L0_attn_in['W_out'], 'L0_ffn_router_w': _L0_ffn_in['router_w'], 'L0_ffn_expert_w1': _L0_ffn_in['expert_w1'], 'L0_ffn_expert_b1': _L0_ffn_in['expert_b1'], 'L0_ffn_expert_w2': _L0_ffn_in['expert_w2'], 'L0_ffn_expert_b2': _L0_ffn_in['expert_b2']}
    _x0 = _d['L0_attn_x']
    _d['L0_attn_x'] = jax.random.normal(jax.random.fold_in(jax.random.key(seed), 1), (4, 1024, 256), dtype=_x0.dtype)
    del _x0
    return _d

def reference(L0_attn_x, L0_attn_W_in, L0_attn_conv_w, L0_attn_conv_b, L0_attn_W_x, L0_attn_W_dt, L0_attn_b_dt, L0_attn_A_log, L0_attn_D, L0_attn_W_out, L0_ffn_router_w, L0_ffn_expert_w1, L0_ffn_expert_b1, L0_ffn_expert_w2, L0_ffn_expert_b2):

    def _L0_attn_ref(x, W_in, conv_w, conv_b, W_x, W_dt, b_dt, A_log, D, W_out):
        import jax, jax.numpy as jnp
        import numpy as np
        DIM = 256
        D_STATE = 16
        D_CONV = 4
        EXPAND = 2
        D_INNER = EXPAND * DIM

        def _mamba_forward(x, W_in, conv_w, conv_b, W_x, W_dt, b_dt, A_log, D, W_out):
            b, seq_len, _ = x.shape
            x_and_res = x @ W_in.T
            xp, res = jnp.split(x_and_res, 2, axis=-1)
            xc = jnp.swapaxes(xp, 1, 2)
            xc = jax.lax.conv_general_dilated(xc, conv_w, window_strides=(1,), padding=[(D_CONV - 1, 0)], dimension_numbers=('NCH', 'OIH', 'NCH'), feature_group_count=D_INNER)
            xc = xc + conv_b[None, :, None]
            xc = jnp.swapaxes(xc, 1, 2)
            xc = jax.nn.silu(xc)
            ssm = xc @ W_x.T
            B = ssm[..., :D_STATE]
            C = ssm[..., D_STATE:2 * D_STATE]
            dt = ssm[..., 2 * D_STATE:]
            dt = jax.nn.softplus(dt @ W_dt.T + b_dt)
            A = -jnp.exp(A_log)

            def step(h, inp):
                xt, dt_t, B_t, C_t = inp
                A_disc = jnp.exp(A[None, None, :] * dt_t[:, :, None])
                h = A_disc * h + dt_t[:, :, None] * B_t[:, None, :] * xt[:, :, None]
                y_t = jnp.einsum('bed,bd->be', h, C_t) + D * xt
                return (h, y_t)
            h0 = jnp.zeros((b, D_INNER, D_STATE), dtype=x.dtype)
            xs = (jnp.swapaxes(xc, 0, 1), jnp.swapaxes(dt, 0, 1), jnp.swapaxes(B, 0, 1), jnp.swapaxes(C, 0, 1))
            _, ys = jax.lax.scan(step, h0, xs)
            y = jnp.swapaxes(ys, 0, 1)
            y = jax.nn.silu(y + res)
            return y @ W_out.T
        return _mamba_forward(x, W_in, conv_w, conv_b, W_x, W_dt, b_dt, A_log, D, W_out)

    def _L0_ffn_ref(x, router_w, expert_w1, expert_b1, expert_w2, expert_b2):
        import jax, jax.numpy as jnp
        import numpy as np
        TOP_K = 2
        router_logits = jnp.einsum('bnc,ec->bne', x, router_w)
        router_probs = jax.nn.softmax(router_logits, axis=-1)
        expert_weights, expert_idx = jax.lax.top_k(router_probs, TOP_K)
        expert_weights = expert_weights / (expert_weights.sum(axis=-1, keepdims=True) + 1e-09)
        h = jnp.einsum('bnc,efc->bnef', x, expert_w1) + expert_b1
        h = jax.nn.gelu(h, approximate=False)
        out_all = jnp.einsum('bnef,ecf->bnec', h, expert_w2) + expert_b2
        out_k = jnp.take_along_axis(out_all, expert_idx[..., None], axis=2)
        return (out_k * expert_weights[..., None]).sum(axis=2)
    x = L0_attn_x
    x = _layernorm(x + _L0_attn_ref(x, L0_attn_W_in, L0_attn_conv_w, L0_attn_conv_b, L0_attn_W_x, L0_attn_W_dt, L0_attn_b_dt, L0_attn_A_log, L0_attn_D, L0_attn_W_out), axis=-1)
    x = _layernorm(x + _L0_ffn_ref(x, L0_ffn_router_w, L0_ffn_expert_w1, L0_ffn_expert_b1, L0_ffn_expert_w2, L0_ffn_expert_b2), axis=-1)
    return x

_drawn_inputs = setup_inputs


def setup_inputs(seed=0):
    import zlib

    import numpy as np

    out = dict(_drawn_inputs(seed))
    spreads = {'L0_attn_conv_b': (0.0, 0.1),
     'L0_attn_b_dt': (0.0, 0.1),
     'L0_attn_D': (1.0, 0.2),
     'L0_ffn_expert_b1': (0.0, 0.1),
     'L0_ffn_expert_b2': (0.0, 0.1)}
    factors = {}
    for name, (base, spread) in spreads.items():
        noise = np.random.default_rng([zlib.crc32(name.encode()), seed]).standard_normal(out[name].shape)
        drawn = base * np.exp(spread * noise) if base else spread * noise
        out[name] = jnp.asarray(drawn.astype(out[name].dtype))
    for name, factor in factors.items():
        out[name] = (out[name] * factor).astype(out[name].dtype)
    return out
```

```python
from contextlib import ExitStack

import numpy as np
import concourse.bass as bass
from concourse import mybir

ALU = mybir.AluOpType
ACT = mybir.ActivationFunctionType
AXX = mybir.AxisListType.X
F32 = mybir.dt.float32
I32 = mybir.dt.int32
U32 = mybir.dt.uint32

P = 128
SEQS, SEQ, DIM = 4, 1024, 256
INNER, STATE, TAPS = 512, 16, 4
FF, EXPERTS, TOPK = 1024, 8, 2
TOKENS = SEQS * SEQ

T = 512
BLOCKS = TOKENS // T
HALVES = SEQ // T
KC = DIM // P
EC = INNER // P
TT = T // P
ROW = DIM + 4
REGION = TOKENS + P
SLOTS = TOKENS * TOPK // P + EXPERTS
TRASH = TOKENS * TOPK
EPS = 1e-5

S_RING = 4
P_RING = 4
BC_RING = 4
DA_RING = 2
POOL_DBX = [1] * STATE
POOL_HC = [0] * STATE


def hold(eng, held):
    eng.sem_inc(held, 1)


def setup(nc, d, t):
    with ExitStack() as ctx:
        loaded = ctx.enter_context(nc.semaphore("setup_loaded"))
        pool_done = ctx.enter_context(nc.semaphore("setup_pool"))
        exp_done = ctx.enter_context(nc.semaphore("setup_exp"))
        dve_done = ctx.enter_context(nc.semaphore("setup_dve"))
        block = ctx.enter_context(nc.Block())
        loads = [(t.w_in, d.w_in.rearrange("(k p) n -> p k n", p=P)),
                 (t.conv_w, d.conv_w), (t.conv_b, d.conv_b),
                 (t.w_x, d.w_x.rearrange("(c p) n -> p c n", p=P)),
                 (t.w_dt, d.w_dt), (t.b_dt, d.b_dt),
                 (t.neg_a, d.a_log.partition_broadcast(P)),
                 (t.d_col, d.d_skip),
                 (t.w_out, d.w_out.rearrange("(c p) n -> p c n", p=P)),
                 (t.router, d.router.rearrange("(k p) n -> p k n", p=P))]

        @block.sync
        def _(sp):
            for dst, src in loads:
                sp.dma_start(dst[:], src).then_inc(loaded, 16)

        @block.gpsimd
        def _(pool):
            nc.gpsimd.memset(t.ident[:], 0.0).then_inc(pool_done, 1)
            nc.gpsimd.memset(t.before[:], 1.0).then_inc(pool_done, 1)
            nc.gpsimd.memset(t.ones[:], 1.0).then_inc(pool_done, 1)
            nc.gpsimd.memset(t.minus_half[:], -0.5).then_inc(pool_done, 1)
            nc.gpsimd.iota(t.iota_e[:], pattern=[[1, EXPERTS]], base=0, channel_multiplier=0).then_inc(pool_done, 1)
            nc.gpsimd.iota(t.iota_t[:], pattern=[[2 * P, TT]], base=0, channel_multiplier=2).then_inc(pool_done, 1)
            pool.wait_ge(pool_done, 6)
            nc.gpsimd.affine_select(out=t.ident[:], in_=t.ident[:], compare_op=ALU.not_equal, fill=1.0, base=0,
                                    pattern=[[-1, P]], channel_multiplier=1).then_inc(pool_done, 1)
            nc.gpsimd.affine_select(out=t.before[:], in_=t.before[:], compare_op=ALU.is_gt, fill=0.0, base=0,
                                    pattern=[[1, P]], channel_multiplier=-1).then_inc(pool_done, 1)

        @block.scalar
        def _(act):
            act.wait_ge(loaded, 16 * len(loads))
            nc.scalar.activation(t.neg_a[:], t.neg_a[:], ACT.Exp).then_inc(exp_done, 1)

        @block.vector
        def _(dve):
            nc.vector.memset(t.zeros[:], 0.0)
            nc.vector.memset(t.base[:], 0.0)
            for k in range(DA_RING):
                nc.vector.memset(t.decay[:, k, :, 0:1], 0.0)
            dve.wait_ge(pool_done, 8)
            nc.vector.tensor_copy(t.iota_ef[:], t.iota_e[:])
            nc.vector.tensor_copy(t.token2[:], t.iota_t[:])
            dve.wait_ge(exp_done, 1)
            nc.vector.tensor_scalar(t.neg_a[:], t.neg_a[:], -1.0, None, ALU.mult)
            for c in range(EC):
                nc.vector.tensor_scalar(t.diag_d[:, c, :], t.ident[:], t.d_col[:, c:c + 1], None, ALU.mult)
            nc.vector.memset(t.xp[:, :, T:T + TAPS - 1], 0.0).then_inc(dve_done, 1)
            dve.wait_ge(dve_done, 1)


def mamba(nc, d, t):
    with ExitStack() as ctx:
        def sb(name, shape, dt=F32):
            return ctx.enter_context(nc.sbuf_tensor(name, shape, dt))

        def ps(name, shape):
            return ctx.enter_context(nc.psum_tensor(name, shape, F32))

        def sem(name):
            return ctx.enter_context(nc.semaphore(name))

        x_t = sb("x_t", [P, 2, KC, T])
        x_tok = sb("x_tok", [P, TT, DIM])
        xc = sb("xc", [P, 2, EC, T])
        dt = sb("dt", [P, 2, EC, T])
        u = sb("u", [P, 2, EC, T])
        ssm = sb("ssm", [1 + 2 * STATE, T])
        scan = sb("scan", [P, S_RING, EC, T + 1])
        prod = sb("prod", [P, P_RING, EC, T])
        bc = sb("bc", [P, BC_RING, 2, T])
        carry = sb("carry", [P, STATE, EC])
        ys = sb("ys", [P, EC, T])
        xrow = sb("xrow", [P, 2, TT, ROW])
        x1_t = sb("x1_t", [P, TT, KC, P])
        stats = sb("stats", [P, TT, 6])
        mv = sb("mv", [P, TT, 2])
        var = sb("var", [P, TT])
        rstd = sb("rstd", [P, TT])
        logit = sb("logit", [P, TT, EXPERTS])
        ex = sb("ex", [P, TT, EXPERTS])
        mx = sb("mx", [P, TT])
        prob = sb("prob", [P, TT, EXPERTS])
        top = sb("top", [P, TT, 8])
        idx = sb("idx", [P, TT, 8], U32)
        wk = sb("wk", [P, TT, TOPK])
        ek = sb("ek", [P, TT, TOPK])
        onehot = sb("onehot", [P, TT, TOPK, EXPERTS])
        member = sb("member", [P, TT, EXPERTS])
        rank = sb("rank", [P, TT, EXPERTS])
        rsel = sb("rsel", [P, TT, TOPK, EXPERTS])
        rk = sb("rk", [P, TT, TOPK])
        pos = sb("pos", [P, 2, TT, TOPK], U32)

        y_ps = ps("y_ps", [P, EC, T])
        in_ps = ps("in_ps", [P, 2, T])
        aux_ps = ps("aux_ps", [P, T])
        out_ps = ps("out_ps", [P, 2, DIM])

        xt_loaded = [sem(f"xt_loaded{k}") for k in range(2)]
        xtok_loaded = sem("xtok_loaded")
        inproj_done = sem("inproj_done")
        halo_done = sem("halo_done")
        xp_done = sem("xp_done")
        tap_done = sem("tap_done")
        silu_done = sem("silu_done")
        ssm_ps_done = sem("ssm_ps_done")
        ssm_done = sem("ssm_done")
        bc_stored = sem("bc_stored")
        bc_loaded = [sem(f"bc_loaded{k}") for k in range(BC_RING)]
        z_done = sem("z_done")
        z_read = sem("z_read")
        ln_done = sem("ln_done")
        dt_done = sem("dt_done")
        u_done = sem("u_done")
        carried_in = sem("carried_in")
        carried_out = sem("carried_out")
        decay_done = sem("decay_done")
        dbx_pool, dbx_dve = sem("dbx_pool"), sem("dbx_dve")
        hc_pool, hc_dve = sem("hc_pool"), sem("hc_dve")
        scan_done = sem("scan_done")
        sum_done = sem("sum_done")
        ys_done = sem("ys_done")
        outproj_done = sem("outproj_done")
        pre_done = sem("pre_done")
        stats_done = sem("stats_done")
        norm_chain = sem("norm_chain")
        rstd_done = sem("rstd_done")
        x1_done = sem("x1_done")
        x1_stored = [sem(f"x1_stored{k}") for k in range(2)]
        turned = sem("turned")
        turned_read = sem("turned_read")
        logit_ps_done = sem("logit_ps_done")
        logit_done = sem("logit_done")
        route = sem("route")
        shifted = sem("shifted")
        place_chain = sem("place_chain")
        ex_done = sem("ex_done")
        member_done = sem("member_done")
        rank_ps_done = sem("rank_ps_done")
        rank_read = sem("rank_read")
        pos_done = sem("pos_done")
        rows_sent = [sem(f"rows_sent{k}") for k in range(2)]
        rows_free = sem("rows_free")
        held_sp, held_dve, held_pool = sem("held_sp"), sem("held_dve"), sem("held_pool")
        block = ctx.enter_context(nc.Block())

        n_pd, n_ph = sum(POOL_DBX), sum(POOL_HC)

        def earlier(i, n, k):
            return (i, n - k) if n >= k else (i - 1, n - k + STATE)

        def known_past(i):
            return not isinstance(i, int) or i >= 0

        def wait_dbx(eng, i, n):
            if not known_past(i):
                return
            if POOL_DBX[n]:
                eng.wait_ge(dbx_pool, n_pd * i + sum(POOL_DBX[:n + 1]))
            else:
                eng.wait_ge(dbx_dve, (STATE - n_pd) * i + n + 1 - sum(POOL_DBX[:n + 1]))

        def wait_hc(eng, i, n):
            if not known_past(i):
                return
            if POOL_HC[n]:
                eng.wait_ge(hc_pool, n_ph * i + sum(POOL_HC[:n + 1]))
            else:
                eng.wait_ge(hc_dve, (STATE - n_ph) * i + n + 1 - sum(POOL_HC[:n + 1]))

        def wait_past(eng, s, per, i, n):
            if known_past(i):
                eng.wait_ge(s, per * i + n)

        def wait_bc(eng, i, n):
            eng.wait_ge(bc_loaded[n % BC_RING], (16 * STATE // BC_RING) * i + 16 * (n // BC_RING + 1))

        def steps(eng, step):
            step(-1, 1, False, True, False, False)
            step(0, 0, True, True, False, False)
            step(1, 1, True, True, True, False)
            with eng.Fori(0, SEQS - 2) as q:
                i = 2 * q + 2
                step(i, 0, True, True, True, True)
                step(i + 1, 1, True, True, True, True)
            step(BLOCKS - 2, 0, True, True, True, True)
            step(BLOCKS - 1, 1, True, False, True, True)
            step(BLOCKS, 0, False, False, True, True)
            step(BLOCKS + 1, 1, False, False, False, True)

        @block.sync
        def _(sp):
            def step(i, half, scans, front, back, place):
                f, r, fp, rp = i + 1, i - 1, 1 - half, 1 - half
                if front:
                    wait_past(sp, sum_done, STATE, f - 2, STATE)
                    hold(sp, held_sp)
                    sp.dma_start(x_t[:, fp], d.x_t[f]).then_inc(xt_loaded[fp], 16)
                if back:
                    wait_past(sp, pre_done, TT, r - 1, TT)
                    hold(sp, held_sp)
                    sp.dma_start(x_tok[:], d.x_tok[r]).then_inc(xtok_loaded, 16)
                for n in range(STATE):
                    if scans:
                        wait_hc(sp, *earlier(i, n, BC_RING))
                        hold(sp, held_sp)
                        sp.dma_start(bc[:, n % BC_RING], d.bc[i, n::STATE, :].partition_broadcast(P))\
                            .then_inc(bc_loaded[n % BC_RING], 16)
                    if front and n == 13:
                        sp.wait_ge(ssm_done, f + 1)
                        hold(sp, held_sp)
                        sp.dma_start(d.bc[f], ssm[1:1 + 2 * STATE, :]).then_inc(bc_stored, 16)
                    if back and n == 13:
                        sp.wait_ge(x1_done, TT * r + TT)
                        hold(sp, held_sp)
                        sp.dma_start(d.x1[r], xrow[:, rp, :, 0:DIM]).then_inc(x1_stored[rp], 16)
                if front:
                    sp.wait_ge(bc_stored, 16 * f + 16)
                    hold(sp, held_sp)

            for k in range(2):
                sp.sem_inc(x1_stored[k], 16)
            steps(sp, step)
            for k in range(2):
                sp.wait_ge(x1_stored[k], 16 * BLOCKS // 2 + 16)

        @block.tensor
        def _(pe):
            def step(i, half, scans, front, back, place):
                f, r, fp, par = i + 1, i - 1, 1 - half, half

                def in_projection(c):
                    if c == 0:
                        pe.wait_ge(xt_loaded[fp], 16 * ((f - fp) // 2 + 1) if isinstance(f, int)
                                   else 8 * (f - fp) + 16)
                        wait_past(pe, z_read, 2 * EC, f - 1, 2 * EC)
                        wait_past(pe, logit_done, 1, f - 3, 1)
                    if c >= 2:
                        pe.wait_ge(xp_done, EC * f + c - 1)
                    for k in range(KC):
                        last = nc.tensor.matmul(in_ps[:, c % 2, :], t.w_in[:, k, c * P:(c + 1) * P],
                                                x_t[:, fp, k, :], start=(k == 0), stop=(k == KC - 1))
                    last.then_inc(inproj_done, 1)

                def ssm_projection():
                    pe.wait_ge(silu_done, f + 1)
                    if place:
                        pe.wait_ge(rank_read, i - 1)
                    for c in range(EC):
                        last = nc.tensor.matmul(aux_ps[0:1 + 2 * STATE, :], t.w_x[:, c, :], xc[:, fp, c, :],
                                                start=(c == 0), stop=(c == EC - 1))
                    last.then_inc(ssm_ps_done, 1)

                def z_products(c):
                    if c == 0:
                        pe.wait_ge(ssm_done, f + 1)
                        pe.wait_ge(xp_done, EC * f + EC)
                    if c >= 2:
                        pe.wait_ge(z_read, 2 * EC * f + 2 * (c - 1))
                    nc.tensor.matmul(in_ps[:, c % 2, :], t.w_dt[0:1, c * P:(c + 1) * P], ssm[0:1, :],
                                     start=True, stop=True).then_inc(z_done, 1)

                def skip_terms(m):
                    c = m % EC
                    if m < KC * EC:
                        k = m // EC
                        nc.tensor.matmul(y_ps[:, c, :], t.w_in[:, k, INNER + c * P:INNER + (c + 1) * P],
                                         x_t[:, par, k, :], start=False, stop=False)
                    else:
                        nc.tensor.matmul(y_ps[:, c, :], t.diag_d[:, c, :], xc[:, par, c, :],
                                         start=False, stop=False)

                def sum_states(n):
                    wait_hc(pe, i, n)
                    if n == 0:
                        wait_past(pe, ys_done, 1, i - 1, 1)
                    for c in range(EC):
                        last = nc.tensor.matmul(y_ps[:, c, :], t.ident[:], prod[:, n % P_RING, c, :],
                                                start=(n == 0), stop=(n == STATE - 1))
                    last.then_inc(sum_done, 1)

                def out_projection(j):
                    if j == 0:
                        pe.wait_ge(ys_done, r + 1)
                    if j == 2:
                        pe.wait_ge(pre_done, TT * r + 2)
                    if j == 0:
                        wait_past(pe, pre_done, TT, r - 1, TT)
                    for c in range(EC):
                        last = nc.tensor.matmul(out_ps[:, j % 2, :], ys[:, c, j * P:(j + 1) * P],
                                                t.w_out[:, c, :], start=(c == 0), stop=(c == EC - 1))
                    if j % 2 == 1:
                        last.then_inc(outproj_done, 1)

                def turn(h):
                    if h == 0:
                        pe.wait_ge(x1_done, TT * r + TT)
                        if front:
                            pe.wait_ge(ssm_done, f + 1)
                        elif place:
                            pe.wait_ge(rank_read, i - 1)
                    else:
                        pe.wait_ge(turned_read, 2 * r + 1)
                    for jj in range(2):
                        for k in range(KC):
                            at = (jj * KC + k) * P
                            last = nc.tensor.transpose(aux_ps[:, at:at + P],
                                                       xrow[:, 1 - par, 2 * h + jj, k * P:(k + 1) * P], t.ident[:])
                    last.then_inc(turned, 1)

                def logits():
                    pe.wait_ge(turned_read, 2 * r + 2)
                    if front:
                        pe.wait_ge(z_read, 2 * EC * (f + 1))
                    for j in range(TT):
                        for k in range(KC):
                            last = nc.tensor.matmul(in_ps[:, 0, j * EXPERTS:(j + 1) * EXPERTS], x1_t[:, j, k, :],
                                                    t.router[:, k, :], start=(k == 0), stop=(k == KC - 1))
                    last.then_inc(logit_ps_done, 1)

                def ranks():
                    pe.wait_ge(member_done, r + 1)
                    for j in range(TT + 1):
                        dst = aux_ps[:, j * EXPERTS:(j + 1) * EXPERTS]
                        if j < TT:
                            nc.tensor.matmul(dst, t.before[:], member[:, j, :], start=True, stop=(j == 0))
                        for k in range(j):
                            last = nc.tensor.matmul(dst, t.ones[:], member[:, k, :],
                                                    start=(j == TT and k == 0), stop=(k == j - 1))
                    last.then_inc(rank_ps_done, 1)

                for n in range(STATE):
                    if scans:
                        sum_states(n)
                        if 1 <= n <= 12:
                            skip_terms(n - 1)
                    if front:
                        if 1 <= n <= 4:
                            in_projection(n - 1)
                        if n == 9:
                            ssm_projection()
                        if n == 11:
                            z_products(0)
                            z_products(1)
                        if n == 12:
                            z_products(2)
                            z_products(3)
                    if back:
                        if n == 2 or n == 5:
                            out_projection(2 * (n // 3))
                            out_projection(2 * (n // 3) + 1)
                        if n == 11:
                            turn(0)
                        if n == 12:
                            turn(1)
                        if n == 14:
                            logits()
                        if n == 15:
                            ranks()

            steps(pe, step)

        @block.scalar
        def _(act):
            def step(i, half, scans, front, back, place):
                f, r, fp, par = i + 1, i - 1, 1 - half, half

                def halo():
                    wait_past(act, tap_done, TAPS * EC, f - 1, TAPS * EC)
                    wait_past(act, dt_done, 1, f - 1, 1)
                    src = t.xp[:, :, T:T + TAPS - 1] if fp == 1 else t.zeros[:, :, 0:TAPS - 1]
                    nc.scalar.copy(t.xp[:, :, 0:TAPS - 1], src).then_inc(halo_done, 1)

                def xp_out(c):
                    act.wait_ge(inproj_done, EC * f + c + 1)
                    if c == 0:
                        act.wait_ge(halo_done, f + 1)
                    nc.scalar.copy(t.xp[:, c, TAPS - 1:], in_ps[:, c % 2, :]).then_inc(xp_done, 1)

                def silu():
                    act.wait_ge(tap_done, TAPS * EC * (f + 1))
                    nc.scalar.activation(xc[:, fp], xc[:, fp], ACT.Silu).then_inc(silu_done, 1)

                def ssm_out():
                    act.wait_ge(ssm_ps_done, f + 1)
                    wait_past(act, bc_stored, 16, f - 1, 16)
                    wait_past(act, z_done, EC, f - 1, EC)
                    nc.scalar.copy(ssm[:], aux_ps[0:1 + 2 * STATE, :]).then_inc(ssm_done, 1)

                def z_parts(c):
                    act.wait_ge(z_done, EC * f + c + 1)
                    if c == 0:
                        wait_past(act, decay_done, STATE, f - 2, STATE)
                    nc.scalar.activation(t.xp[:, c, 0:T], in_ps[:, c % 2, :], ACT.Abs,
                                         bias=t.b_dt[:, c:c + 1]).then_inc(z_read, 1)
                    nc.scalar.activation(dt[:, fp, c, :], in_ps[:, c % 2, :], ACT.Relu,
                                         bias=t.b_dt[:, c:c + 1]).then_inc(z_read, 1)

                def soft_tail():
                    act.wait_ge(z_read, 2 * EC * (f + 1))
                    nc.scalar.activation(t.xp[:, :, 0:T], t.xp[:, :, 0:T], ACT.Exp, scale=-1.0).then_inc(ln_done, 1)
                    act.wait_ge(ln_done, 2 * f + 1)
                    nc.scalar.activation(t.xp[:, :, 0:T], t.xp[:, :, 0:T], ACT.Ln, bias=t.ones[:, 0:1])\
                        .then_inc(ln_done, 1)

                def carry_in(n):
                    wait_hc(act, *earlier(i, n, S_RING))
                    if par == 1:
                        act.wait_ge(carried_out, STATE * ((i - 1) // 2) + n + 1 if isinstance(i, int)
                                    else 8 * (i - 1) + n + 1)
                    src = carry[:, n, :].unsqueeze(2) if par == 1 else t.zeros[:, :, 0:1]
                    nc.scalar.copy(scan[:, n % S_RING, :, 0:1], src).then_inc(carried_in, 1)

                def carry_out(n):
                    act.wait_ge(scan_done, STATE * i + n + 1)
                    nc.scalar.copy(carry[:, n, :].unsqueeze(2), scan[:, n % S_RING, :, T:T + 1])\
                        .then_inc(carried_out, 1)

                def decays(n):
                    if n == 0:
                        act.wait_ge(dt_done, i + 1)
                    wait_past(act, scan_done, STATE, *[(a, b + 1) for a, b in [earlier(i, n, DA_RING)]][0])
                    nc.scalar.activation(t.decay[:, n % DA_RING, :, 1:], dt[:, par], ACT.Exp,
                                         scale=t.neg_a[:, n:n + 1]).then_inc(decay_done, 1)

                def y_silu():
                    act.wait_ge(sum_done, STATE * (r + 1))
                    wait_past(act, outproj_done, 2, r - 1, 2)
                    nc.scalar.activation(ys[:], y_ps[:], ACT.Silu).then_inc(ys_done, 1)

                def turned_out(h):
                    act.wait_ge(turned, 2 * r + h + 1)
                    wait_past(act, logit_ps_done, 1, r - 1, 1)
                    nc.scalar.copy(x1_t[:, 2 * h:2 * h + 2].rearrange("p j k q -> p (j k q)"), aux_ps[:])\
                        .then_inc(turned_read, 1)

                def router_exp():
                    act.wait_ge(shifted, r + 1)
                    nc.scalar.activation(ex[:], ex[:], ACT.Exp).then_inc(ex_done, 1)

                for n in range(STATE):
                    if scans:
                        carry_in(n)
                        decays(n)
                        if par == 0 and n >= 2:
                            carry_out(n - 2)
                    if back and n == 1:
                        y_silu()
                    if front:
                        if n == 1:
                            halo()
                        if 3 <= n <= 6:
                            xp_out(n - 3)
                        if n == 9:
                            silu()
                        if n == 11:
                            ssm_out()
                        if n == 12:
                            z_parts(0)
                            z_parts(1)
                        if n == 13:
                            z_parts(2)
                            z_parts(3)
                            soft_tail()
                    if back:
                        if n == 12:
                            turned_out(0)
                        if n == 13:
                            turned_out(1)
                        if n == 15:
                            router_exp()
                if scans and par == 0:
                    carry_out(STATE - 2)
                    carry_out(STATE - 1)

            steps(act, step)

        LINKS = 11
        PLACE_LINKS = 6

        @block.vector
        def _(dve):
            def step(i, half, scans, front, back, place):
                f, r, fp, par, rp = i + 1, i - 1, 1 - half, half, 1 - half

                def tap(c, k):
                    col = TAPS - 1 - k
                    src = t.xp[:, c, col:col + T]
                    if k == 0:
                        dve.wait_ge(xp_done, EC * f + c + 1)
                        if c == 0:
                            wait_past(dve, sum_done, STATE, f - 2, STATE)
                        nc.vector.tensor_scalar(xc[:, fp, c, :], src, t.conv_w[:, c, col:col + 1],
                                                t.conv_b[:, c:c + 1], ALU.mult, ALU.add).then_inc(tap_done, 1)
                        return
                    dve.wait_ge(tap_done, TAPS * EC * f + TAPS * c + k)
                    nc.vector.scalar_tensor_tensor(out=xc[:, fp, c, :], in0=src, scalar=t.conv_w[:, c, col:col + 1],
                                                   in1=xc[:, fp, c, :], op0=ALU.mult, op1=ALU.add)\
                        .then_inc(tap_done, 1)

                def step_sizes():
                    dve.wait_ge(ln_done, 2 * f + 2)
                    nc.vector.tensor_tensor(dt[:, fp], dt[:, fp], t.xp[:, :, 0:T], ALU.add).then_inc(dt_done, 1)
                    dve.wait_ge(dt_done, f + 1)
                    wait_dbx(dve, f - 2, STATE - 1)
                    nc.vector.tensor_tensor(u[:, fp], dt[:, fp], xc[:, fp], ALU.mult).then_inc(u_done, 1)

                def dbx(n):
                    wait_bc(dve, i, n)
                    dve.wait_ge(carried_in, STATE * i + n + 1)
                    dve.wait_ge(u_done, i + 1)
                    nc.vector.tensor_tensor(scan[:, n % S_RING, :, 1:], u[:, par],
                                            bc[:, n % BC_RING, 0:1, :].broadcast_to([P, EC, T]), ALU.mult)\
                        .then_inc(dbx_dve, 1)

                def hc(n):
                    wait_bc(dve, i, n)
                    dve.wait_ge(scan_done, STATE * i + n + 1)
                    wait_past(dve, sum_done, STATE, *[(a, b + 1) for a, b in [earlier(i, n, P_RING)]][0])
                    nc.vector.tensor_tensor(prod[:, n % P_RING], scan[:, n % S_RING, :, 1:],
                                            bc[:, n % BC_RING, 1:2, :].broadcast_to([P, EC, T]), ALU.mult)\
                        .then_inc(hc_dve, 1)

                def recurrence(n):
                    dve.wait_ge(decay_done, STATE * i + n + 1)
                    dve.wait_ge(carried_in, STATE * i + n + 1)
                    wait_dbx(dve, i, n)
                    line = scan[:, n % S_RING].rearrange("p c t -> p (c t)")
                    nc.vector.tensor_tensor_scan(line, t.decay[:, n % DA_RING].rearrange("p c t -> p (c t)"), line,
                                                 0.0, ALU.mult, ALU.add).then_inc(scan_done, 1)

                def residual(j):
                    dve.wait_ge(outproj_done, 2 * r + j // 2 + 1)
                    if j == 0:
                        dve.wait_ge(xtok_loaded, 16 * (r + 1))
                        dve.wait_ge(x1_stored[rp], 8 * (r - rp) + 16)
                        dve.wait_ge(rows_free, r + 1)
                    nc.vector.tensor_tensor(xrow[:, rp, j, 0:DIM], out_ps[:, j % 2, :], x_tok[:, j, :], ALU.add)\
                        .then_inc(pre_done, 1)

                def moments(j):
                    dve.wait_ge(pre_done, TT * r + j + 1)
                    nc.vector.bn_stats(stats[:, j, :], xrow[:, rp, j, 0:DIM]).then_inc(stats_done, 1)

                def variance():
                    dve.wait_ge(stats_done, TT * (r + 1))
                    wait_past(dve, x1_done, TT, r - 1, TT)
                    hold(dve, held_dve)
                    for j in range(TT):
                        last = nc.vector.bn_aggr(mv[:, j, :], stats[:, j, :])
                    last.then_inc(norm_chain, 1)
                    dve.wait_ge(norm_chain, 2 * r + 1)
                    nc.vector.tensor_scalar(var[:], mv[:, :, 1], EPS, None, ALU.add).then_inc(norm_chain, 1)

                def normed(j):
                    dve.wait_ge(rstd_done, r + 1)
                    nc.vector.tensor_scalar(xrow[:, rp, j, 0:DIM], xrow[:, rp, j, 0:DIM], mv[:, j, 0:1],
                                            rstd[:, j:j + 1], ALU.subtract, ALU.mult).then_inc(x1_done, 1)

                links, placed = [0], [0]

                def link(ins):
                    links[0] += 1
                    ins.then_inc(route, 1)
                    dve.wait_ge(route, LINKS * r + links[0])

                def place_link(ins):
                    placed[0] += 1
                    ins.then_inc(place_chain, 1)
                    dve.wait_ge(place_chain, PLACE_LINKS * (i - 2) + placed[0])

                def router_shift():
                    dve.wait_ge(logit_ps_done, r + 1)
                    nc.vector.tensor_copy(logit[:].rearrange("p j e -> p (j e)"),
                                          in_ps[:, 0, 0:TT * EXPERTS]).then_inc(logit_done, 1)
                    dve.wait_ge(logit_done, r + 1)
                    link(nc.vector.tensor_reduce(mx[:], logit[:], AXX, ALU.max))
                    nc.vector.tensor_tensor(ex[:], logit[:], mx[:].unsqueeze(2).broadcast_to([P, TT, EXPERTS]),
                                            ALU.subtract).then_inc(shifted, 1)

                def router_top():
                    dve.wait_ge(ex_done, r + 1)
                    link(nc.vector.tensor_reduce(mx[:], ex[:], AXX, ALU.add))
                    link(nc.vector.reciprocal(mx[:], mx[:]))
                    link(nc.vector.tensor_tensor(prob[:], ex[:], mx[:].unsqueeze(2).broadcast_to([P, TT, EXPERTS]),
                                                 ALU.mult))
                    hold(dve, held_dve)
                    for j in range(TT):
                        last = nc.vector.max(top[:, j, :], prob[:, j, :])
                    link(last)
                    hold(dve, held_dve)
                    for j in range(TT):
                        last = nc.vector.max_index(idx[:, j, :], top[:, j, :], prob[:, j, :])
                    link(last)
                    link(nc.vector.scalar_tensor_tensor(out=mx[:], in0=top[:, :, 0], scalar=1e-9, in1=top[:, :, 1],
                                                        op0=ALU.add, op1=ALU.add))
                    link(nc.vector.reciprocal(mx[:], mx[:]))
                    link(nc.vector.tensor_tensor(wk[:], top[:, :, 0:TOPK],
                                                 mx[:].unsqueeze(2).broadcast_to([P, TT, TOPK]), ALU.mult))
                    link(nc.vector.tensor_copy(ek[:], idx[:, :, 0:TOPK]))
                    link(nc.vector.tensor_tensor(
                        onehot[:].rearrange("p j k e -> p (j k) e"),
                        t.iota_ef[:].unsqueeze(1).broadcast_to([P, TT * TOPK, EXPERTS]),
                        ek[:].rearrange("p j k -> p (j k)").unsqueeze(2).broadcast_to([P, TT * TOPK, EXPERTS]),
                        ALU.is_equal))
                    nc.vector.tensor_tensor(member[:], onehot[:, :, 0, :], onehot[:, :, 1, :], ALU.add)\
                        .then_inc(member_done, 1)
                    assert links[0] == LINKS, links

                def router_place():
                    dve.wait_ge(rank_ps_done, i - 1)
                    place_link(nc.vector.tensor_tensor(rank[:], aux_ps[:, 0:TT * EXPERTS].rearrange("p (j e) -> p j e",
                                                                                             e=EXPERTS),
                                                 t.base[:].unsqueeze(1).broadcast_to([P, TT, EXPERTS]), ALU.add))
                    nc.vector.tensor_tensor(t.base[:], t.base[:], aux_ps[:, TT * EXPERTS:(TT + 1) * EXPERTS],
                                            ALU.add).then_inc(rank_read, 1)
                    for k in range(TOPK):
                        place_link(nc.vector.tensor_tensor(rsel[:, :, k, :], onehot[:, :, k, :], rank[:], ALU.mult))
                    place_link(nc.vector.tensor_reduce(rk[:], rsel[:], AXX, ALU.add))
                    place_link(nc.vector.scalar_tensor_tensor(out=rk[:], in0=ek[:], scalar=float(REGION), in1=rk[:],
                                                        op0=ALU.mult, op1=ALU.add))
                    nc.vector.tensor_copy(pos[:, par], rk[:])
                    nc.vector.tensor_copy(xrow[:, par, :, DIM:DIM + 2], wk[:, :, 0:1].broadcast_to([P, TT, 2]))
                    nc.vector.tensor_copy(xrow[:, par, :, DIM + 2], wk[:, :, 1])
                    dve.wait_ge(rank_read, i - 1)
                    place_link(nc.vector.tensor_copy(xrow[:, par, :, DIM + 3], t.token2[:]))
                    nc.vector.tensor_copy(xrow[:, par, :, DIM + 1], ek[:, :, 0])
                    nc.vector.tensor_scalar(t.token2[:], t.token2[:], float(TOPK * T), None, ALU.add)\
                        .then_inc(pos_done, 1)
                    dve.wait_ge(pos_done, i - 1)
                    assert placed[0] == PLACE_LINKS, placed

                for n in range(STATE):
                    if scans:
                        if not POOL_DBX[n]:
                            dbx(n)
                        recurrence(n)
                        if n >= 1 and not POOL_HC[n - 1]:
                            hc(n - 1)
                    if front:
                        if 4 <= n <= 7:
                            for k in range(TAPS):
                                tap(n - 4, k)
                        if n == 14:
                            step_sizes()
                    if place and n == 1:
                        router_place()
                    if back:
                        if n == 3 or n == 6:
                            residual(2 * (n // 4))
                            residual(2 * (n // 4) + 1)
                            moments(2 * (n // 4))
                            moments(2 * (n // 4) + 1)
                        if n == 7:
                            variance()
                        if n == 10:
                            for j in range(TT):
                                normed(j)
                        if n == 15:
                            router_shift()
                if scans and not POOL_HC[STATE - 1]:
                    hc(STATE - 1)
                if back:
                    router_top()

            steps(dve, step)

        @block.gpsimd
        def _(pool):
            def step(i, half, scans, front, back, place):
                f, r, par, rp = i + 1, i - 1, half, 1 - half

                def dbx(n):
                    if n == 0:
                        pool.wait_ge(u_done, i + 1)
                    wait_bc(pool, i, n)
                    pool.wait_ge(carried_in, STATE * i + n + 1)
                    nc.gpsimd.tensor_tensor(scan[:, n % S_RING, :, 1:], u[:, par],
                                            bc[:, n % BC_RING, 0:1, :].broadcast_to([P, EC, T]), ALU.mult)\
                        .then_inc(dbx_pool, 1)

                def hc(n):
                    wait_bc(pool, i, n)
                    pool.wait_ge(scan_done, STATE * i + n + 1)
                    wait_past(pool, sum_done, STATE, *[(a, b + 1) for a, b in [earlier(i, n, P_RING)]][0])
                    nc.gpsimd.tensor_tensor(prod[:, n % P_RING], scan[:, n % S_RING, :, 1:],
                                            bc[:, n % BC_RING, 1:2, :].broadcast_to([P, EC, T]), ALU.mult)\
                        .then_inc(hc_pool, 1)

                def rstds():
                    pool.wait_ge(norm_chain, 2 * r + 2)
                    nc.gpsimd.tensor_tensor(rstd[:], var[:], t.minus_half[:], ALU.pow).then_inc(rstd_done, 1)

                def send_rows():
                    pool.wait_ge(pos_done, i - 1)
                    hold(pool, held_pool)
                    for j in range(TT):
                        for k in range(TOPK):
                            pool.indirect_dma_start(
                                out=d.rows, out_offset=bass.IndirectOffsetOnAxis(ap=pos[:, par, j, k:k + 1], axis=0),
                                in_=xrow[:, par, j, :], in_offset=None).then_inc(rows_sent[par], 16)

                for n in range(STATE):
                    if scans:
                        if POOL_DBX[n]:
                            dbx(n)
                        if n >= 1 and POOL_HC[n - 1]:
                            hc(n - 1)
                    if place and n == 3:
                        send_rows()
                    if back and n == 10:
                        rstds()
                if scans and POOL_HC[STATE - 1]:
                    hc(STATE - 1)
                if place:
                    pool.wait_ge(rows_sent[par], 8 * TT * TOPK * (i - 2 - par) + 16 * TT * TOPK)
                    pool.sem_inc(rows_free, 1)

            pool.sem_inc(rows_free, 2)
            steps(pool, step)
            for k in range(2):
                pool.wait_ge(rows_sent[k], 16 * TT * TOPK * BLOCKS // 2)


def experts(nc, d, t):
    with ExitStack() as ctx:
        def sb(name, shape, dt=F32):
            return ctx.enter_context(nc.sbuf_tensor(name, shape, dt))

        def ps(name, shape):
            return ctx.enter_context(nc.psum_tensor(name, shape, F32))

        def sem(name):
            return ctx.enter_context(nc.semaphore(name))

        w1 = sb("w1", [P, EXPERTS, KC, FF])
        w2 = sb("w2", [P, EXPERTS, FF // P, DIM])
        b1 = sb("b1", [P, EXPERTS, FF])
        b2 = sb("b2", [P, EXPERTS, DIM])
        FC = FF // P
        MAX_J = TOKENS // P
        thresholds_i = sb("thresholds_i", [P, MAX_J], I32)
        thresholds = sb("thresholds", [P, MAX_J])
        over = sb("over", [P, EXPERTS, MAX_J])
        n_slots = sb("n_slots", [P, EXPERTS])
        ends = sb("ends", [P, EXPERTS])
        slot_i = sb("slot_i", [P, SLOTS], I32)
        slot_f = sb("slot_f", [P, SLOTS])
        passed = sb("passed", [P, SLOTS, EXPERTS])
        slot_e = sb("slot_e", [P, SLOTS])
        slot_start = sb("slot_start", [P, SLOTS])
        slot_valid = sb("slot_valid", [P, SLOTS])
        slot_ei = sb("slot_ei", [P, SLOTS], I32)
        slot_row = sb("slot_row", [P, SLOTS], I32)
        tail_i = sb("tail_i", [P, EXPERTS], I32)
        tail_pos = sb("tail_pos", [P, EXPERTS], U32)
        tail_f = sb("tail_f", [P, EXPERTS])
        tail_row = sb("tail_row", [P, ROW])
        pad_i = sb("pad_i", [P, 1], I32)
        tags = sb("tags", [P, 2, 6])
        dest = sb("dest", [P, 2], U32)
        xg = sb("xg", [P, 2, ROW])
        xg_t = sb("xg_t", [P, KC, P])
        h = sb("h", [P, FF])
        h_t = sb("h_t", [P, FC, P])
        y = sb("y", [P, 2, DIM])

        xt_ps = ps("xt_ps", [P, T])
        h_ps = ps("h_ps", [P, 2, T])
        ht_ps = ps("ht_ps", [P, FC, P])
        y_ps2 = ps("y_ps2", [P, 2, T])

        made = sem("tables_iota")
        chain = sem("tables_chain")
        tables_done = sem("tables_done")
        tails_sent = sem("tails_sent")
        w_loaded = [sem(f"w_loaded{e}") for e in range(EXPERTS)]
        w_ready = sem("w_ready")
        x_loaded = [sem(f"x_loaded{k}") for k in range(2)]
        xt_done = sem("xt_done")
        xt_read = sem("xt_read")
        h_ps_done = sem("h_ps_done")
        h_done = sem("h_done")
        ht_ps_done = sem("ht_ps_done")
        ht_done = sem("ht_done")
        y_ps_done = sem("y_ps_done")
        y_biased = sem("y_biased")
        y_done = sem("y_done")
        tag_chain = sem("tag_chain")
        y_sent = [sem(f"y_sent{k}") for k in range(2)]
        y_free = sem("y_free")
        held_sp, held_pool = sem("held_sp2"), sem("held_pool2")
        block = ctx.enter_context(nc.Block())
        HALF = FF // 2

        def halves(i, k):
            return 8 * (i - k) + 16

        @block.sync
        def _(sp):
            def load_x(s, k):
                if not isinstance(s, int) or s >= 2:
                    sp.wait_ge(xt_done, s - 1)
                    sp.wait_ge(y_done, s - 1)
                    hold(sp, held_sp)
                row = sp.value_load(slot_row[0:1, bass.ds(s, 1)], min_val=0, max_val=EXPERTS * REGION)
                sp.dma_start(xg[:, k], d.rows[bass.ds(row, P), :]).then_inc(x_loaded[k], 16)

            sp.wait_ge(tables_done, 1)
            sp.wait_ge(tails_sent, 16 * (EXPERTS + 1))
            load_x(0, 0)
            load_x(1, 1)
            with sp.Fori(1, SLOTS // 2) as q:
                load_x(2 * q, 0)
                load_x(2 * q + 1, 1)

        @block.gpsimd
        def _(pool):
            nc.gpsimd.iota(thresholds_i[:], pattern=[[P, MAX_J]], base=0, channel_multiplier=0).then_inc(made, 1)
            nc.gpsimd.iota(slot_i[:], pattern=[[1, SLOTS]], base=0, channel_multiplier=0).then_inc(made, 1)
            nc.gpsimd.iota(tail_i[:], pattern=[[REGION, EXPERTS]], base=0, channel_multiplier=1).then_inc(made, 1)
            nc.gpsimd.iota(pad_i[:], pattern=[[0, 1]], base=TRASH - 1, channel_multiplier=1).then_inc(made, 1)
            pool.wait_ge(tables_done, 1)
            for e in range(EXPERTS):
                pool.indirect_dma_start(out=d.rows, out_offset=bass.IndirectOffsetOnAxis(ap=tail_pos[:, e:e + 1], axis=0),
                                        in_=tail_row[:], in_offset=None).then_inc(tails_sent, 16)
            pool.dma_start(d.rows[EXPERTS * REGION:EXPERTS * REGION + P, :], tail_row[:]).then_inc(tails_sent, 16)

            pool.sem_inc(y_free, 2)

            def send(s, k):
                if not isinstance(s, int) or s >= 2:
                    pool.wait_ge(y_sent[k], 8 * (s - k))
                    pool.sem_inc(y_free, 1)
                pool.wait_ge(y_done, s + 1)
                hold(pool, held_pool)
                pool.indirect_dma_start(out=d.y, out_offset=bass.IndirectOffsetOnAxis(ap=dest[:, k:k + 1], axis=0),
                                        in_=y[:, k, :], in_offset=None).then_inc(y_sent[k], 16)

            send(0, 0)
            send(1, 1)
            with pool.Fori(1, SLOTS // 2) as q:
                send(2 * q, 0)
                send(2 * q + 1, 1)
            for k in range(2):
                pool.wait_ge(y_sent[k], 16 * SLOTS // 2)

        @block.scalar
        def _(act):
            for e in range(EXPERTS):
                act.dma_start(w1[:, e], d.w1[e].rearrange("(k p) f -> p k f", p=P)).then_inc(w_loaded[e], 16)
                act.dma_start(w2[:, e], d.w2[e].rearrange("(g p) n -> p g n", p=P)).then_inc(w_loaded[e], 16)
                act.dma_start(b1[:, e], d.b1[e].partition_broadcast(P)).then_inc(w_loaded[e], 16)
                act.dma_start(b2[:, e], d.b2[e].partition_broadcast(P)).then_inc(w_loaded[e], 16)
            for e in range(EXPERTS):
                act.wait_ge(w_loaded[e], 64)
                act.sem_inc(w_ready, 1)

            def read_xt(s):
                act.wait_ge(xt_done, s + 1)
                if not isinstance(s, int) or s >= 1:
                    act.wait_ge(h_ps_done, 2 * s)
                nc.scalar.copy(xg_t[:].rearrange("p k q -> p (k q)"), xt_ps[:, 0:KC * P]).then_inc(xt_read, 1)

            def gelu(s):
                for g in range(2):
                    act.wait_ge(ht_ps_done, 2 * s + g + 1)
                    if g == 0 and (not isinstance(s, int) or s >= 1):
                        act.wait_ge(y_ps_done, s)
                    lo, hi = g * FC // 2, (g + 1) * FC // 2
                    nc.scalar.activation(h_t[:, lo:hi, :], ht_ps[:, lo:hi, :], ACT.Gelu).then_inc(ht_done, 1)

            read_xt(0)
            gelu(0)
            with act.Fori(1, SLOTS) as s:
                read_xt(s)
                gelu(s)

        @block.tensor
        def _(pe):
            def turn_x(s, k):
                pe.wait_ge(x_loaded[k], halves(s, k))
                if not isinstance(s, int) or s >= 1:
                    pe.wait_ge(xt_read, s)
                for c in range(KC):
                    last = nc.tensor.transpose(xt_ps[:, c * P:(c + 1) * P], xg[:, k, c * P:(c + 1) * P], t.ident[:])
                last.then_inc(xt_done, 1)

            def up(s, k):
                e = pe.value_load(slot_ei[0:1, bass.ds(s, 1)], min_val=0, max_val=EXPERTS - 1)
                pe.wait_ge(w_ready, e + 1)
                pe.wait_ge(xt_read, s + 1)
                for g in range(2):
                    if not isinstance(s, int) or s >= 1:
                        pe.wait_ge(h_done, 2 * s - 1 + g)
                    for c in range(KC):
                        last = nc.tensor.matmul(h_ps[:, g, :], xg_t[:, c, :],
                                                w1[:, bass.ds(e, 1), c, g * HALF:(g + 1) * HALF].squeeze(1),
                                                start=(c == 0), stop=(c == KC - 1))
                    last.then_inc(h_ps_done, 1)

            def turn_h(s):
                for g in range(2):
                    pe.wait_ge(h_done, 2 * s + g + 1)
                    if not isinstance(s, int) or s >= 1:
                        pe.wait_ge(ht_done, 2 * s - 1 + g)
                    for j in range(g * FC // 2, (g + 1) * FC // 2):
                        last = nc.tensor.transpose(ht_ps[:, j, :], h[:, j * P:(j + 1) * P], t.ident[:])
                    last.then_inc(ht_ps_done, 1)

            def down(s, k):
                e = pe.value_load(slot_ei[0:1, bass.ds(s, 1)], min_val=0, max_val=EXPERTS - 1)
                pe.wait_ge(y_biased, s)
                for j in range(FC):
                    if j % (FC // 2) == 0:
                        pe.wait_ge(ht_done, 2 * s + 1 + j // (FC // 2))
                    last = nc.tensor.matmul(y_ps2[:, k, 0:DIM], h_t[:, j, :], w2[:, bass.ds(e, 1), j, :].squeeze(1),
                                            start=(j == 0), stop=(j == FC - 1))
                last.then_inc(y_ps_done, 1)

            pe.wait_ge(tables_done, 1)
            turn_x(0, 0)
            up(0, 0)
            turn_x(1, 1)
            turn_h(0)
            up(1, 1)
            down(0, 0)
            with pe.Fori(0, SLOTS // 2 - 1) as q:
                s = 2 * q + 1
                turn_x(s + 1, 0)
                turn_h(s)
                up(s + 1, 0)
                down(s, 1)
                turn_x(s + 2, 1)
                turn_h(s + 1)
                up(s + 2, 1)
                down(s + 1, 0)
            turn_h(SLOTS - 1)
            down(SLOTS - 1, 1)

        @block.vector
        def _(dve):
            links = [0]

            def link(ins):
                links[0] += 1
                ins.then_inc(chain, 1)
                dve.wait_ge(chain, links[0])

            dve.wait_ge(made, 4)
            link(nc.vector.tensor_copy(thresholds[:], thresholds_i[:]))
            link(nc.vector.tensor_copy(slot_f[:], slot_i[:]))
            link(nc.vector.tensor_copy(tail_f[:], tail_i[:]))
            link(nc.vector.memset(tail_row[:], 0.0))
            link(nc.vector.memset(tail_row[:, DIM + 1:DIM + 2], -1.0))
            link(nc.vector.tensor_copy(tail_row[:, DIM + 3:DIM + 4], pad_i[:]))
            link(nc.vector.tensor_tensor(tail_f[:], tail_f[:], t.base[:], ALU.add))
            link(nc.vector.tensor_copy(tail_pos[:], tail_f[:]))
            link(nc.vector.tensor_tensor(over[:], t.base[:].unsqueeze(2).broadcast_to([P, EXPERTS, MAX_J]),
                                         thresholds[:].unsqueeze(1).broadcast_to([P, EXPERTS, MAX_J]), ALU.is_gt))
            link(nc.vector.tensor_reduce(n_slots[:], over[:], AXX, ALU.add))
            link(nc.vector.tensor_tensor_scan(ends[:], t.ones[:, 0:EXPERTS], n_slots[:], 0.0, ALU.mult, ALU.add))
            link(nc.vector.tensor_tensor(passed[:], slot_f[:].unsqueeze(2).broadcast_to([P, SLOTS, EXPERTS]),
                                         ends[:].unsqueeze(1).broadcast_to([P, SLOTS, EXPERTS]), ALU.is_ge))
            link(nc.vector.tensor_reduce(slot_e[:], passed[:], AXX, ALU.add))
            link(nc.vector.tensor_tensor(passed[:], passed[:],
                                         n_slots[:].unsqueeze(1).broadcast_to([P, SLOTS, EXPERTS]), ALU.mult))
            link(nc.vector.tensor_reduce(slot_start[:], passed[:], AXX, ALU.add))
            link(nc.vector.tensor_scalar(slot_valid[:], slot_e[:], float(EXPERTS), None, ALU.is_lt))
            link(nc.vector.tensor_tensor(slot_start[:], slot_f[:], slot_start[:], ALU.subtract))
            link(nc.vector.tensor_scalar(slot_start[:], slot_start[:], float(P), None, ALU.mult))
            link(nc.vector.scalar_tensor_tensor(out=slot_start[:], in0=slot_e[:], scalar=float(REGION),
                                                in1=slot_start[:], op0=ALU.mult, op1=ALU.add))
            link(nc.vector.tensor_tensor(slot_start[:], slot_start[:], slot_valid[:], ALU.mult))
            link(nc.vector.tensor_tensor(slot_e[:], slot_e[:], slot_valid[:], ALU.mult))
            link(nc.vector.tensor_scalar(slot_valid[:], slot_valid[:], -float(EXPERTS * REGION),
                                         float(EXPERTS * REGION), ALU.mult, ALU.add))
            link(nc.vector.tensor_tensor(slot_start[:], slot_start[:], slot_valid[:], ALU.add))
            link(nc.vector.tensor_scalar(slot_f[:], slot_f[:], float(P), None, ALU.mult))
            link(nc.vector.tensor_copy(slot_ei[:], slot_e[:]))
            link(nc.vector.tensor_copy(slot_row[:], slot_start[:]))
            nc.vector.memset(dest[:], 0).then_inc(tables_done, 1)
            dve.wait_ge(tables_done, 1)

            def tag(s, k):
                dve.wait_ge(x_loaded[k], halves(s, k))
                dve.wait_ge(y_free, s + 1)
                e0 = xg[:, k, DIM + 1:DIM + 2]
                nc.vector.tensor_tensor(tags[:, k, 0:1], e0, slot_e[:, bass.ds(s, 1)], ALU.is_equal)
                nc.vector.tensor_tensor(tags[:, k, 1:2], e0, slot_e[:, bass.ds(s, 1)], ALU.not_equal)
                nc.vector.tensor_scalar(tags[:, k, 4:5], e0, 0.0, slot_f[:, bass.ds(s, 1)], ALU.is_lt, ALU.mult)\
                    .then_inc(tag_chain, 1)
                dve.wait_ge(tag_chain, 4 * s + 1)
                nc.vector.tensor_tensor(tags[:, k, 2:3], xg[:, k, DIM:DIM + 1], tags[:, k, 0:1], ALU.mult)
                nc.vector.tensor_tensor(tags[:, k, 5:6], xg[:, k, DIM + 3:DIM + 4], tags[:, k, 1:2], ALU.add)\
                    .then_inc(tag_chain, 1)
                dve.wait_ge(tag_chain, 4 * s + 2)
                nc.vector.tensor_tensor(dest[:, k:k + 1], tags[:, k, 5:6], tags[:, k, 4:5], ALU.add)\
                    .then_inc(tag_chain, 1)
                nc.vector.scalar_tensor_tensor(out=tags[:, k, 3:4], in0=xg[:, k, DIM + 2:DIM + 3],
                                               scalar=tags[:, k, 1:2], in1=tags[:, k, 2:3], op0=ALU.mult,
                                               op1=ALU.add).then_inc(tag_chain, 1)

            def bias_h(s):
                e = dve.value_load(slot_ei[0:1, bass.ds(s, 1)], min_val=0, max_val=EXPERTS - 1)
                for g in range(2):
                    dve.wait_ge(h_ps_done, 2 * s + g + 1)
                    if not isinstance(s, int) or s >= 1:
                        dve.wait_ge(ht_ps_done, 2 * s - 1 + g)
                    nc.vector.tensor_tensor(h[:, g * HALF:(g + 1) * HALF], h_ps[:, g, :],
                                            b1[:, bass.ds(e, 1), g * HALF:(g + 1) * HALF].squeeze(1),
                                            ALU.add).then_inc(h_done, 1)

            def bias_y(s, k):
                e = dve.value_load(slot_ei[0:1, bass.ds(s, 1)], min_val=0, max_val=EXPERTS - 1)
                dve.wait_ge(y_ps_done, s + 1)
                nc.vector.tensor_tensor(y[:, k, :], y_ps2[:, k, 0:DIM], b2[:, bass.ds(e, 1), :].squeeze(1),
                                        ALU.add).then_inc(y_biased, 1)
                dve.wait_ge(y_biased, s + 2)
                dve.wait_ge(tag_chain, 4 * s + 4)
                nc.vector.tensor_scalar(y[:, k, :], y[:, k, :], tags[:, k, 3:4], None, ALU.mult)\
                    .then_inc(y_done, 1)

            dve.sem_inc(y_biased, 1)
            bias_h(0)
            bias_h(1)
            tag(0, 0)
            bias_y(0, 0)
            with dve.Fori(0, SLOTS // 2 - 1) as q:
                s = 2 * q + 1
                bias_h(s + 1)
                tag(s, 1)
                bias_y(s, 1)
                bias_h(s + 2)
                tag(s + 1, 0)
                bias_y(s + 1, 0)
            tag(SLOTS - 1, 1)
            bias_y(SLOTS - 1, 1)


def combine(nc, d, t):
    with ExitStack() as ctx:
        G = 2
        N = TOKENS // P // G
        B = 3
        x1 = ctx.enter_context(nc.sbuf_tensor("c_x1", [P, B, G, DIM], F32))
        ye = ctx.enter_context(nc.sbuf_tensor("c_y", [P, B, G, TOPK, DIM], F32))
        o = ctx.enter_context(nc.sbuf_tensor("c_o", [P, B, G, DIM], F32))
        stats = ctx.enter_context(nc.sbuf_tensor("c_stats", [P, G, 6], F32))
        mv = ctx.enter_context(nc.sbuf_tensor("c_mv", [P, B, G, 2], F32))
        var = ctx.enter_context(nc.sbuf_tensor("c_var", [P, B, G], F32))
        rstd = ctx.enter_context(nc.sbuf_tensor("c_rstd", [P, B, G], F32))
        sem = lambda name: ctx.enter_context(nc.semaphore(name))
        loaded = [sem(f"c_loaded{k}") for k in range(B)]
        stored = [sem(f"c_stored{k}") for k in range(B)]
        chain = sem("c_chain")
        rstd_done = sem("c_rstd_done")
        o_done = sem("c_o_done")
        block = ctx.enter_context(nc.Block())
        y_v = d.y[0:TRASH, :].rearrange("(i p k) n -> p i k n", p=P, k=TOPK)
        o_v = d.out.rearrange("(i p) n -> p i n", p=P)

        @block.sync
        def _(sp):
            for m in range(N):
                if m >= B:
                    sp.wait_ge(o_done, m - B + 1)
                sp.dma_start(ye[:, m % B], y_v[:, G * m:G * m + G]).then_inc(loaded[m % B], 16)
                b, j = divmod(G * m, TT)
                sp.dma_start(x1[:, m % B], d.x1[b, :, j:j + G, :]).then_inc(loaded[m % B], 16)

        @block.scalar
        def _(act):
            for m in range(N):
                act.wait_ge(o_done, m + 1)
                act.dma_start(o_v[:, G * m:G * m + G, :], o[:, m % B]).then_inc(stored[m % B], 16)
            for k in range(B):
                act.wait_ge(stored[k], 16 * len(range(k, N, B)))

        @block.gpsimd
        def _(pool):
            for m in range(N):
                pool.wait_ge(chain, 5 * m + 5)
                nc.gpsimd.tensor_tensor(rstd[:, m % B], var[:, m % B], t.minus_half[:, 0:G], ALU.pow)\
                    .then_inc(rstd_done, 1)

        @block.vector
        def _(dve):
            def finish(m):
                b = m % B
                dve.wait_ge(rstd_done, m + 1)
                for g in range(G):
                    last = nc.vector.tensor_scalar(o[:, b, g, :], o[:, b, g, :], mv[:, b, g, 0:1],
                                                   rstd[:, b, g:g + 1], ALU.subtract, ALU.mult)
                last.then_inc(o_done, 1)

            for m in range(N):
                b = m % B
                links = [5 * m]

                def link(ins):
                    links[0] += 1
                    ins.then_inc(chain, 1)
                    dve.wait_ge(chain, links[0])

                dve.wait_ge(loaded[b], 32 * (m // B + 1))
                if m >= B:
                    dve.wait_ge(stored[b], 16 * (m // B))
                link(nc.vector.tensor_tensor(o[:, b], ye[:, b, :, 0, :], ye[:, b, :, 1, :], ALU.add))
                link(nc.vector.tensor_tensor(o[:, b], o[:, b], x1[:, b], ALU.add))
                for g in range(G):
                    last = nc.vector.bn_stats(stats[:, g, :], o[:, b, g, :])
                link(last)
                for g in range(G):
                    last = nc.vector.bn_aggr(mv[:, b, g, :], stats[:, g, :])
                link(last)
                nc.vector.tensor_scalar(var[:, b], mv[:, b, :, 1], EPS, None, ALU.add).then_inc(chain, 1)
                if m >= 1:
                    finish(m - 1)
            finish(N - 1)


class Names:
    pass


def build(nc, d):
    d.bc = nc.dram_tensor("bc_rows", [BLOCKS, 2 * STATE, T], F32, kind="Internal").ap()
    d.x1 = nc.dram_tensor("x1_rows", [BLOCKS, P, TT, DIM], F32, kind="Internal").ap()
    d.rows = nc.dram_tensor("expert_rows", [EXPERTS * REGION + P, ROW], F32, kind="Internal").ap()
    d.y = nc.dram_tensor("expert_out", [TRASH + SLOTS * P, DIM], F32, kind="Internal").ap()
    t = Names()
    with ExitStack() as ctx:
        def sb(name, shape, dt=F32):
            return ctx.enter_context(nc.sbuf_tensor(name, shape, dt))

        t.ident = sb("ident", [P, P])
        t.before = sb("before", [P, P])
        t.ones = sb("ones", [P, P])
        t.minus_half = sb("minus_half", [P, TT])
        t.iota_e = sb("iota_e", [P, EXPERTS], I32)
        t.iota_ef = sb("iota_ef", [P, EXPERTS])
        t.iota_t = sb("iota_t", [P, TT], I32)
        t.token2 = sb("token2", [P, TT])
        t.base = sb("base", [P, EXPERTS])
        with ExitStack() as phase:
            def sb(name, shape, dt=F32):
                return phase.enter_context(nc.sbuf_tensor(name, shape, dt))

            t.w_in = sb("w_in", [P, KC, 2 * INNER])
            t.conv_w = sb("conv_w", [P, EC, TAPS])
            t.conv_b = sb("conv_b", [P, EC])
            t.w_x = sb("w_x", [P, EC, 1 + 2 * STATE])
            t.w_dt = sb("w_dt", [1, INNER])
            t.b_dt = sb("b_dt", [P, EC])
            t.neg_a = sb("neg_a", [P, STATE])
            t.d_col = sb("d_col", [P, EC])
            t.diag_d = sb("diag_d", [P, EC, P])
            t.w_out = sb("w_out", [P, EC, DIM])
            t.router = sb("router", [P, KC, EXPERTS])
            t.zeros = sb("zeros", [P, EC, TAPS])
            t.xp = sb("xp", [P, EC, T + TAPS - 1])
            t.decay = sb("decay", [P, DA_RING, EC, T + 1])
            setup(nc, d, t)
            mamba(nc, d, t)
        experts(nc, d, t)
        combine(nc, d, t)


def kernel(L0_attn_x, L0_attn_W_in, L0_attn_conv_w, L0_attn_conv_b, L0_attn_W_x, L0_attn_W_dt, L0_attn_b_dt,
           L0_attn_A_log, L0_attn_D, L0_attn_W_out, L0_ffn_router_w, L0_ffn_expert_w1, L0_ffn_expert_b1,
           L0_ffn_expert_w2, L0_ffn_expert_b2):
    import concourse.bacc as bacc
    from concourse.bass_utils import run_bass_kernel_spmd

    def lay(a):
        return np.ascontiguousarray(a)

    def columns(a):
        return lay(a.reshape(EC, P, -1).transpose(1, 0, 2))

    x = np.asarray(L0_attn_x)
    w_x = np.asarray(L0_attn_W_x)
    arrays = {
        "x_t": lay(x.reshape(BLOCKS, T, KC, P).transpose(0, 3, 2, 1)),
        "x_tok": lay(x.reshape(BLOCKS, TT, P, DIM).transpose(0, 2, 1, 3)),
        "w_in": lay(np.asarray(L0_attn_W_in).T),
        "conv_w": columns(np.asarray(L0_attn_conv_w)),
        "conv_b": columns(np.asarray(L0_attn_conv_b))[:, :, 0],
        "w_x": lay(np.concatenate([w_x[2 * STATE:], w_x[:2 * STATE]]).T),
        "w_dt": lay(np.asarray(L0_attn_W_dt).T),
        "b_dt": columns(np.asarray(L0_attn_b_dt))[:, :, 0],
        "a_log": lay(np.asarray(L0_attn_A_log)),
        "d_skip": columns(np.asarray(L0_attn_D))[:, :, 0],
        "w_out": lay(np.asarray(L0_attn_W_out).T),
        "router": lay(np.asarray(L0_ffn_router_w).T),
        "w1": lay(np.asarray(L0_ffn_expert_w1).transpose(0, 2, 1)),
        "b1": lay(np.asarray(L0_ffn_expert_b1)),
        "w2": lay(np.asarray(L0_ffn_expert_w2).transpose(0, 2, 1)),
        "b2": lay(np.asarray(L0_ffn_expert_b2)),
    }
    arrays = {f"in_{n}": lay(a) for n, a in arrays.items()}
    nc = bacc.Bacc("TRN2", target_bir_lowering=False, num_devices=1)
    d = Names()
    d.x_t = nc.dram_tensor("in_x_t", arrays["in_x_t"].shape, F32, kind="ExternalInput").ap()
    d.x_tok = nc.dram_tensor("in_x_tok", arrays["in_x_tok"].shape, F32, kind="ExternalInput").ap()
    d.w_in = nc.dram_tensor("in_w_in", arrays["in_w_in"].shape, F32, kind="ExternalInput").ap()
    d.conv_w = nc.dram_tensor("in_conv_w", arrays["in_conv_w"].shape, F32, kind="ExternalInput").ap()
    d.conv_b = nc.dram_tensor("in_conv_b", arrays["in_conv_b"].shape, F32, kind="ExternalInput").ap()
    d.w_x = nc.dram_tensor("in_w_x", arrays["in_w_x"].shape, F32, kind="ExternalInput").ap()
    d.w_dt = nc.dram_tensor("in_w_dt", arrays["in_w_dt"].shape, F32, kind="ExternalInput").ap()
    d.b_dt = nc.dram_tensor("in_b_dt", arrays["in_b_dt"].shape, F32, kind="ExternalInput").ap()
    d.a_log = nc.dram_tensor("in_a_log", arrays["in_a_log"].shape, F32, kind="ExternalInput").ap()
    d.d_skip = nc.dram_tensor("in_d_skip", arrays["in_d_skip"].shape, F32, kind="ExternalInput").ap()
    d.w_out = nc.dram_tensor("in_w_out", arrays["in_w_out"].shape, F32, kind="ExternalInput").ap()
    d.router = nc.dram_tensor("in_router", arrays["in_router"].shape, F32, kind="ExternalInput").ap()
    d.w1 = nc.dram_tensor("in_w1", arrays["in_w1"].shape, F32, kind="ExternalInput").ap()
    d.b1 = nc.dram_tensor("in_b1", arrays["in_b1"].shape, F32, kind="ExternalInput").ap()
    d.w2 = nc.dram_tensor("in_w2", arrays["in_w2"].shape, F32, kind="ExternalInput").ap()
    d.b2 = nc.dram_tensor("in_b2", arrays["in_b2"].shape, F32, kind="ExternalInput").ap()
    d.out = nc.dram_tensor("out_0", (TOKENS, DIM), F32, kind="ExternalOutput").ap()
    build(nc, d)
    got = run_bass_kernel_spmd(nc, [arrays], core_ids=[0])
    return got.results[0]["out_0"].reshape(SEQS, SEQ, DIM)
```

```python
from contextlib import ExitStack

import numpy as np
import concourse.bass as bass
from concourse import mybir

ALU = mybir.AluOpType
ACT = mybir.ActivationFunctionType
AXX = mybir.AxisListType.X
F32 = mybir.dt.float32
I32 = mybir.dt.int32
U32 = mybir.dt.uint32

P = 128
SEQS, SEQ, DIM = 4, 1024, 256
INNER, STATE, TAPS = 512, 16, 4
FF, EXPERTS, TOPK = 1024, 8, 2
TOKENS = SEQS * SEQ

T = 512
BLOCKS = TOKENS // T
HALVES = SEQ // T
KC = DIM // P
EC = INNER // P
TT = T // P
ROW = DIM + 4
REGION = TOKENS + P
SLOTS = TOKENS * TOPK // P + EXPERTS
TRASH = TOKENS * TOPK
EPS = 1e-5

S_RING = 4
P_RING = 4
BC_RING = 4
C_LAG = 3
DA_RING = 2
X_RING = 4
POOL_DBX = [1] * STATE
POOL_HC = [0] * STATE


def hold(eng, held):
    eng.sem_inc(held, 1)


def setup(nc, d, t):
    with ExitStack() as ctx:
        loaded = ctx.enter_context(nc.semaphore("setup_loaded"))
        pool_done = ctx.enter_context(nc.semaphore("setup_pool"))
        exp_done = ctx.enter_context(nc.semaphore("setup_exp"))
        dve_done = ctx.enter_context(nc.semaphore("setup_dve"))
        block = ctx.enter_context(nc.Block())
        loads = [(t.w_in, d.w_in.rearrange("(k p) n -> p k n", p=P)),
                 (t.conv_w, d.conv_w), (t.conv_b, d.conv_b),
                 (t.w_x, d.w_x.rearrange("(c p) n -> p c n", p=P)),
                 (t.w_dt, d.w_dt), (t.dt_col, d.dt_col), (t.b_dt, d.b_dt),
                 (t.neg_a, d.a_log.partition_broadcast(P)),
                 (t.d_col, d.d_skip),
                 (t.w_out, d.w_out.rearrange("(c p) n -> p c n", p=P)),
                 (t.router, d.router.rearrange("(k p) n -> p k n", p=P))]

        @block.sync
        def _(sp):
            for dst, src in loads:
                sp.dma_start(dst[:], src).then_inc(loaded, 16)

        @block.gpsimd
        def _(pool):
            nc.gpsimd.memset(t.ident[:], 0.0).then_inc(pool_done, 1)
            nc.gpsimd.memset(t.before[:], 1.0).then_inc(pool_done, 1)
            nc.gpsimd.memset(t.ones[:], 1.0).then_inc(pool_done, 1)
            nc.gpsimd.memset(t.minus_half[:], -0.5).then_inc(pool_done, 1)
            nc.gpsimd.iota(t.iota_e[:], pattern=[[1, EXPERTS]], base=0, channel_multiplier=0).then_inc(pool_done, 1)
            nc.gpsimd.iota(t.iota_t[:], pattern=[[2 * P, TT]], base=0, channel_multiplier=2).then_inc(pool_done, 1)
            pool.wait_ge(pool_done, 6)
            nc.gpsimd.affine_select(out=t.ident[:], in_=t.ident[:], compare_op=ALU.not_equal, fill=1.0, base=0,
                                    pattern=[[-1, P]], channel_multiplier=1).then_inc(pool_done, 1)
            nc.gpsimd.affine_select(out=t.before[:], in_=t.before[:], compare_op=ALU.is_gt, fill=0.0, base=0,
                                    pattern=[[1, P]], channel_multiplier=-1).then_inc(pool_done, 1)

        @block.scalar
        def _(act):
            act.wait_ge(loaded, 16 * len(loads))
            nc.scalar.activation(t.neg_a[:], t.neg_a[:], ACT.Exp).then_inc(exp_done, 1)

        @block.vector
        def _(dve):
            nc.vector.memset(t.zeros[:], 0.0)
            nc.vector.memset(t.base[:], 0.0)
            for k in range(DA_RING):
                nc.vector.memset(t.decay[:, k, :, 0:1], 0.0)
            dve.wait_ge(pool_done, 8)
            nc.vector.tensor_copy(t.iota_ef[:], t.iota_e[:])
            nc.vector.tensor_copy(t.token2[:], t.iota_t[:])
            dve.wait_ge(exp_done, 1)
            nc.vector.tensor_scalar(t.neg_a[:], t.neg_a[:], -1.0, None, ALU.mult)
            for c in range(EC):
                nc.vector.tensor_scalar(t.diag_d[:, c, :], t.ident[:], t.d_col[:, c:c + 1], None, ALU.mult)
                nc.vector.tensor_scalar(t.w_xdt[:, c, :], t.ones[:], t.dt_col[:, c:c + 1], None, ALU.mult)
            nc.vector.memset(t.xp[:, :, T:T + TAPS - 1], 0.0).then_inc(dve_done, 1)
            dve.wait_ge(dve_done, 1)


def mamba(nc, d, t):
    with ExitStack() as ctx:
        def sb(name, shape, dt=F32):
            return ctx.enter_context(nc.sbuf_tensor(name, shape, dt))

        def ps(name, shape):
            return ctx.enter_context(nc.psum_tensor(name, shape, F32))

        def sem(name):
            return ctx.enter_context(nc.semaphore(name))

        x_t = sb("x_t", [P, 2, KC, T])
        x_tok = sb("x_tok", [P, TT, DIM])
        xc = sb("xc", [P, 2, EC, T])
        dt = sb("dt", [P, 2, EC, T])
        u = sb("u", [P, 2, EC, T])
        ssm = sb("ssm", [2 * STATE, T])
        scan = sb("scan", [P, S_RING, EC, T + 1])
        prod = sb("prod", [P, P_RING, EC, T])
        b_row = sb("b_row", [P, BC_RING, T])
        c_row = sb("c_row", [P, BC_RING, T])
        carry = sb("carry", [P, STATE, EC])
        ys = sb("ys", [P, EC, T])
        xrow = sb("xrow", [P, 2, TT, ROW])
        x1_t = sb("x1_t", [P, TT, KC, P])
        stats = sb("stats", [P, TT, 6])
        mv = sb("mv", [P, TT, 2])
        var = sb("var", [P, TT])
        rstd = sb("rstd", [P, TT])
        logit = sb("logit", [P, TT, EXPERTS])
        ex = sb("ex", [P, TT, EXPERTS])
        mx = sb("mx", [P, TT])
        prob = sb("prob", [P, TT, EXPERTS])
        top = sb("top", [P, TT, 8])
        idx = sb("idx", [P, TT, 8], U32)
        wk = sb("wk", [P, TT, TOPK])
        ek = sb("ek", [P, TT, TOPK])
        onehot = sb("onehot", [P, TT, TOPK, EXPERTS])
        member = sb("member", [P, TT + 1, EXPERTS])
        rank = sb("rank", [P, TT, EXPERTS])
        rsel = sb("rsel", [P, TT, TOPK, EXPERTS])
        rk = sb("rk", [P, TT, TOPK])
        pos = sb("pos", [P, 2, TT, TOPK], U32)

        y_ps = ps("y_ps", [P, EC, T])
        in_ps = ps("in_ps", [P, 2, T])
        aux_ps = ps("aux_ps", [P, T])
        out_ps = ps("out_ps", [P, 2, DIM])

        xt_loaded = [sem(f"xt_loaded{k}") for k in range(2)]
        xtok_loaded = sem("xtok_loaded")
        inproj_done = sem("inproj_done")
        halo_done = sem("halo_done")
        xp_done = sem("xp_done")
        tap_done = sem("tap_done")
        silu_done = sem("silu_done")
        ssm_ps_done = sem("ssm_ps_done")
        ssm_done = sem("ssm_done")
        bc_stored = sem("bc_stored")
        b_loaded = [sem(f"b_loaded{k}") for k in range(BC_RING)]
        c_loaded = [sem(f"c_loaded{k}") for k in range(BC_RING)]
        z_done = sem("z_done")
        z_read = sem("z_read")
        ln_done = sem("ln_done")
        dt_done = sem("dt_done")
        u_done = sem("u_done")
        carried_in = sem("carried_in")
        carried_out = sem("carried_out")
        decay_done = sem("decay_done")
        dbx_pool, dbx_dve = sem("dbx_pool"), sem("dbx_dve")
        hc_pool, hc_dve = sem("hc_pool"), sem("hc_dve")
        scan_done = sem("scan_done")
        sum_done = sem("sum_done")
        ys_done = sem("ys_done")
        outproj_done = sem("outproj_done")
        pre_done = sem("pre_done")
        stats_done = sem("stats_done")
        norm_chain = sem("norm_chain")
        rstd_done = sem("rstd_done")
        x1_done = sem("x1_done")
        x1_stored = [sem(f"x1_stored{k}") for k in range(2)]
        turned = sem("turned")
        turned_read = sem("turned_read")
        logit_ps_done = sem("logit_ps_done")
        logit_done = sem("logit_done")
        route = sem("route")
        shifted = sem("shifted")
        place_chain = sem("place_chain")
        ex_done = sem("ex_done")
        member_done = sem("member_done")
        rank_ps_done = sem("rank_ps_done")
        rank_read = sem("rank_read")
        pos_done = sem("pos_done")
        rows_sent = [sem(f"rows_sent{k}") for k in range(2)]
        rows_free = sem("rows_free")
        held_sp, held_act, held_dve, held_pool = sem("held_sp"), sem("held_act"), sem("held_dve"), sem("held_pool")
        block = ctx.enter_context(nc.Block())

        n_pd, n_ph = sum(POOL_DBX), sum(POOL_HC)

        def earlier(i, n, k):
            return (i, n - k) if n >= k else (i - 1, n - k + STATE)

        def known_past(i):
            return not isinstance(i, int) or i >= 0

        def wait_dbx(eng, i, n):
            if not known_past(i):
                return
            if POOL_DBX[n]:
                eng.wait_ge(dbx_pool, n_pd * i + sum(POOL_DBX[:n + 1]))
            else:
                eng.wait_ge(dbx_dve, (STATE - n_pd) * i + n + 1 - sum(POOL_DBX[:n + 1]))

        def wait_hc(eng, i, n):
            if not known_past(i):
                return
            if POOL_HC[n]:
                eng.wait_ge(hc_pool, n_ph * i + sum(POOL_HC[:n + 1]))
            else:
                eng.wait_ge(hc_dve, (STATE - n_ph) * i + n + 1 - sum(POOL_HC[:n + 1]))

        def wait_past(eng, s, per, i, n):
            if known_past(i):
                eng.wait_ge(s, per * i + n)

        def wait_row(eng, loaded, i, n):
            eng.wait_ge(loaded[n % BC_RING], (16 * STATE // BC_RING) * i + 16 * (n // BC_RING + 1))

        def steps(eng, step):
            step(-1, 1, False, True, False, False)
            step(0, 0, True, True, False, False)
            step(1, 1, True, True, True, False)
            with eng.Fori(0, SEQS - 2) as q:
                i = 2 * q + 2
                step(i, 0, True, True, True, True)
                step(i + 1, 1, True, True, True, True)
            step(BLOCKS - 2, 0, True, True, True, True)
            step(BLOCKS - 1, 1, True, False, True, True)
            step(BLOCKS, 0, False, False, True, True)
            step(BLOCKS + 1, 1, False, False, False, True)

        @block.sync
        def _(sp):
            def step(i, half, scans, front, back, place):
                f, r, fp, rp = i + 1, i - 1, 1 - half, 1 - half
                if front:
                    wait_past(sp, sum_done, STATE, f - 2, KC * EC + 2)
                    hold(sp, held_sp)
                    sp.dma_start(x_t[:, fp], d.x_t[f]).then_inc(xt_loaded[fp], 16)
                if back:
                    wait_past(sp, pre_done, TT, r - 1, TT)
                    hold(sp, held_sp)
                    sp.dma_start(x_tok[:], d.x_tok[r]).then_inc(xtok_loaded, 16)
                def load_b(n):
                    if n == 0:
                        sp.wait_ge(bc_stored, 16 * i + 16)
                        hold(sp, held_sp)
                    wait_dbx(sp, *earlier(i, n, BC_RING))
                    hold(sp, held_sp)
                    sp.dma_start(b_row[:, n % BC_RING], d.bc[i, n, :].partition_broadcast(P))\
                        .then_inc(b_loaded[n % BC_RING], 16)

                def load_c(i, n):
                    wait_hc(sp, *earlier(i, n, BC_RING))
                    hold(sp, held_sp)
                    sp.dma_start(c_row[:, n % BC_RING], d.bc[i, STATE + n, :].partition_broadcast(P))\
                        .then_inc(c_loaded[n % BC_RING], 16)

                for n in range(STATE):
                    if scans:
                        load_b(n)
                        if n >= C_LAG:
                            load_c(i, n - C_LAG)
                    if back and n < C_LAG:
                        load_c(i - 1, n - C_LAG + STATE)

            steps(sp, step)

        @block.tensor
        def _(pe):
            def step(i, half, scans, front, back, place):
                f, r, fp, par = i + 1, i - 1, 1 - half, half

                def in_projection(c):
                    if c == 0:
                        pe.wait_ge(xt_loaded[fp], 16 * ((f - fp) // 2 + 1) if isinstance(f, int)
                                   else 8 * (f - fp) + 16)
                        wait_past(pe, z_read, 2 * EC, f - 1, 2 * EC)
                        if place:
                            pe.wait_ge(turned_read, 2 * (i - 2) + 2)
                    if c >= 2:
                        pe.wait_ge(xp_done, EC * f + c - 1)
                    for k in range(KC):
                        last = nc.tensor.matmul(in_ps[:, c % 2, :], t.w_in[:, k, c * P:(c + 1) * P],
                                                x_t[:, fp, k, :], start=(k == 0), stop=(k == KC - 1))
                    last.then_inc(inproj_done, 1)

                def ssm_projection():
                    pe.wait_ge(silu_done, f + 1)
                    if place:
                        pe.wait_ge(logit_done, i - 1)
                    for c in range(EC):
                        last = nc.tensor.matmul(aux_ps[0:2 * STATE, :], t.w_x[:, c, :], xc[:, fp, c, :],
                                                start=(c == 0), stop=(c == EC - 1))
                    last.then_inc(ssm_ps_done, 1)
                    pe.wait_ge(xp_done, EC * f + EC)
                    for c in range(EC):
                        last = nc.tensor.matmul(in_ps[:, 0, :], t.w_xdt[:, c, :], xc[:, fp, c, :],
                                                start=(c == 0), stop=(c == EC - 1))
                    last.then_inc(z_done, 1)

                def skip_terms(m):
                    c = m % EC
                    if m < KC * EC:
                        k = m // EC
                        nc.tensor.matmul(y_ps[:, c, :], t.w_in[:, k, INNER + c * P:INNER + (c + 1) * P],
                                         x_t[:, par, k, :], start=False, stop=False)
                    else:
                        nc.tensor.matmul(y_ps[:, c, :], t.diag_d[:, c, :], xc[:, par, c, :],
                                         start=False, stop=False)

                def sum_states(n):
                    wait_hc(pe, i, n)
                    if n == 0:
                        wait_past(pe, ys_done, 1, i - 1, 1)
                    for c in range(EC):
                        last = nc.tensor.matmul(y_ps[:, c, :], t.ident[:], prod[:, n % P_RING, c, :],
                                                start=(n == 0), stop=(n == STATE - 1))
                    last.then_inc(sum_done, 1)

                def out_projection(j):
                    if j == 0:
                        pe.wait_ge(ys_done, r + 1)
                    if j == 2:
                        pe.wait_ge(pre_done, TT * r + 2)
                    if j == 0:
                        wait_past(pe, pre_done, TT, r - 1, TT)
                        wait_past(pe, rank_read, 1, i - 3, 1)
                    for c in range(EC):
                        last = nc.tensor.matmul(out_ps[:, j % 2, :], ys[:, c, j * P:(j + 1) * P],
                                                t.w_out[:, c, :], start=(c == 0), stop=(c == EC - 1))
                    if j % 2 == 1:
                        last.then_inc(outproj_done, 1)

                def turn(h):
                    if h == 0:
                        pe.wait_ge(x1_done, TT * r + TT)
                    elif front:
                        pe.wait_ge(ssm_done, f + 1)
                    elif place:
                        pe.wait_ge(logit_done, i - 1)
                    for jj in range(2):
                        for k in range(KC):
                            at = (jj * KC + k) * P
                            dst = in_ps[:, 1, at:at + P] if h == 0 else aux_ps[:, at:at + P]
                            last = nc.tensor.transpose(dst, xrow[:, 1 - par, 2 * h + jj, k * P:(k + 1) * P],
                                                       t.ident[:])
                    last.then_inc(turned, 1)

                def logits():
                    pe.wait_ge(turned_read, 2 * (i - 2) + 2)
                    for j in range(TT):
                        for k in range(KC):
                            last = nc.tensor.matmul(aux_ps[:, j * EXPERTS:(j + 1) * EXPERTS], x1_t[:, j, k, :],
                                                    t.router[:, k, :], start=(k == 0), stop=(k == KC - 1))
                    last.then_inc(logit_ps_done, 1)

                def ranks():
                    pe.wait_ge(member_done, i - 1)
                    if back:
                        pe.wait_ge(pre_done, TT * r + TT)
                    flat = member[:].rearrange("p j e -> p (j e)")
                    dst = out_ps[:].rearrange("p h n -> p (h n)")
                    nc.tensor.matmul(dst[:, 0:(TT + 1) * EXPERTS], t.before[:], flat, start=True, stop=False)
                    for k in range(TT):
                        n_after = TT - k
                        last = nc.tensor.matmul(
                            dst[:, (k + 1) * EXPERTS:(TT + 1) * EXPERTS].rearrange("p (j e) -> p j e", e=EXPERTS),
                            t.ones[:], member[:, k:k + 1, :].broadcast_to([P, n_after, EXPERTS]),
                            start=False, stop=(k == TT - 1))
                    last.then_inc(rank_ps_done, 1)

                for n in range(STATE):
                    if scans:
                        sum_states(n)
                        if 1 <= n <= 12:
                            skip_terms(n - 1)
                    if place and n == 0:
                        logits()
                    if front:
                        if n <= 3:
                            in_projection(n)
                        if n == 8:
                            ssm_projection()
                    if back:
                        if n == 2 or n == 6:
                            out_projection(0 if n == 2 else 2)
                            out_projection(1 if n == 2 else 3)
                    if place and n == 9:
                        ranks()
                    if back:
                        if n == 13:
                            turn(0)
                            turn(1)

            steps(pe, step)

        @block.scalar
        def _(act):
            def step(i, half, scans, front, back, place):
                f, r, fp, par = i + 1, i - 1, 1 - half, half

                def halo():
                    wait_past(act, tap_done, TAPS * EC, f - 1, TAPS * EC)
                    wait_past(act, dt_done, 1, f - 1, 1)
                    src = t.xp[:, :, T:T + TAPS - 1] if fp == 1 else t.zeros[:, :, 0:TAPS - 1]
                    nc.scalar.copy(t.xp[:, :, 0:TAPS - 1], src).then_inc(halo_done, 1)

                def xp_out(c):
                    act.wait_ge(inproj_done, EC * f + c + 1)
                    if c == 0:
                        act.wait_ge(halo_done, f + 1)
                    nc.scalar.copy(t.xp[:, c, TAPS - 1:], in_ps[:, c % 2, :]).then_inc(xp_done, 1)

                def silu():
                    act.wait_ge(tap_done, TAPS * EC * (f + 1))
                    nc.scalar.activation(xc[:, fp], xc[:, fp], ACT.Silu).then_inc(silu_done, 1)

                def ssm_out():
                    act.wait_ge(ssm_ps_done, f + 1)
                    wait_past(act, bc_stored, 16, f - 1, 16)
                    nc.scalar.copy(ssm[:], aux_ps[0:2 * STATE, :]).then_inc(ssm_done, 1)
                    act.wait_ge(ssm_done, f + 1)
                    hold(act, held_act)
                    act.dma_start(d.bc[f], ssm[:]).then_inc(bc_stored, 16)

                def store_x1():
                    act.wait_ge(x1_done, TT * r + TT)
                    hold(act, held_act)
                    act.dma_start(d.x1[r], xrow[:, 1 - half, :, 0:DIM]).then_inc(x1_stored[1 - half], 16)

                def z_parts(c):
                    act.wait_ge(z_done, f + 1)
                    if c == 0:
                        wait_past(act, decay_done, STATE, f - 2, STATE)
                    nc.scalar.activation(t.xp[:, c, 0:T], in_ps[:, 0, :], ACT.Abs,
                                         bias=t.b_dt[:, c:c + 1], scale=t.w_dt[:, c:c + 1]).then_inc(z_read, 1)
                    nc.scalar.activation(dt[:, fp, c, :], in_ps[:, 0, :], ACT.Relu,
                                         bias=t.b_dt[:, c:c + 1], scale=t.w_dt[:, c:c + 1]).then_inc(z_read, 1)

                def soft_tail():
                    act.wait_ge(z_read, 2 * EC * (f + 1))
                    nc.scalar.activation(t.xp[:, :, 0:T], t.xp[:, :, 0:T], ACT.Exp, scale=-1.0).then_inc(ln_done, 1)
                    act.wait_ge(ln_done, 2 * f + 1)
                    nc.scalar.activation(t.xp[:, :, 0:T], t.xp[:, :, 0:T], ACT.Ln, bias=t.ones[:, 0:1])\
                        .then_inc(ln_done, 1)

                def carry_in(n):
                    wait_hc(act, *earlier(i, n, S_RING))
                    if par == 1:
                        act.wait_ge(carried_out, STATE * ((i - 1) // 2) + n + 1 if isinstance(i, int)
                                    else 8 * (i - 1) + n + 1)
                    src = carry[:, n, :].unsqueeze(2) if par == 1 else t.zeros[:, :, 0:1]
                    nc.scalar.copy(scan[:, n % S_RING, :, 0:1], src).then_inc(carried_in, 1)

                def carry_out(n):
                    act.wait_ge(scan_done, STATE * i + n + 1)
                    nc.scalar.copy(carry[:, n, :].unsqueeze(2), scan[:, n % S_RING, :, T:T + 1])\
                        .then_inc(carried_out, 1)

                def decays(n):
                    if n == 0:
                        act.wait_ge(dt_done, i + 1)
                    wait_past(act, scan_done, STATE, *[(a, b + 1) for a, b in [earlier(i, n, DA_RING)]][0])
                    nc.scalar.activation(t.decay[:, n % DA_RING, :, 1:], dt[:, par], ACT.Exp,
                                         scale=t.neg_a[:, n:n + 1]).then_inc(decay_done, 1)

                def y_silu():
                    act.wait_ge(sum_done, STATE * (r + 1))
                    wait_past(act, outproj_done, 2, r - 1, 2)
                    nc.scalar.activation(ys[:], y_ps[:], ACT.Silu).then_inc(ys_done, 1)

                def turned_out(h):
                    act.wait_ge(turned, 2 * (i - 2) + h + 1)
                    wait_past(act, logit_ps_done, 1, i - 3, 1)
                    nc.scalar.copy(x1_t[:, 2 * h:2 * h + 2].rearrange("p j k q -> p (j k q)"),
                                   in_ps[:, 1, :] if h == 0 else aux_ps[:])\
                        .then_inc(turned_read, 1)

                def router_exp():
                    act.wait_ge(shifted, i - 1)
                    nc.scalar.activation(ex[:], ex[:], ACT.Exp).then_inc(ex_done, 1)

                for n in range(STATE):
                    if scans:
                        if n == 0:
                            carry_in(0)
                        if n < STATE - 1:
                            carry_in(n + 1)
                        decays(n)
                        if par == 0 and n >= 2:
                            carry_out(n - 2)
                    if place:
                        if n == 0:
                            turned_out(0)
                            turned_out(1)
                        if n == 5:
                            router_exp()
                    if back and n == 2:
                        y_silu()
                    if front:
                        if n == 1:
                            halo()
                        if 4 <= n <= 7:
                            xp_out(n - 4)
                        if n == 10:
                            silu()
                        if n == 12:
                            ssm_out()
                            z_parts(0)
                            z_parts(1)
                            z_parts(2)
                            z_parts(3)
                        if n == 13:
                            soft_tail()
                    if back and n == 15:
                        store_x1()
                if scans and par == 0:
                    carry_out(STATE - 2)
                    carry_out(STATE - 1)

            for k in range(2):
                act.sem_inc(x1_stored[k], 16)
            steps(act, step)
            for k in range(2):
                act.wait_ge(x1_stored[k], 16 * BLOCKS // 2 + 16)

        LINKS = 11
        PLACE_LINKS = 6

        @block.vector
        def _(dve):
            def step(i, half, scans, front, back, place):
                f, r, fp, par, rp = i + 1, i - 1, 1 - half, half, 1 - half

                def tap(c, k):
                    col = TAPS - 1 - k
                    src = t.xp[:, c, col:col + T]
                    if k == 0:
                        dve.wait_ge(xp_done, EC * f + c + 1)
                        if c == 0:
                            wait_past(dve, sum_done, STATE, f - 2, STATE)
                        nc.vector.tensor_scalar(xc[:, fp, c, :], src, t.conv_w[:, c, col:col + 1],
                                                t.conv_b[:, c:c + 1], ALU.mult, ALU.add).then_inc(tap_done, 1)
                        return
                    dve.wait_ge(tap_done, TAPS * EC * f + TAPS * c + k)
                    nc.vector.scalar_tensor_tensor(out=xc[:, fp, c, :], in0=src, scalar=t.conv_w[:, c, col:col + 1],
                                                   in1=xc[:, fp, c, :], op0=ALU.mult, op1=ALU.add)\
                        .then_inc(tap_done, 1)

                def step_sizes():
                    dve.wait_ge(ln_done, 2 * f + 2)
                    nc.vector.tensor_tensor(dt[:, fp], dt[:, fp], t.xp[:, :, 0:T], ALU.add).then_inc(dt_done, 1)
                    dve.wait_ge(dt_done, f + 1)
                    wait_dbx(dve, f - 2, STATE - 1)
                    nc.vector.tensor_tensor(u[:, fp], dt[:, fp], xc[:, fp], ALU.mult).then_inc(u_done, 1)

                def dbx(n):
                    wait_row(dve, b_loaded, i, n)
                    dve.wait_ge(carried_in, STATE * i + n + 1)
                    dve.wait_ge(u_done, i + 1)
                    nc.vector.tensor_tensor(scan[:, n % S_RING, :, 1:], u[:, par],
                                            b_row[:, n % BC_RING:n % BC_RING + 1, :].broadcast_to([P, EC, T]), ALU.mult)\
                        .then_inc(dbx_dve, 1)

                def hc(n):
                    wait_row(dve, c_loaded, i, n)
                    dve.wait_ge(scan_done, STATE * i + n + 1)
                    wait_past(dve, sum_done, STATE, *[(a, b + 1) for a, b in [earlier(i, n, P_RING)]][0])
                    nc.vector.tensor_tensor(prod[:, n % P_RING], scan[:, n % S_RING, :, 1:],
                                            c_row[:, n % BC_RING:n % BC_RING + 1, :].broadcast_to([P, EC, T]), ALU.mult)\
                        .then_inc(hc_dve, 1)

                def recurrence(n):
                    dve.wait_ge(decay_done, STATE * i + n + 1)
                    dve.wait_ge(carried_in, STATE * i + n + 1)
                    wait_dbx(dve, i, n)
                    line = scan[:, n % S_RING].rearrange("p c t -> p (c t)")
                    nc.vector.tensor_tensor_scan(line, t.decay[:, n % DA_RING].rearrange("p c t -> p (c t)"), line,
                                                 0.0, ALU.mult, ALU.add).then_inc(scan_done, 1)

                def residual(j):
                    dve.wait_ge(outproj_done, 2 * r + j // 2 + 1)
                    if j == 0:
                        dve.wait_ge(xtok_loaded, 16 * (r + 1))
                        dve.wait_ge(x1_stored[rp], 8 * (r - rp) + 16)
                        dve.wait_ge(rows_free, r + 1)
                    nc.vector.tensor_tensor(xrow[:, rp, j, 0:DIM], out_ps[:, j % 2, :], x_tok[:, j, :], ALU.add)\
                        .then_inc(pre_done, 1)

                def moments(j):
                    dve.wait_ge(pre_done, TT * r + j + 1)
                    nc.vector.bn_stats(stats[:, j, :], xrow[:, rp, j, 0:DIM]).then_inc(stats_done, 1)

                def variance():
                    dve.wait_ge(stats_done, TT * (r + 1))
                    wait_past(dve, x1_done, TT, r - 1, TT)
                    hold(dve, held_dve)
                    for j in range(TT):
                        last = nc.vector.bn_aggr(mv[:, j, :], stats[:, j, :])
                    last.then_inc(norm_chain, 1)
                    dve.wait_ge(norm_chain, 2 * r + 1)
                    nc.vector.tensor_scalar(var[:], mv[:, :, 1], EPS, None, ALU.add).then_inc(norm_chain, 1)

                def normed(j):
                    dve.wait_ge(rstd_done, r + 1)
                    nc.vector.tensor_scalar(xrow[:, rp, j, 0:DIM], xrow[:, rp, j, 0:DIM], mv[:, j, 0:1],
                                            rstd[:, j:j + 1], ALU.subtract, ALU.mult).then_inc(x1_done, 1)

                links, placed = [0], [0]

                def link(ins):
                    links[0] += 1
                    ins.then_inc(route, 1)
                    dve.wait_ge(route, LINKS * (i - 2) + links[0])

                def place_link(ins):
                    placed[0] += 1
                    ins.then_inc(place_chain, 1)
                    dve.wait_ge(place_chain, PLACE_LINKS * (i - 2) + placed[0])

                def router_shift():
                    dve.wait_ge(logit_ps_done, i - 1)
                    nc.vector.tensor_copy(logit[:].rearrange("p j e -> p (j e)"),
                                          aux_ps[:, 0:TT * EXPERTS]).then_inc(logit_done, 1)
                    dve.wait_ge(logit_done, i - 1)
                    link(nc.vector.tensor_reduce(mx[:], logit[:], AXX, ALU.max))
                    nc.vector.tensor_tensor(ex[:], logit[:], mx[:].unsqueeze(2).broadcast_to([P, TT, EXPERTS]),
                                            ALU.subtract).then_inc(shifted, 1)

                def router_top():
                    dve.wait_ge(ex_done, i - 1)
                    link(nc.vector.tensor_reduce(mx[:], ex[:], AXX, ALU.add))
                    link(nc.vector.reciprocal(mx[:], mx[:]))
                    link(nc.vector.tensor_tensor(prob[:], ex[:], mx[:].unsqueeze(2).broadcast_to([P, TT, EXPERTS]),
                                                 ALU.mult))
                    hold(dve, held_dve)
                    for j in range(TT):
                        last = nc.vector.max(top[:, j, :], prob[:, j, :])
                    link(last)
                    hold(dve, held_dve)
                    for j in range(TT):
                        last = nc.vector.max_index(idx[:, j, :], top[:, j, :], prob[:, j, :])
                    link(last)
                    link(nc.vector.scalar_tensor_tensor(out=mx[:], in0=top[:, :, 0], scalar=1e-9, in1=top[:, :, 1],
                                                        op0=ALU.add, op1=ALU.add))
                    link(nc.vector.reciprocal(mx[:], mx[:]))
                    link(nc.vector.tensor_tensor(wk[:], top[:, :, 0:TOPK],
                                                 mx[:].unsqueeze(2).broadcast_to([P, TT, TOPK]), ALU.mult))
                    link(nc.vector.tensor_copy(ek[:], idx[:, :, 0:TOPK]))
                    link(nc.vector.tensor_tensor(
                        onehot[:].rearrange("p j k e -> p (j k) e"),
                        t.iota_ef[:].unsqueeze(1).broadcast_to([P, TT * TOPK, EXPERTS]),
                        ek[:].rearrange("p j k -> p (j k)").unsqueeze(2).broadcast_to([P, TT * TOPK, EXPERTS]),
                        ALU.is_equal))
                    nc.vector.tensor_tensor(member[:, 0:TT], onehot[:, :, 0, :], onehot[:, :, 1, :], ALU.add)\
                        .then_inc(member_done, 1)
                    assert links[0] == LINKS, links

                def router_place():
                    dve.wait_ge(rank_ps_done, i - 1)
                    place_link(nc.vector.tensor_tensor(rank[:], out_ps[:, 0, 0:TT * EXPERTS].rearrange("p (j e) -> p j e",
                                                                                                e=EXPERTS),
                                                 t.base[:].unsqueeze(1).broadcast_to([P, TT, EXPERTS]), ALU.add))
                    nc.vector.tensor_tensor(t.base[:], t.base[:], out_ps[:, 0, TT * EXPERTS:(TT + 1) * EXPERTS],
                                            ALU.add).then_inc(rank_read, 1)
                    for k in range(TOPK):
                        place_link(nc.vector.tensor_tensor(rsel[:, :, k, :], onehot[:, :, k, :], rank[:], ALU.mult))
                    place_link(nc.vector.tensor_reduce(rk[:], rsel[:], AXX, ALU.add))
                    place_link(nc.vector.scalar_tensor_tensor(out=rk[:], in0=ek[:], scalar=float(REGION), in1=rk[:],
                                                        op0=ALU.mult, op1=ALU.add))
                    nc.vector.tensor_copy(pos[:, par], rk[:])
                    nc.vector.tensor_copy(xrow[:, par, :, DIM:DIM + 2], wk[:, :, 0:1].broadcast_to([P, TT, 2]))
                    nc.vector.tensor_copy(xrow[:, par, :, DIM + 2], wk[:, :, 1])
                    dve.wait_ge(rank_read, i - 1)
                    place_link(nc.vector.tensor_copy(xrow[:, par, :, DIM + 3], t.token2[:]))
                    nc.vector.tensor_copy(xrow[:, par, :, DIM + 1], ek[:, :, 0])
                    nc.vector.tensor_scalar(t.token2[:], t.token2[:], float(TOPK * T), None, ALU.add)\
                        .then_inc(pos_done, 1)
                    dve.wait_ge(pos_done, i - 1)
                    assert placed[0] == PLACE_LINKS, placed

                for n in range(STATE):
                    if scans:
                        if not POOL_DBX[n]:
                            dbx(n)
                        recurrence(n)
                        if n >= 1 and not POOL_HC[n - 1]:
                            hc(n - 1)
                    if place and n == 2:
                        router_shift()
                    if front:
                        if 4 <= n <= 7:
                            for k in range(TAPS):
                                tap(n - 4, k)
                    if back and (n == 5 or n == 8):
                        for j in range(2) if n == 5 else range(2, TT):
                            residual(j)
                        for j in range(2) if n == 5 else range(2, TT):
                            moments(j)
                    if place and n == 6:
                        router_top()
                    if back:
                        if n == 9:
                            variance()
                        if n == 12:
                            for j in range(TT):
                                normed(j)
                    if place and n == 11:
                        router_place()
                    if front and n == 14:
                        step_sizes()
                if scans and not POOL_HC[STATE - 1]:
                    hc(STATE - 1)

            nc.vector.memset(member[:, TT, :], 0.0)
            steps(dve, step)

        @block.gpsimd
        def _(pool):
            def step(i, half, scans, front, back, place):
                f, r, par, rp = i + 1, i - 1, half, 1 - half

                def dbx(n):
                    if n == 0:
                        pool.wait_ge(u_done, i + 1)
                    wait_row(pool, b_loaded, i, n)
                    pool.wait_ge(carried_in, STATE * i + n + 1)
                    nc.gpsimd.tensor_tensor(scan[:, n % S_RING, :, 1:], u[:, par],
                                            b_row[:, n % BC_RING:n % BC_RING + 1, :].broadcast_to([P, EC, T]), ALU.mult)\
                        .then_inc(dbx_pool, 1)

                def hc(n):
                    wait_row(pool, c_loaded, i, n)
                    pool.wait_ge(scan_done, STATE * i + n + 1)
                    wait_past(pool, sum_done, STATE, *[(a, b + 1) for a, b in [earlier(i, n, P_RING)]][0])
                    nc.gpsimd.tensor_tensor(prod[:, n % P_RING], scan[:, n % S_RING, :, 1:],
                                            c_row[:, n % BC_RING:n % BC_RING + 1, :].broadcast_to([P, EC, T]), ALU.mult)\
                        .then_inc(hc_pool, 1)

                def rstds():
                    pool.wait_ge(norm_chain, 2 * r + 2)
                    nc.gpsimd.tensor_tensor(rstd[:], var[:], t.minus_half[:], ALU.pow).then_inc(rstd_done, 1)

                def send_rows():
                    pool.wait_ge(pos_done, i - 1)
                    hold(pool, held_pool)
                    for j in range(TT):
                        for k in range(TOPK):
                            pool.indirect_dma_start(
                                out=d.rows, out_offset=bass.IndirectOffsetOnAxis(ap=pos[:, par, j, k:k + 1], axis=0),
                                in_=xrow[:, par, j, :], in_offset=None).then_inc(rows_sent[par], 16)

                for n in range(STATE):
                    if scans:
                        if POOL_DBX[n]:
                            dbx(n)
                        if n >= 1 and POOL_HC[n - 1]:
                            hc(n - 1)
                    if back and n == 11:
                        rstds()
                    if place and n == 13:
                        send_rows()
                if scans and POOL_HC[STATE - 1]:
                    hc(STATE - 1)
                if place:
                    pool.wait_ge(rows_sent[par], 8 * TT * TOPK * (i - 2 - par) + 16 * TT * TOPK)
                    pool.sem_inc(rows_free, 1)

            pool.sem_inc(rows_free, 2)
            steps(pool, step)
            for k in range(2):
                pool.wait_ge(rows_sent[k], 16 * TT * TOPK * BLOCKS // 2)


def experts(nc, d, t):
    with ExitStack() as ctx:
        def sb(name, shape, dt=F32):
            return ctx.enter_context(nc.sbuf_tensor(name, shape, dt))

        def ps(name, shape):
            return ctx.enter_context(nc.psum_tensor(name, shape, F32))

        def sem(name):
            return ctx.enter_context(nc.semaphore(name))

        w1 = sb("w1", [P, EXPERTS, KC, FF])
        w2 = sb("w2", [P, EXPERTS, FF // P, DIM])
        b1 = sb("b1", [P, EXPERTS, FF])
        b2 = sb("b2", [P, EXPERTS, DIM])
        FC = FF // P
        MAX_J = TOKENS // P
        thresholds_i = sb("thresholds_i", [P, MAX_J], I32)
        thresholds = sb("thresholds", [P, MAX_J])
        over = sb("over", [P, EXPERTS, MAX_J])
        n_slots = sb("n_slots", [P, EXPERTS])
        ends = sb("ends", [P, EXPERTS])
        slot_i = sb("slot_i", [P, SLOTS], I32)
        slot_f = sb("slot_f", [P, SLOTS])
        passed = sb("passed", [P, SLOTS, EXPERTS])
        slot_e = sb("slot_e", [P, SLOTS])
        slot_start = sb("slot_start", [P, SLOTS])
        slot_valid = sb("slot_valid", [P, SLOTS])
        slot_ei = sb("slot_ei", [P, SLOTS], I32)
        slot_row = sb("slot_row", [P, SLOTS], I32)
        tail_i = sb("tail_i", [P, EXPERTS], I32)
        tail_pos = sb("tail_pos", [P, EXPERTS], U32)
        tail_f = sb("tail_f", [P, EXPERTS])
        tail_row = sb("tail_row", [P, ROW])
        pad_i = sb("pad_i", [P, 1], I32)
        tags = sb("tags", [P, 2, 6])
        dest = sb("dest", [P, 2], U32)
        xg = sb("xg", [P, X_RING, ROW])
        xg_t = sb("xg_t", [P, 2, KC, P])
        h = sb("h", [P, FF])
        h_t = sb("h_t", [P, FC, P])
        y = sb("y", [P, 2, DIM])

        xt_ps = ps("xt_ps", [P, T])
        h_ps = ps("h_ps", [P, 2, T])
        ht_ps = ps("ht_ps", [P, FC, P])
        y_ps2 = ps("y_ps2", [P, 2, T])

        made = sem("tables_iota")
        chain = sem("tables_chain")
        tables_done = sem("tables_done")
        tails_sent = sem("tails_sent")
        w_loaded = [sem(f"w_loaded{e}") for e in range(EXPERTS)]
        w_ready = sem("w_ready")
        x_loaded = [sem(f"x_loaded{k}") for k in range(X_RING)]
        xt_done = sem("xt_done")
        xt_read = sem("xt_read")
        h_ps_done = sem("h_ps_done")
        h_done = sem("h_done")
        ht_ps_done = sem("ht_ps_done")
        ht_done = sem("ht_done")
        y_ps_done = sem("y_ps_done")
        y_biased = sem("y_biased")
        y_done = sem("y_done")
        tag_chain = sem("tag_chain")
        y_sent = [sem(f"y_sent{k}") for k in range(2)]
        y_free = sem("y_free")
        held_sp, held_pool = sem("held_sp2"), sem("held_pool2")
        block = ctx.enter_context(nc.Block())
        HALF = FF // 2

        def wait_x(eng, s, k):
            eng.wait_ge(x_loaded[k], (16 // X_RING) * (s - k) + 16)

        @block.sync
        def _(sp):
            def load_x(s, k):
                if not isinstance(s, int) or s >= X_RING:
                    sp.wait_ge(xt_done, s - (X_RING - 1))
                    sp.wait_ge(tag_chain, 4 * (s - X_RING) + 4)
                    hold(sp, held_sp)
                row = sp.value_load(slot_row[0:1, bass.ds(s, 1)], min_val=0, max_val=EXPERTS * REGION)
                sp.dma_start(xg[:, k], d.rows[bass.ds(row, P), :]).then_inc(x_loaded[k], 16)

            sp.wait_ge(tables_done, 1)
            sp.wait_ge(tails_sent, 16 * (EXPERTS + 1))
            for s in range(X_RING):
                load_x(s, s)
            with sp.Fori(1, SLOTS // X_RING) as q:
                for m in range(X_RING):
                    load_x(X_RING * q + m, m)

        @block.gpsimd
        def _(pool):
            nc.gpsimd.iota(thresholds_i[:], pattern=[[P, MAX_J]], base=0, channel_multiplier=0).then_inc(made, 1)
            nc.gpsimd.iota(slot_i[:], pattern=[[1, SLOTS]], base=0, channel_multiplier=0).then_inc(made, 1)
            nc.gpsimd.iota(tail_i[:], pattern=[[REGION, EXPERTS]], base=0, channel_multiplier=1).then_inc(made, 1)
            nc.gpsimd.iota(pad_i[:], pattern=[[0, 1]], base=TRASH - 1, channel_multiplier=1).then_inc(made, 1)
            pool.wait_ge(tables_done, 1)
            for e in range(EXPERTS):
                pool.indirect_dma_start(out=d.rows, out_offset=bass.IndirectOffsetOnAxis(ap=tail_pos[:, e:e + 1], axis=0),
                                        in_=tail_row[:], in_offset=None).then_inc(tails_sent, 16)
            pool.dma_start(d.rows[EXPERTS * REGION:EXPERTS * REGION + P, :], tail_row[:]).then_inc(tails_sent, 16)

            pool.sem_inc(y_free, 2)

            def send(s, k):
                if not isinstance(s, int) or s >= 2:
                    pool.wait_ge(y_sent[k], 8 * (s - k))
                    pool.sem_inc(y_free, 1)
                pool.wait_ge(y_done, s + 1)
                hold(pool, held_pool)
                pool.indirect_dma_start(out=d.y, out_offset=bass.IndirectOffsetOnAxis(ap=dest[:, k:k + 1], axis=0),
                                        in_=y[:, k, :], in_offset=None).then_inc(y_sent[k], 16)

            send(0, 0)
            send(1, 1)
            with pool.Fori(1, SLOTS // 2) as q:
                send(2 * q, 0)
                send(2 * q + 1, 1)
            for k in range(2):
                pool.wait_ge(y_sent[k], 16 * SLOTS // 2)

        @block.scalar
        def _(act):
            for e in range(EXPERTS):
                act.dma_start(w1[:, e], d.w1[e].rearrange("(k p) f -> p k f", p=P)).then_inc(w_loaded[e], 16)
                act.dma_start(w2[:, e], d.w2[e].rearrange("(g p) n -> p g n", p=P)).then_inc(w_loaded[e], 16)
                act.dma_start(b1[:, e], d.b1[e].partition_broadcast(P)).then_inc(w_loaded[e], 16)
                act.dma_start(b2[:, e], d.b2[e].partition_broadcast(P)).then_inc(w_loaded[e], 16)
            for e in range(EXPERTS):
                act.wait_ge(w_loaded[e], 64)
                act.sem_inc(w_ready, 1)

            def read_xt(s, k):
                act.wait_ge(xt_done, s + 1)
                if not isinstance(s, int) or s >= 2:
                    act.wait_ge(h_ps_done, 2 * (s - 1))
                nc.scalar.copy(xg_t[:, k].rearrange("p k q -> p (k q)"), xt_ps[:, 0:KC * P]).then_inc(xt_read, 1)

            def gelu(s):
                for g in range(2):
                    act.wait_ge(ht_ps_done, 2 * s + g + 1)
                    if g == 0 and (not isinstance(s, int) or s >= 1):
                        act.wait_ge(y_ps_done, s)
                    lo, hi = g * FC // 2, (g + 1) * FC // 2
                    nc.scalar.activation(h_t[:, lo:hi, :], ht_ps[:, lo:hi, :], ACT.Gelu).then_inc(ht_done, 1)

            read_xt(0, 0)
            read_xt(1, 1)
            gelu(0)
            read_xt(2, 0)
            with act.Fori(0, SLOTS // 2 - 2) as q:
                gelu(2 * q + 1)
                read_xt(2 * q + 3, 1)
                gelu(2 * q + 2)
                read_xt(2 * q + 4, 0)
            gelu(SLOTS - 3)
            read_xt(SLOTS - 1, 1)
            gelu(SLOTS - 2)
            gelu(SLOTS - 1)

        @block.tensor
        def _(pe):
            def turn_x(s, k):
                wait_x(pe, s, k)
                if not isinstance(s, int) or s >= 1:
                    pe.wait_ge(xt_read, s)
                for c in range(KC):
                    last = nc.tensor.transpose(xt_ps[:, c * P:(c + 1) * P], xg[:, k, c * P:(c + 1) * P], t.ident[:])
                last.then_inc(xt_done, 1)

            def up(s, k):
                e = pe.value_load(slot_ei[0:1, bass.ds(s, 1)], min_val=0, max_val=EXPERTS - 1)
                pe.wait_ge(w_ready, e + 1)
                pe.wait_ge(xt_read, s + 1)
                for g in range(2):
                    if not isinstance(s, int) or s >= 1:
                        pe.wait_ge(h_done, 2 * s - 1 + g)
                    for c in range(KC):
                        last = nc.tensor.matmul(h_ps[:, g, :], xg_t[:, k % 2, c, :],
                                                w1[:, bass.ds(e, 1), c, g * HALF:(g + 1) * HALF].squeeze(1),
                                                start=(c == 0), stop=(c == KC - 1))
                    last.then_inc(h_ps_done, 1)

            def turn_h(s):
                for g in range(2):
                    pe.wait_ge(h_done, 2 * s + g + 1)
                    if not isinstance(s, int) or s >= 1:
                        pe.wait_ge(ht_done, 2 * s - 1 + g)
                    for j in range(g * FC // 2, (g + 1) * FC // 2):
                        last = nc.tensor.transpose(ht_ps[:, j, :], h[:, j * P:(j + 1) * P], t.ident[:])
                    last.then_inc(ht_ps_done, 1)

            def down(s, k):
                e = pe.value_load(slot_ei[0:1, bass.ds(s, 1)], min_val=0, max_val=EXPERTS - 1)
                pe.wait_ge(y_biased, s)
                for j in range(FC):
                    if j % (FC // 2) == 0:
                        pe.wait_ge(ht_done, 2 * s + 1 + j // (FC // 2))
                    last = nc.tensor.matmul(y_ps2[:, k % 2, 0:DIM], h_t[:, j, :],
                                            w2[:, bass.ds(e, 1), j, :].squeeze(1),
                                            start=(j == 0), stop=(j == FC - 1))
                last.then_inc(y_ps_done, 1)

            def slot(s, k, turn=True, first=True):
                turn_h(s)
                if turn:
                    turn_x(s + 2, (k + 2) % X_RING)
                if first:
                    up(s + 1, (k + 1) % X_RING)
                down(s, k)

            pe.wait_ge(tables_done, 1)
            turn_x(0, 0)
            turn_x(1, 1)
            up(0, 0)
            slot(0, 0)
            slot(1, 1)
            with pe.Fori(0, (SLOTS - 4) // X_RING) as q:
                for m in range(X_RING):
                    slot(X_RING * q + (2 + m), (2 + m) % X_RING)
            slot(SLOTS - 2, 2, turn=False)
            slot(SLOTS - 1, 3, turn=False, first=False)

        @block.vector
        def _(dve):
            links = [0]

            def link(ins):
                links[0] += 1
                ins.then_inc(chain, 1)
                dve.wait_ge(chain, links[0])

            dve.wait_ge(made, 4)
            link(nc.vector.tensor_copy(thresholds[:], thresholds_i[:]))
            link(nc.vector.tensor_copy(slot_f[:], slot_i[:]))
            link(nc.vector.tensor_copy(tail_f[:], tail_i[:]))
            link(nc.vector.memset(tail_row[:], 0.0))
            link(nc.vector.memset(tail_row[:, DIM + 1:DIM + 2], -1.0))
            link(nc.vector.tensor_copy(tail_row[:, DIM + 3:DIM + 4], pad_i[:]))
            link(nc.vector.tensor_tensor(tail_f[:], tail_f[:], t.base[:], ALU.add))
            link(nc.vector.tensor_copy(tail_pos[:], tail_f[:]))
            link(nc.vector.tensor_tensor(over[:], t.base[:].unsqueeze(2).broadcast_to([P, EXPERTS, MAX_J]),
                                         thresholds[:].unsqueeze(1).broadcast_to([P, EXPERTS, MAX_J]), ALU.is_gt))
            link(nc.vector.tensor_reduce(n_slots[:], over[:], AXX, ALU.add))
            link(nc.vector.tensor_tensor_scan(ends[:], t.ones[:, 0:EXPERTS], n_slots[:], 0.0, ALU.mult, ALU.add))
            link(nc.vector.tensor_tensor(passed[:], slot_f[:].unsqueeze(2).broadcast_to([P, SLOTS, EXPERTS]),
                                         ends[:].unsqueeze(1).broadcast_to([P, SLOTS, EXPERTS]), ALU.is_ge))
            link(nc.vector.tensor_reduce(slot_e[:], passed[:], AXX, ALU.add))
            link(nc.vector.tensor_tensor(passed[:], passed[:],
                                         n_slots[:].unsqueeze(1).broadcast_to([P, SLOTS, EXPERTS]), ALU.mult))
            link(nc.vector.tensor_reduce(slot_start[:], passed[:], AXX, ALU.add))
            link(nc.vector.tensor_scalar(slot_valid[:], slot_e[:], float(EXPERTS), None, ALU.is_lt))
            link(nc.vector.tensor_tensor(slot_start[:], slot_f[:], slot_start[:], ALU.subtract))
            link(nc.vector.tensor_scalar(slot_start[:], slot_start[:], float(P), None, ALU.mult))
            link(nc.vector.scalar_tensor_tensor(out=slot_start[:], in0=slot_e[:], scalar=float(REGION),
                                                in1=slot_start[:], op0=ALU.mult, op1=ALU.add))
            link(nc.vector.tensor_tensor(slot_start[:], slot_start[:], slot_valid[:], ALU.mult))
            link(nc.vector.tensor_tensor(slot_e[:], slot_e[:], slot_valid[:], ALU.mult))
            link(nc.vector.tensor_scalar(slot_valid[:], slot_valid[:], -float(EXPERTS * REGION),
                                         float(EXPERTS * REGION), ALU.mult, ALU.add))
            link(nc.vector.tensor_tensor(slot_start[:], slot_start[:], slot_valid[:], ALU.add))
            link(nc.vector.tensor_scalar(slot_f[:], slot_f[:], float(P), None, ALU.mult))
            link(nc.vector.tensor_copy(slot_ei[:], slot_e[:]))
            link(nc.vector.tensor_copy(slot_row[:], slot_start[:]))
            nc.vector.memset(dest[:], 0).then_inc(tables_done, 1)
            dve.wait_ge(tables_done, 1)

            def tag(s, x):
                k = x % 2
                wait_x(dve, s, x)
                dve.wait_ge(y_free, s + 1)
                e0 = xg[:, x, DIM + 1:DIM + 2]
                nc.vector.tensor_tensor(tags[:, k, 0:1], e0, slot_e[:, bass.ds(s, 1)], ALU.is_equal)
                nc.vector.tensor_tensor(tags[:, k, 1:2], e0, slot_e[:, bass.ds(s, 1)], ALU.not_equal)
                nc.vector.tensor_scalar(tags[:, k, 4:5], e0, 0.0, slot_f[:, bass.ds(s, 1)], ALU.is_lt, ALU.mult)\
                    .then_inc(tag_chain, 1)
                dve.wait_ge(tag_chain, 4 * s + 1)
                nc.vector.tensor_tensor(tags[:, k, 2:3], xg[:, x, DIM:DIM + 1], tags[:, k, 0:1], ALU.mult)
                nc.vector.tensor_tensor(tags[:, k, 5:6], xg[:, x, DIM + 3:DIM + 4], tags[:, k, 1:2], ALU.add)\
                    .then_inc(tag_chain, 1)
                dve.wait_ge(tag_chain, 4 * s + 2)
                nc.vector.tensor_tensor(dest[:, k:k + 1], tags[:, k, 5:6], tags[:, k, 4:5], ALU.add)\
                    .then_inc(tag_chain, 1)
                nc.vector.scalar_tensor_tensor(out=tags[:, k, 3:4], in0=xg[:, x, DIM + 2:DIM + 3],
                                               scalar=tags[:, k, 1:2], in1=tags[:, k, 2:3], op0=ALU.mult,
                                               op1=ALU.add).then_inc(tag_chain, 1)

            def bias_h(s):
                e = dve.value_load(slot_ei[0:1, bass.ds(s, 1)], min_val=0, max_val=EXPERTS - 1)
                for g in range(2):
                    dve.wait_ge(h_ps_done, 2 * s + g + 1)
                    if not isinstance(s, int) or s >= 1:
                        dve.wait_ge(ht_ps_done, 2 * s - 1 + g)
                    nc.vector.tensor_tensor(h[:, g * HALF:(g + 1) * HALF], h_ps[:, g, :],
                                            b1[:, bass.ds(e, 1), g * HALF:(g + 1) * HALF].squeeze(1),
                                            ALU.add).then_inc(h_done, 1)

            def bias_y(s, k):
                e = dve.value_load(slot_ei[0:1, bass.ds(s, 1)], min_val=0, max_val=EXPERTS - 1)
                dve.wait_ge(y_ps_done, s + 1)
                nc.vector.tensor_tensor(y[:, k, :], y_ps2[:, k, 0:DIM], b2[:, bass.ds(e, 1), :].squeeze(1),
                                        ALU.add).then_inc(y_biased, 1)
                dve.wait_ge(y_biased, s + 2)
                dve.wait_ge(tag_chain, 4 * s + 4)
                nc.vector.tensor_scalar(y[:, k, :], y[:, k, :], tags[:, k, 3:4], None, ALU.mult)\
                    .then_inc(y_done, 1)

            dve.sem_inc(y_biased, 1)
            bias_h(0)

            def slot(s, k, first=True):
                tag(s, k)
                if first:
                    bias_h(s + 1)
                bias_y(s, k % 2)

            slot(0, 0)
            slot(1, 1)
            with dve.Fori(0, (SLOTS - 4) // X_RING) as q:
                for m in range(X_RING):
                    slot(X_RING * q + (2 + m), (2 + m) % X_RING)
            slot(SLOTS - 2, 2)
            slot(SLOTS - 1, 3, first=False)


def combine(nc, d, t):
    with ExitStack() as ctx:
        G = 2
        N = TOKENS // P // G
        B = 3
        x1 = ctx.enter_context(nc.sbuf_tensor("c_x1", [P, B, G, DIM], F32))
        ye = ctx.enter_context(nc.sbuf_tensor("c_y", [P, B, G, TOPK, DIM], F32))
        o = ctx.enter_context(nc.sbuf_tensor("c_o", [P, B, G, DIM], F32))
        stats = ctx.enter_context(nc.sbuf_tensor("c_stats", [P, G, 6], F32))
        mv = ctx.enter_context(nc.sbuf_tensor("c_mv", [P, B, G, 2], F32))
        var = ctx.enter_context(nc.sbuf_tensor("c_var", [P, B, G], F32))
        rstd = ctx.enter_context(nc.sbuf_tensor("c_rstd", [P, B, G], F32))
        sem = lambda name: ctx.enter_context(nc.semaphore(name))
        loaded = [sem(f"c_loaded{k}") for k in range(B)]
        stored = [sem(f"c_stored{k}") for k in range(B)]
        chain = sem("c_chain")
        rstd_done = sem("c_rstd_done")
        o_done = sem("c_o_done")
        block = ctx.enter_context(nc.Block())
        y_v = d.y[0:TRASH, :].rearrange("(i p k) n -> p i k n", p=P, k=TOPK)
        o_v = d.out.rearrange("(i p) n -> p i n", p=P)

        @block.sync
        def _(sp):
            for m in range(N):
                if m >= B:
                    sp.wait_ge(o_done, m - B + 1)
                sp.dma_start(ye[:, m % B], y_v[:, G * m:G * m + G]).then_inc(loaded[m % B], 16)
                b, j = divmod(G * m, TT)
                sp.dma_start(x1[:, m % B], d.x1[b, :, j:j + G, :]).then_inc(loaded[m % B], 16)

        @block.scalar
        def _(act):
            for m in range(N):
                act.wait_ge(o_done, m + 1)
                act.dma_start(o_v[:, G * m:G * m + G, :], o[:, m % B]).then_inc(stored[m % B], 16)
            for k in range(B):
                act.wait_ge(stored[k], 16 * len(range(k, N, B)))

        @block.gpsimd
        def _(pool):
            for m in range(N):
                pool.wait_ge(chain, 5 * m + 5)
                nc.gpsimd.tensor_tensor(rstd[:, m % B], var[:, m % B], t.minus_half[:, 0:G], ALU.pow)\
                    .then_inc(rstd_done, 1)

        @block.vector
        def _(dve):
            def finish(m):
                b = m % B
                dve.wait_ge(rstd_done, m + 1)
                for g in range(G):
                    last = nc.vector.tensor_scalar(o[:, b, g, :], o[:, b, g, :], mv[:, b, g, 0:1],
                                                   rstd[:, b, g:g + 1], ALU.subtract, ALU.mult)
                last.then_inc(o_done, 1)

            for m in range(N):
                b = m % B
                links = [5 * m]

                def link(ins):
                    links[0] += 1
                    ins.then_inc(chain, 1)
                    dve.wait_ge(chain, links[0])

                dve.wait_ge(loaded[b], 32 * (m // B + 1))
                if m >= B:
                    dve.wait_ge(stored[b], 16 * (m // B))
                link(nc.vector.tensor_tensor(o[:, b], ye[:, b, :, 0, :], ye[:, b, :, 1, :], ALU.add))
                link(nc.vector.tensor_tensor(o[:, b], o[:, b], x1[:, b], ALU.add))
                for g in range(G):
                    last = nc.vector.bn_stats(stats[:, g, :], o[:, b, g, :])
                link(last)
                for g in range(G):
                    last = nc.vector.bn_aggr(mv[:, b, g, :], stats[:, g, :])
                link(last)
                nc.vector.tensor_scalar(var[:, b], mv[:, b, :, 1], EPS, None, ALU.add).then_inc(chain, 1)
                if m >= 1:
                    finish(m - 1)
            finish(N - 1)


class Names:
    pass


def build(nc, d):
    d.bc = nc.dram_tensor("bc_rows", [BLOCKS, 2 * STATE, T], F32, kind="Internal").ap()
    d.x1 = nc.dram_tensor("x1_rows", [BLOCKS, P, TT, DIM], F32, kind="Internal").ap()
    d.rows = nc.dram_tensor("expert_rows", [EXPERTS * REGION + P, ROW], F32, kind="Internal").ap()
    d.y = nc.dram_tensor("expert_out", [TRASH + SLOTS * P, DIM], F32, kind="Internal").ap()
    t = Names()
    with ExitStack() as ctx:
        def sb(name, shape, dt=F32):
            return ctx.enter_context(nc.sbuf_tensor(name, shape, dt))

        t.ident = sb("ident", [P, P])
        t.before = sb("before", [P, P])
        t.ones = sb("ones", [P, P])
        t.minus_half = sb("minus_half", [P, TT])
        t.iota_e = sb("iota_e", [P, EXPERTS], I32)
        t.iota_ef = sb("iota_ef", [P, EXPERTS])
        t.iota_t = sb("iota_t", [P, TT], I32)
        t.token2 = sb("token2", [P, TT])
        t.base = sb("base", [P, EXPERTS])
        with ExitStack() as phase:
            def sb(name, shape, dt=F32):
                return phase.enter_context(nc.sbuf_tensor(name, shape, dt))

            t.w_in = sb("w_in", [P, KC, 2 * INNER])
            t.conv_w = sb("conv_w", [P, EC, TAPS])
            t.conv_b = sb("conv_b", [P, EC])
            t.w_x = sb("w_x", [P, EC, 2 * STATE])
            t.w_dt = sb("w_dt", [P, EC])
            t.w_xdt = sb("w_xdt", [P, EC, P])
            t.dt_col = sb("dt_col", [P, EC])
            t.b_dt = sb("b_dt", [P, EC])
            t.neg_a = sb("neg_a", [P, STATE])
            t.d_col = sb("d_col", [P, EC])
            t.diag_d = sb("diag_d", [P, EC, P])
            t.w_out = sb("w_out", [P, EC, DIM])
            t.router = sb("router", [P, KC, EXPERTS])
            t.zeros = sb("zeros", [P, EC, TAPS])
            t.xp = sb("xp", [P, EC, T + TAPS - 1])
            t.decay = sb("decay", [P, DA_RING, EC, T + 1])
            setup(nc, d, t)
            mamba(nc, d, t)
        experts(nc, d, t)
        combine(nc, d, t)


def kernel(L0_attn_x, L0_attn_W_in, L0_attn_conv_w, L0_attn_conv_b, L0_attn_W_x, L0_attn_W_dt, L0_attn_b_dt,
           L0_attn_A_log, L0_attn_D, L0_attn_W_out, L0_ffn_router_w, L0_ffn_expert_w1, L0_ffn_expert_b1,
           L0_ffn_expert_w2, L0_ffn_expert_b2):
    import concourse.bacc as bacc
    from concourse.bass_utils import run_bass_kernel_spmd

    def lay(a):
        return np.ascontiguousarray(a)

    def columns(a):
        return lay(a.reshape(EC, P, -1).transpose(1, 0, 2))

    x = np.asarray(L0_attn_x)
    w_x = np.asarray(L0_attn_W_x)
    arrays = {
        "x_t": lay(x.reshape(BLOCKS, T, KC, P).transpose(0, 3, 2, 1)),
        "x_tok": lay(x.reshape(BLOCKS, TT, P, DIM).transpose(0, 2, 1, 3)),
        "w_in": lay(np.asarray(L0_attn_W_in).T),
        "conv_w": columns(np.asarray(L0_attn_conv_w)),
        "conv_b": columns(np.asarray(L0_attn_conv_b))[:, :, 0],
        "w_x": lay(w_x[:2 * STATE].T),
        "dt_col": columns(w_x[2 * STATE])[:, :, 0],
        "w_dt": columns(np.asarray(L0_attn_W_dt))[:, :, 0],
        "b_dt": columns(np.asarray(L0_attn_b_dt))[:, :, 0],
        "a_log": lay(np.asarray(L0_attn_A_log)),
        "d_skip": columns(np.asarray(L0_attn_D))[:, :, 0],
        "w_out": lay(np.asarray(L0_attn_W_out).T),
        "router": lay(np.asarray(L0_ffn_router_w).T),
        "w1": lay(np.asarray(L0_ffn_expert_w1).transpose(0, 2, 1)),
        "b1": lay(np.asarray(L0_ffn_expert_b1)),
        "w2": lay(np.asarray(L0_ffn_expert_w2).transpose(0, 2, 1)),
        "b2": lay(np.asarray(L0_ffn_expert_b2)),
    }
    arrays = {f"in_{n}": lay(a) for n, a in arrays.items()}
    nc = bacc.Bacc("TRN2", target_bir_lowering=False, num_devices=1)
    d = Names()
    d.x_t = nc.dram_tensor("in_x_t", arrays["in_x_t"].shape, F32, kind="ExternalInput").ap()
    d.x_tok = nc.dram_tensor("in_x_tok", arrays["in_x_tok"].shape, F32, kind="ExternalInput").ap()
    d.w_in = nc.dram_tensor("in_w_in", arrays["in_w_in"].shape, F32, kind="ExternalInput").ap()
    d.conv_w = nc.dram_tensor("in_conv_w", arrays["in_conv_w"].shape, F32, kind="ExternalInput").ap()
    d.conv_b = nc.dram_tensor("in_conv_b", arrays["in_conv_b"].shape, F32, kind="ExternalInput").ap()
    d.w_x = nc.dram_tensor("in_w_x", arrays["in_w_x"].shape, F32, kind="ExternalInput").ap()
    d.w_dt = nc.dram_tensor("in_w_dt", arrays["in_w_dt"].shape, F32, kind="ExternalInput").ap()
    d.dt_col = nc.dram_tensor("in_dt_col", arrays["in_dt_col"].shape, F32, kind="ExternalInput").ap()
    d.b_dt = nc.dram_tensor("in_b_dt", arrays["in_b_dt"].shape, F32, kind="ExternalInput").ap()
    d.a_log = nc.dram_tensor("in_a_log", arrays["in_a_log"].shape, F32, kind="ExternalInput").ap()
    d.d_skip = nc.dram_tensor("in_d_skip", arrays["in_d_skip"].shape, F32, kind="ExternalInput").ap()
    d.w_out = nc.dram_tensor("in_w_out", arrays["in_w_out"].shape, F32, kind="ExternalInput").ap()
    d.router = nc.dram_tensor("in_router", arrays["in_router"].shape, F32, kind="ExternalInput").ap()
    d.w1 = nc.dram_tensor("in_w1", arrays["in_w1"].shape, F32, kind="ExternalInput").ap()
    d.b1 = nc.dram_tensor("in_b1", arrays["in_b1"].shape, F32, kind="ExternalInput").ap()
    d.w2 = nc.dram_tensor("in_w2", arrays["in_w2"].shape, F32, kind="ExternalInput").ap()
    d.b2 = nc.dram_tensor("in_b2", arrays["in_b2"].shape, F32, kind="ExternalInput").ap()
    d.out = nc.dram_tensor("out_0", (TOKENS, DIM), F32, kind="ExternalOutput").ap()
    build(nc, d)
    got = run_bass_kernel_spmd(nc, [arrays], core_ids=[0])
    return got.results[0]["out_0"].reshape(SEQS, SEQ, DIM)
```

```python
from contextlib import ExitStack

import numpy as np
import concourse.bass as bass
from concourse import mybir

ALU = mybir.AluOpType
ACT = mybir.ActivationFunctionType
AXX = mybir.AxisListType.X
F32 = mybir.dt.float32
I32 = mybir.dt.int32
U32 = mybir.dt.uint32
F32R = mybir.dt.float32r

P = 128
SEQS, SEQ, DIM = 4, 1024, 256
INNER, STATE, TAPS = 512, 16, 4
FF, EXPERTS, TOPK = 1024, 8, 2
TOKENS = SEQS * SEQ

T = 512
BLOCKS = TOKENS // T
HALVES = SEQ // T
KC = DIM // P
EC = INNER // P
TT = T // P
ROW = DIM + 4
REGION = TOKENS + P
SLOTS = TOKENS * TOPK // P + EXPERTS - 1
TRASH = TOKENS * TOPK
EPS = 1e-5

S_RING = 4
P_RING = 3
B_RING = 3
C_RING = 2
C_LAG = 2
DA_RING = 3
PIECES, PW = 16, 256
W_LOADS = 4
W_RING = 3
Y_RING = 4
X_RING = 4
POOL_DBX = [0] + [1] * (STATE - 1)
POOL_HC = [0] * STATE


def hold(eng, held):
    eng.sem_inc(held, 1)


def setup(nc, d, t):
    with ExitStack() as ctx:
        loaded = ctx.enter_context(nc.semaphore("setup_loaded"))
        pool_done = ctx.enter_context(nc.semaphore("setup_pool"))
        exp_done = ctx.enter_context(nc.semaphore("setup_exp"))
        dve_done = ctx.enter_context(nc.semaphore("setup_dve"))
        block = ctx.enter_context(nc.Block())
        loads = [(t.w_in, d.w_in.rearrange("(k p) n -> p k n", p=P)),
                 (t.conv_w, d.conv_w), (t.conv_b, d.conv_b),
                 (t.w_x, d.w_x.rearrange("(c p) n -> p c n", p=P)),
                 (t.w_dt, d.w_dt), (t.dt_col, d.dt_col), (t.b_dt, d.b_dt),
                 (t.neg_a, d.a_log.partition_broadcast(P)),
                 (t.d_col, d.d_skip),
                 (t.w_out, d.w_out.rearrange("(c p) n -> p c n", p=P)),
                 (t.router, d.router.rearrange("(k p) n -> p k n", p=P))]

        @block.sync
        def _(sp):
            for dst, src in loads:
                sp.dma_start(dst[:], src).then_inc(loaded, 16)

        @block.gpsimd
        def _(pool):
            nc.gpsimd.memset(t.ident[:], 0.0).then_inc(pool_done, 1)
            nc.gpsimd.memset(t.before[:], 1.0).then_inc(pool_done, 1)
            nc.gpsimd.memset(t.ones[:], 1.0).then_inc(pool_done, 1)
            nc.gpsimd.memset(t.minus_half[:], -0.5).then_inc(pool_done, 1)
            nc.gpsimd.iota(t.iota_e[:], pattern=[[1, EXPERTS]], base=0, channel_multiplier=0).then_inc(pool_done, 1)
            nc.gpsimd.iota(t.iota_t[:], pattern=[[2 * P, TT]], base=0, channel_multiplier=2).then_inc(pool_done, 1)
            pool.wait_ge(pool_done, 6)
            nc.gpsimd.affine_select(out=t.ident[:], in_=t.ident[:], compare_op=ALU.not_equal, fill=1.0, base=0,
                                    pattern=[[-1, P]], channel_multiplier=1).then_inc(pool_done, 1)
            nc.gpsimd.affine_select(out=t.before[:], in_=t.before[:], compare_op=ALU.is_gt, fill=0.0, base=0,
                                    pattern=[[1, P]], channel_multiplier=-1).then_inc(pool_done, 1)

        @block.scalar
        def _(act):
            act.wait_ge(loaded, 16 * len(loads))
            nc.scalar.activation(t.neg_a[:], t.neg_a[:], ACT.Exp).then_inc(exp_done, 1)

        @block.vector
        def _(dve):
            nc.vector.memset(t.zeros[:], 0.0)
            nc.vector.memset(t.base[:], 0.0)
            dve.wait_ge(pool_done, 8)
            nc.vector.tensor_copy(t.iota_ef[:], t.iota_e[:])
            nc.vector.tensor_copy(t.token2[:], t.iota_t[:])
            dve.wait_ge(exp_done, 1)
            nc.vector.tensor_scalar(t.neg_a[:], t.neg_a[:], -1.0, None, ALU.mult)
            for c in range(EC):
                nc.vector.tensor_scalar(t.diag_d[:, c, :], t.ident[:], t.d_col[:, c:c + 1], None, ALU.mult)
                nc.vector.tensor_scalar(t.w_xdt[:, c, :], t.ones[:], t.dt_col[:, c:c + 1], None, ALU.mult)
            nc.vector.memset(t.xp[:, :, T:T + TAPS - 1], 0.0).then_inc(dve_done, 1)
            dve.wait_ge(dve_done, 1)


def mamba(nc, d, t):
    with ExitStack() as ctx:
        def sb(name, shape, dt=F32):
            return ctx.enter_context(nc.sbuf_tensor(name, shape, dt))

        def ps(name, shape):
            return ctx.enter_context(nc.psum_tensor(name, shape, F32))

        def sem(name):
            return ctx.enter_context(nc.semaphore(name))

        x_t = sb("x_t", [P, 2, KC, T])
        x_tok = sb("x_tok", [P, TT, DIM])
        xc = sb("xc", [P, 2, EC, T])
        dt = sb("dt", [P, 2, EC, T])
        u = sb("u", [P, 2, EC, T])
        ssm = sb("ssm", [2 * STATE, T])
        cut = [0]

        def view(*shape):
            size = int(np.prod(shape))
            at, cut[0] = cut[0], cut[0] + size
            assert cut[0] <= t.arena.shape[1]
            names = "abcd"[:len(shape)]
            return t.arena[:, at:at + size].rearrange(
                f"p ({' '.join(names)}) -> p {' '.join(names)}", **dict(zip(names, shape)))

        scan = view(S_RING, EC, T + 1)
        assert cut[0] >= PIECES * 2 * PW
        prod = view(P_RING, EC, T)
        decay = view(DA_RING, EC, T + 1)
        raw = view(2, PW)
        parts = view(2, 2, PW)
        b_row = view(B_RING, T)
        c_row = view(C_RING, T)
        carry = sb("carry", [P, STATE, EC])
        ys = sb("ys", [P, EC, T])
        xrow = sb("xrow", [P, 2, TT, ROW])
        x1_t = sb("x1_t", [P, TT, KC, P])
        stats = sb("stats", [P, TT, 6])
        mv = sb("mv", [P, TT, 2])
        var = sb("var", [P, 2 * TT])
        rstd = sb("rstd", [P, TT])
        shift = sb("shift", [P, TT])
        logit = sb("logit", [P, TT, EXPERTS])
        ex = sb("ex", [P, TT, EXPERTS])
        mx = sb("mx", [P, TT])
        top = sb("top", [P, TT, 8])
        idx = sb("idx", [P, TT, 8], U32)
        wk = sb("wk", [P, TT, TOPK])
        ek = sb("ek", [P, TT, TOPK])
        onehot = sb("onehot", [P, TT, TOPK, EXPERTS])
        member = sb("member", [P, TT + 1, EXPERTS])
        rank = sb("rank", [P, TT, EXPERTS])
        rk = sb("rk", [P, TT, TOPK])
        pos = sb("pos", [P, 2, TT, TOPK], U32)

        MAX_J = TOKENS // P
        cut[0] = S_RING * EC * (T + 1)
        thresholds_i = view(MAX_J).bitcast(I32)
        slot_i = view(SLOTS).bitcast(I32)
        tail_i = view(EXPERTS).bitcast(I32)
        pad_i = view(1).bitcast(I32)
        thresholds = view(MAX_J)
        over = view(EXPERTS, MAX_J)
        n_slots = view(EXPERTS)
        ends = view(EXPERTS)
        passed = view(SLOTS, EXPERTS)
        slot_start = view(SLOTS)
        slot_valid = view(SLOTS)
        tail_f = view(EXPERTS)
        tail_row = view(ROW)
        assert cut[0] <= (S_RING + P_RING) * EC * T

        y_ps = ps("y_ps", [P, EC, T])
        in_ps = ps("in_ps", [P, 2, T])
        aux_ps = ps("aux_ps", [P, T])
        out_ps = ps("out_ps", [P, 2, DIM])

        xt_loaded = [sem(f"xt_loaded{k}") for k in range(2)]
        xtok_loaded = sem("xtok_loaded")
        inproj_done = sem("inproj_done")
        halo_done = sem("halo_done")
        xp_done = sem("xp_done")
        tap_done = sem("tap_done")
        silu_done = sem("silu_done")
        ssm_ps_done = sem("ssm_ps_done")
        ssm_done = sem("ssm_done")
        bc_stored = sem("bc_stored")
        b_loaded = [sem(f"b_loaded{k}") for k in range(B_RING)]
        c_loaded = [sem(f"c_loaded{k}") for k in range(C_RING)]
        z_done = sem("z_done")
        z_read = sem("z_read")
        ln_done = sem("ln_done")
        dt_done = sem("dt_done")
        u_done = sem("u_done")
        carried_in = sem("carried_in")
        carried_out = sem("carried_out")
        decay_done = sem("decay_done")
        dbx_pool, dbx_dve = sem("dbx_pool"), sem("dbx_dve")
        hc_pool, hc_dve = sem("hc_pool"), sem("hc_dve")
        scan_done = sem("scan_done")
        sum_done = sem("sum_done")
        ys_done = sem("ys_done")
        outproj_done = sem("outproj_done")
        pre_done = sem("pre_done")
        stats_done = sem("stats_done")
        norm_chain = sem("norm_chain")
        rstd_done = sem("rstd_done")
        x1_done = sem("x1_done")
        x1_stored = [sem(f"x1_stored{k}") for k in range(2)]
        turned = sem("turned")
        turned_read = sem("turned_read")
        logit_ps_done = sem("logit_ps_done")
        logit_done = sem("logit_done")
        route = sem("route")
        shifted = sem("shifted")
        place_chain = sem("place_chain")
        ex_done = sem("ex_done")
        member_done = sem("member_done")
        rank_ps_done = sem("rank_ps_done")
        rank_read = sem("rank_read")
        pos_done = sem("pos_done")
        early_sent = [sem(f"early_sent{k}") for k in range(2)]
        late_sent = [sem(f"late_sent{k}") for k in range(2)]
        early_free = sem("early_free")
        late_free = sem("late_free")
        cut_done = sem("cut_done")
        made = sem("made")
        chain = sem("chain")
        tails_known = sem("tails_known")
        tails_stored = sem("tails_stored")
        first_loaded = sem("first_loaded")
        raw_loaded = [sem(f"raw_loaded{k}") for k in range(2)]
        high_done = sem("high_done")
        low_done = sem("low_done")
        parts_stored = [sem(f"parts_stored{k}") for k in range(2)]
        held_sp, held_act, held_dve, held_pool = sem("held_sp"), sem("held_act"), sem("held_dve"), sem("held_pool")
        block = ctx.enter_context(nc.Block())

        n_pd, n_ph = sum(POOL_DBX), sum(POOL_HC)

        def earlier(i, n, k):
            return (i, n - k) if n >= k else (i - 1, n - k + STATE)

        def slot_before(i, n, ring):
            return (i, n - ring) if n >= ring else (i - 1, max(m for m in range(STATE) if m % ring == n))

        def known_past(i):
            return not isinstance(i, int) or i >= 0

        def wait_dbx(eng, i, n):
            if not known_past(i):
                return
            if POOL_DBX[n]:
                eng.wait_ge(dbx_pool, n_pd * i + sum(POOL_DBX[:n + 1]))
            else:
                eng.wait_ge(dbx_dve, (STATE - n_pd) * i + n + 1 - sum(POOL_DBX[:n + 1]))

        def wait_hc(eng, i, n):
            if not known_past(i):
                return
            if POOL_HC[n]:
                eng.wait_ge(hc_pool, n_ph * i + sum(POOL_HC[:n + 1]))
            else:
                eng.wait_ge(hc_dve, (STATE - n_ph) * i + n + 1 - sum(POOL_HC[:n + 1]))

        def wait_past(eng, s, per, i, n):
            if known_past(i):
                eng.wait_ge(s, per * i + n)

        def wait_row(eng, loaded, i, n):
            ring = len(loaded)
            a_block = len(range(n % ring, STATE, ring))
            eng.wait_ge(loaded[n % ring], 16 * a_block * i + 16 * (n // ring + 1))

        def steps(eng, step):
            step(-1, 1, False, True, False, False)
            step(0, 0, True, True, False, False)
            step(1, 1, True, True, True, False)
            step(2, 0, True, True, True, True)
            with nc.Fori(0, SEQS - 2, engines=(eng.engine,), hint_back_edge=True) as q:
                i = 2 * q + 3
                step(i, 1, True, True, True, True)
                step(i + 1, 0, True, True, True, True)
            step(BLOCKS - 1, 1, True, False, True, True)
            step(BLOCKS, 0, False, False, True, True)
            step(BLOCKS + 1, 1, False, False, False, True)

        def store_tails(eng, experts):
            eng.wait_ge(tails_known, 1)
            for e in experts:
                row = eng.value_load(t.tail_at[0:1, e:e + 1], min_val=0, max_val=EXPERTS * REGION)
                eng.dma_start(d.rows[bass.ds(row, P), :], tail_row[:]).then_inc(tails_stored, 16)

        @block.sync
        def _(sp):
            def step(i, half, scans, front, back, place):
                f, r, fp, rp = i + 1, i - 1, 1 - half, 1 - half
                if front:
                    wait_past(sp, sum_done, STATE, f - 2, KC * EC + 2)
                    hold(sp, held_sp)
                    sp.dma_start(x_t[:, fp], d.x_t[f]).then_inc(xt_loaded[fp], 16)
                if back:
                    wait_past(sp, pre_done, TT, r - 1, TT)
                    hold(sp, held_sp)
                    sp.dma_start(x_tok[:], d.x_tok[r]).then_inc(xtok_loaded, 16)
                def load_b(n):
                    if n == 0:
                        sp.wait_ge(bc_stored, 16 * i + 16)
                        hold(sp, held_sp)
                    wait_dbx(sp, *slot_before(i, n, B_RING))
                    hold(sp, held_sp)
                    sp.dma_start(b_row[:, n % B_RING], d.bc[i, n, :].partition_broadcast(P))\
                        .then_inc(b_loaded[n % B_RING], 16)

                def load_c(i, n):
                    wait_hc(sp, *earlier(i, n, C_RING))
                    hold(sp, held_sp)
                    sp.dma_start(c_row[:, n % C_RING], d.bc[i, STATE + n, :].partition_broadcast(P))\
                        .then_inc(c_loaded[n % C_RING], 16)

                for n in range(STATE):
                    if back and n < C_LAG:
                        load_c(i - 1, n - C_LAG + STATE)
                    if scans:
                        if n >= C_LAG:
                            load_c(i, n - C_LAG)
                        load_b(n)

            steps(sp, step)
            sp.wait_ge(sum_done, STATE * BLOCKS)
            for k in range(2):
                sp.wait_ge(parts_stored[k], 16 * PIECES // 2)
            for m in range(W_LOADS):
                lo, hi = m * PIECES // W_LOADS, (m + 1) * PIECES // W_LOADS
                sp.dma_start(t.w[:, 0, lo:hi].rearrange("p q h n -> p q (h n)"),
                             d.parts[0, lo:hi].rearrange("q p h n -> p q (h n)")).then_inc(first_loaded, 16)
            store_tails(sp, range(0, EXPERTS // 2))
            sp.dma_start(d.rows[EXPERTS * REGION:EXPERTS * REGION + P, :], tail_row[:]).then_inc(tails_stored, 16)
            sp.wait_ge(first_loaded, 16 * W_LOADS)
            sp.wait_ge(tails_stored, 16 * (EXPERTS + 1))

        @block.tensor
        def _(pe):
            def step(i, half, scans, front, back, place):
                f, r, fp, par = i + 1, i - 1, 1 - half, half

                def in_projection(c):
                    if c == 0:
                        pe.wait_ge(xt_loaded[fp], 16 * ((f - fp) // 2 + 1) if isinstance(f, int)
                                   else 8 * (f - fp) + 16)
                        wait_past(pe, z_read, 2 * EC, f - 1, 2 * EC)
                        if place:
                            pe.wait_ge(turned_read, 2 * (i - 2) + 2)
                    if c >= 2:
                        pe.wait_ge(xp_done, 2 * EC * f + 2 * (c - 1))
                    for k in range(KC):
                        last = nc.tensor.matmul(in_ps[:, c % 2, :], t.w_in[:, k, c * P:(c + 1) * P],
                                                x_t[:, fp, k, :], start=(k == 0), stop=(k == KC - 1))
                    last.then_inc(inproj_done, 1)

                def ssm_projection():
                    pe.wait_ge(silu_done, f + 1)
                    pe.wait_ge(xp_done, 2 * EC * (f + 1))
                    for c in range(EC):
                        last = nc.tensor.matmul(in_ps[:, 0, :], t.w_xdt[:, c, :], xc[:, fp, c, :],
                                                start=(c == 0), stop=(c == EC - 1))
                    last.then_inc(z_done, 1)
                    if place:
                        pe.wait_ge(logit_done, i - 1)
                    for c in range(EC):
                        last = nc.tensor.matmul(aux_ps[0:2 * STATE, :], t.w_x[:, c, :], xc[:, fp, c, :],
                                                start=(c == 0), stop=(c == EC - 1))
                    last.then_inc(ssm_ps_done, 1)

                def skip_terms(m):
                    c = m % EC
                    if m < KC * EC:
                        k = m // EC
                        nc.tensor.matmul(y_ps[:, c, :], t.w_in[:, k, INNER + c * P:INNER + (c + 1) * P],
                                         x_t[:, par, k, :], start=False, stop=False)
                    else:
                        nc.tensor.matmul(y_ps[:, c, :], t.diag_d[:, c, :], xc[:, par, c, :],
                                         start=False, stop=False)

                def sum_states(n):
                    wait_hc(pe, i, n)
                    if n == 0:
                        wait_past(pe, ys_done, 1, i - 1, 1)
                    for c in range(EC):
                        last = nc.tensor.matmul(y_ps[:, c, :], t.ident[:], prod[:, n % P_RING, c, :],
                                                start=(n == 0), stop=(n == STATE - 1))
                    last.then_inc(sum_done, 1)

                def out_projection(j):
                    if j == 0:
                        pe.wait_ge(ys_done, r + 1)
                    if j == 2:
                        pe.wait_ge(pre_done, TT * r + 2)
                    if j == 0:
                        wait_past(pe, pre_done, TT, r - 1, TT)
                        wait_past(pe, rank_read, 1, i - 3, 1)
                    for c in range(EC):
                        last = nc.tensor.matmul(out_ps[:, j % 2, :], ys[:, c, j * P:(j + 1) * P],
                                                t.w_out[:, c, :], start=(c == 0), stop=(c == EC - 1))
                    if j % 2 == 1:
                        last.then_inc(outproj_done, 1)

                def turn(h):
                    if h == 0:
                        pe.wait_ge(x1_done, TT * r + TT)
                    elif front:
                        pe.wait_ge(ssm_done, f + 1)
                    elif place:
                        pe.wait_ge(logit_done, i - 1)
                    for jj in range(2):
                        for k in range(KC):
                            at = (jj * KC + k) * P
                            dst = in_ps[:, 1, at:at + P] if h == 0 else aux_ps[:, at:at + P]
                            last = nc.tensor.transpose(dst, xrow[:, 1 - par, 2 * h + jj, k * P:(k + 1) * P],
                                                       t.ident[:])
                    last.then_inc(turned, 1)

                def logits():
                    pe.wait_ge(turned_read, 2 * (i - 2) + 2)
                    for j in range(TT):
                        for k in range(KC):
                            last = nc.tensor.matmul(aux_ps[:, j * EXPERTS:(j + 1) * EXPERTS], x1_t[:, j, k, :],
                                                    t.router[:, k, :], start=(k == 0), stop=(k == KC - 1))
                    last.then_inc(logit_ps_done, 1)

                def ranks():
                    pe.wait_ge(member_done, i - 1)
                    if back:
                        pe.wait_ge(pre_done, TT * r + TT)
                    flat = member[:].rearrange("p j e -> p (j e)")
                    dst = out_ps[:].rearrange("p h n -> p (h n)")
                    nc.tensor.matmul(dst[:, 0:(TT + 1) * EXPERTS], t.before[:], flat, start=True, stop=False)
                    for k in range(TT):
                        n_after = TT - k
                        last = nc.tensor.matmul(
                            dst[:, (k + 1) * EXPERTS:(TT + 1) * EXPERTS].rearrange("p (j e) -> p j e", e=EXPERTS),
                            t.ones[:], member[:, k:k + 1, :].broadcast_to([P, n_after, EXPERTS]),
                            start=False, stop=(k == TT - 1))
                    last.then_inc(rank_ps_done, 1)

                for n in range(STATE):
                    if place and n == 0:
                        logits()
                    if scans:
                        sum_states(n)
                        if 1 <= n <= 12:
                            skip_terms(n - 1)
                    if front:
                        if n <= 3:
                            in_projection(n)
                        if n == 8:
                            ssm_projection()
                    if back:
                        if n == 2 or n == 6:
                            out_projection(0 if n == 2 else 2)
                            out_projection(1 if n == 2 else 3)
                    if place and n == 9:
                        ranks()
                    if back:
                        if n == 13:
                            turn(0)
                            turn(1)

            steps(pe, step)

        @block.scalar
        def _(act):
            def step(i, half, scans, front, back, place):
                f, r, fp, par = i + 1, i - 1, 1 - half, half

                def halo():
                    wait_past(act, tap_done, (TAPS - 1) * EC, f - 1, (TAPS - 1) * EC)
                    wait_past(act, dt_done, 1, f - 1, 1)
                    src = t.xp[:, :, T:T + TAPS - 1] if fp == 1 else t.zeros[:, :, 0:TAPS - 1]
                    nc.scalar.copy(t.xp[:, :, 0:TAPS - 1], src).then_inc(halo_done, 1)

                def xp_out(c):
                    act.wait_ge(inproj_done, EC * f + c + 1)
                    if c == 0:
                        act.wait_ge(halo_done, f + 1)
                        wait_past(act, sum_done, STATE, f - 2, STATE)
                    nc.scalar.activation(xc[:, fp, c, :], in_ps[:, c % 2, :], ACT.Identity,
                                         bias=t.conv_b[:, c:c + 1], scale=t.conv_w[:, c, TAPS - 1:TAPS])\
                        .then_inc(xp_done, 1)
                    nc.scalar.copy(t.xp[:, c, TAPS - 1:], in_ps[:, c % 2, :]).then_inc(xp_done, 1)

                def silu():
                    act.wait_ge(tap_done, (TAPS - 1) * EC * (f + 1))
                    nc.scalar.activation(xc[:, fp], xc[:, fp], ACT.Silu).then_inc(silu_done, 1)

                def ssm_out():
                    act.wait_ge(ssm_ps_done, f + 1)
                    wait_past(act, bc_stored, 16, f - 1, 16)
                    nc.scalar.copy(ssm[:], aux_ps[0:2 * STATE, :]).then_inc(ssm_done, 1)
                    act.wait_ge(ssm_done, f + 1)
                    hold(act, held_act)
                    act.dma_start(d.bc[f], ssm[:]).then_inc(bc_stored, 16)

                def normed():
                    act.wait_ge(rstd_done, 2 * (r + 1))
                    for j in range(TT):
                        nc.scalar.activation(xrow[:, 1 - half, j, 0:DIM], xrow[:, 1 - half, j, 0:DIM], ACT.Identity,
                                             bias=shift[:, j:j + 1], scale=rstd[:, j:j + 1]).then_inc(x1_done, 1)

                def store_x1():
                    act.wait_ge(x1_done, TT * r + TT)
                    hold(act, held_act)
                    act.dma_start(d.x1[r], xrow[:, 1 - half, :, 0:DIM]).then_inc(x1_stored[1 - half], 16)

                def z_parts(c):
                    act.wait_ge(z_done, f + 1)
                    if c == 0:
                        wait_past(act, decay_done, STATE, f - 2, STATE)
                    nc.scalar.activation(t.xp[:, c, 0:T], in_ps[:, 0, :], ACT.Abs,
                                         bias=t.b_dt[:, c:c + 1], scale=t.w_dt[:, c:c + 1]).then_inc(z_read, 1)
                    nc.scalar.activation(dt[:, fp, c, :], in_ps[:, 0, :], ACT.Relu,
                                         bias=t.b_dt[:, c:c + 1], scale=t.w_dt[:, c:c + 1]).then_inc(z_read, 1)

                def soft_tail():
                    act.wait_ge(z_read, 2 * EC * (f + 1))
                    nc.scalar.activation(t.xp[:, :, 0:T], t.xp[:, :, 0:T], ACT.Exp, scale=-1.0).then_inc(ln_done, 1)
                    act.wait_ge(ln_done, 2 * f + 1)
                    nc.scalar.activation(t.xp[:, :, 0:T], t.xp[:, :, 0:T], ACT.Ln, bias=t.ones[:, 0:1])\
                        .then_inc(ln_done, 1)

                def carry_in(n):
                    wait_hc(act, *earlier(i, n, S_RING))
                    if par == 1:
                        act.wait_ge(carried_out, STATE * ((i - 1) // 2) + n + 1 if isinstance(i, int)
                                    else 8 * (i - 1) + n + 1)
                    src = carry[:, n, :].unsqueeze(2) if par == 1 else t.zeros[:, :, 0:1]
                    nc.scalar.copy(scan[:, n % S_RING, :, 0:1], src).then_inc(carried_in, 1)

                def carry_out(n):
                    act.wait_ge(scan_done, STATE * i + n + 1)
                    nc.scalar.copy(carry[:, n, :].unsqueeze(2), scan[:, n % S_RING, :, T:T + 1])\
                        .then_inc(carried_out, 1)

                def decays(n):
                    if n == 0:
                        act.wait_ge(dt_done, i + 1)
                    wait_past(act, scan_done, STATE, *[(a, b + 1) for a, b in [slot_before(i, n, DA_RING)]][0])
                    nc.scalar.activation(decay[:, n % DA_RING, :, 1:], dt[:, par], ACT.Exp,
                                         scale=t.neg_a[:, n:n + 1]).then_inc(decay_done, 1)

                def y_silu():
                    act.wait_ge(sum_done, STATE * (r + 1))
                    wait_past(act, outproj_done, 2, r - 1, 2)
                    nc.scalar.activation(ys[:], y_ps[:], ACT.Silu).then_inc(ys_done, 1)

                def turned_out(h):
                    act.wait_ge(turned, 2 * (i - 2) + h + 1)
                    wait_past(act, logit_ps_done, 1, i - 3, 1)
                    nc.scalar.copy(x1_t[:, 2 * h:2 * h + 2].rearrange("p j k q -> p (j k q)"),
                                   in_ps[:, 1, :] if h == 0 else aux_ps[:])\
                        .then_inc(turned_read, 1)

                def router_exp():
                    act.wait_ge(shifted, i - 1)
                    nc.scalar.activation(ex[:], ex[:], ACT.Exp).then_inc(ex_done, 1)

                def hand_on(a, n):
                    act.wait_ge(low_done, PIECES * a + n + 1)
                    hold(act, held_act)
                    act.dma_start(d.parts[a, n], parts[:, n % 2]).then_inc(parts_stored[n % 2], 16)
                    if n + 2 < PIECES:
                        act.dma_start(raw[:, n % 2], d.pieces[a, n + 2]).then_inc(raw_loaded[n % 2], 16)
                    elif not isinstance(a, int) or a + 1 < EXPERTS:
                        act.dma_start(raw[:, n % 2], d.pieces[a + 1, n + 2 - PIECES])\
                            .then_inc(raw_loaded[n % 2], 16)

                def high_part(n):
                    act.wait_ge(raw_loaded[n % 2], 8 * PIECES * i + 16 * (n // 2) + 16)
                    if not isinstance(i, int) or PIECES * i + n >= 2:
                        act.wait_ge(parts_stored[n % 2], 8 * PIECES * i + 16 * (n // 2))
                    nc.scalar.copy(parts[:, n % 2, 0].bitcast(F32R), raw[:, n % 2]).then_inc(high_done, 1)

                for n in range(STATE):
                    if n == 0 and not scans and back:
                        hand_on(r, PIECES - 1)
                    if scans:
                        if n == 0:
                            carry_in(0)
                            decays(0)
                        if n < STATE - 1:
                            carry_in(n + 1)
                            decays(n + 1)
                        if par == 0 and n >= 2:
                            carry_out(n - 2)
                        if n >= 1:
                            hand_on(i, n - 1)
                        elif back:
                            hand_on(r, PIECES - 1)
                        high_part(n)
                    if place:
                        if n == 0:
                            turned_out(0)
                            turned_out(1)
                        if n == 6:
                            router_exp()
                    if back and n == 1:
                        y_silu()
                    if back and n == 14:
                        normed()
                    if front:
                        if n == 1:
                            halo()
                        if 4 <= n <= 7:
                            xp_out(n - 4)
                        if n == 10:
                            silu()
                        if n == 12:
                            z_parts(1)
                            z_parts(2)
                        if n == 11:
                            z_parts(0)
                        if n == 13:
                            z_parts(3)
                            ssm_out()
                            soft_tail()
                    if back and n == 15:
                        store_x1()
                if scans and par == 0:
                    carry_out(STATE - 2)
                    carry_out(STATE - 1)

            for k in range(2):
                act.sem_inc(x1_stored[k], 16)
                act.dma_start(raw[:, k], d.pieces[0, k]).then_inc(raw_loaded[k], 16)
            steps(act, step)
            store_tails(act, range(EXPERTS // 2, EXPERTS))
            for k in range(2):
                act.wait_ge(x1_stored[k], 16 * BLOCKS // 2 + 16)
                act.wait_ge(parts_stored[k], 16 * EXPERTS * PIECES // 2)

        LINKS = 11
        PLACE_LINKS = 6

        @block.vector
        def _(dve):
            def step(i, half, scans, front, back, place):
                f, r, fp, par, rp = i + 1, i - 1, 1 - half, half, 1 - half

                def tap(c, k):
                    col = TAPS - 1 - k
                    src = t.xp[:, c, col:col + T]
                    if k == 1:
                        dve.wait_ge(xp_done, 2 * EC * f + 2 * c + 2)
                    else:
                        dve.wait_ge(tap_done, (TAPS - 1) * (EC * f + c) + k - 1)
                    nc.vector.scalar_tensor_tensor(out=xc[:, fp, c, :], in0=src, scalar=t.conv_w[:, c, col:col + 1],
                                                   in1=xc[:, fp, c, :], op0=ALU.mult, op1=ALU.add)\
                        .then_inc(tap_done, 1)

                def step_sizes():
                    dve.wait_ge(ln_done, 2 * f + 2)
                    nc.vector.tensor_tensor(dt[:, fp], dt[:, fp], t.xp[:, :, 0:T], ALU.add).then_inc(dt_done, 1)
                    dve.wait_ge(dt_done, f + 1)
                    wait_dbx(dve, f - 2, STATE - 1)
                    nc.vector.tensor_tensor(u[:, fp], dt[:, fp], xc[:, fp], ALU.mult).then_inc(u_done, 1)

                def dbx(n):
                    wait_row(dve, b_loaded, i, n)
                    dve.wait_ge(carried_in, STATE * i + n + 1)
                    dve.wait_ge(u_done, i + 1)
                    nc.vector.tensor_tensor(scan[:, n % S_RING, :, 1:], u[:, par],
                                            b_row[:, n % B_RING:n % B_RING + 1, :].broadcast_to([P, EC, T]), ALU.mult)\
                        .then_inc(dbx_dve, 1)

                def hc(n):
                    wait_row(dve, c_loaded, i, n)
                    dve.wait_ge(scan_done, STATE * i + n + 1)
                    wait_past(dve, sum_done, STATE, *[(a, b + 1) for a, b in [slot_before(i, n, P_RING)]][0])
                    nc.vector.tensor_tensor(prod[:, n % P_RING], scan[:, n % S_RING, :, 1:],
                                            c_row[:, n % C_RING:n % C_RING + 1, :].broadcast_to([P, EC, T]), ALU.mult)\
                        .then_inc(hc_dve, 1)

                def recurrence(n):
                    dve.wait_ge(decay_done, STATE * i + n + 1)
                    dve.wait_ge(carried_in, STATE * i + n + 1)
                    wait_dbx(dve, i, n)
                    line = scan[:, n % S_RING].rearrange("p c t -> p (c t)")
                    nc.vector.tensor_tensor_scan(line, decay[:, n % DA_RING].rearrange("p c t -> p (c t)"), line,
                                                 0.0, ALU.mult, ALU.add).then_inc(scan_done, 1)

                def residual(j):
                    dve.wait_ge(outproj_done, 2 * r + j // 2 + 1)
                    if j == 0:
                        dve.wait_ge(xtok_loaded, 16 * (r + 1))
                        dve.wait_ge(x1_stored[rp], 8 * (r - rp) + 16)
                        dve.wait_ge(early_free, r + 1)
                    if j == 2:
                        dve.wait_ge(late_free, r + 1)
                    nc.vector.tensor_tensor(xrow[:, rp, j, 0:DIM], out_ps[:, j % 2, :], x_tok[:, j, :], ALU.add)\
                        .then_inc(pre_done, 1)

                def moments(j):
                    dve.wait_ge(pre_done, TT * r + j + 1)
                    nc.vector.bn_stats(stats[:, j, :], xrow[:, rp, j, 0:DIM]).then_inc(stats_done, 1)

                def variance():
                    dve.wait_ge(stats_done, TT * (r + 1))
                    wait_past(dve, x1_done, TT, r - 1, TT)
                    hold(dve, held_dve)
                    for j in range(TT):
                        last = nc.vector.bn_aggr(mv[:, j, :], stats[:, j, :])
                    last.then_inc(norm_chain, 1)
                    dve.wait_ge(norm_chain, 2 * r + 1)
                    nc.vector.tensor_scalar(var[:, TT:], mv[:, :, 0], -1.0, None, ALU.mult)
                    nc.vector.tensor_scalar(var[:, 0:TT], mv[:, :, 1], EPS, None, ALU.add).then_inc(norm_chain, 1)

                links, placed = [0], [0]

                def link(ins):
                    links[0] += 1
                    ins.then_inc(route, 1)
                    dve.wait_ge(route, LINKS * (i - 2) + links[0])

                def place_link(ins):
                    placed[0] += 1
                    ins.then_inc(place_chain, 1)
                    dve.wait_ge(place_chain, PLACE_LINKS * (i - 2) + placed[0])

                def router_shift():
                    dve.wait_ge(logit_ps_done, i - 1)
                    nc.vector.tensor_copy(logit[:].rearrange("p j e -> p (j e)"),
                                          aux_ps[:, 0:TT * EXPERTS]).then_inc(logit_done, 1)
                    dve.wait_ge(logit_done, i - 1)
                    link(nc.vector.tensor_reduce(mx[:], logit[:], AXX, ALU.max))
                    nc.vector.tensor_tensor(ex[:], logit[:], mx[:].unsqueeze(2).broadcast_to([P, TT, EXPERTS]),
                                            ALU.subtract).then_inc(shifted, 1)

                def router_top():
                    dve.wait_ge(ex_done, i - 1)
                    link(nc.vector.tensor_reduce(mx[:], ex[:], AXX, ALU.add))
                    link(nc.vector.reciprocal(mx[:], mx[:]))
                    link(nc.vector.tensor_tensor(ex[:], ex[:], mx[:].unsqueeze(2).broadcast_to([P, TT, EXPERTS]),
                                                 ALU.mult))
                    hold(dve, held_dve)
                    for j in range(TT):
                        last = nc.vector.max(top[:, j, :], ex[:, j, :])
                    link(last)
                    hold(dve, held_dve)
                    for j in range(TT):
                        last = nc.vector.max_index(idx[:, j, :], top[:, j, :], ex[:, j, :])
                    link(last)
                    link(nc.vector.scalar_tensor_tensor(out=mx[:], in0=top[:, :, 0], scalar=1e-9, in1=top[:, :, 1],
                                                        op0=ALU.add, op1=ALU.add))
                    link(nc.vector.reciprocal(mx[:], mx[:]))
                    link(nc.vector.tensor_tensor(wk[:], top[:, :, 0:TOPK],
                                                 mx[:].unsqueeze(2).broadcast_to([P, TT, TOPK]), ALU.mult))
                    link(nc.vector.tensor_copy(ek[:], idx[:, :, 0:TOPK]))
                    link(nc.vector.tensor_tensor(
                        onehot[:].rearrange("p j k e -> p (j k) e"),
                        t.iota_ef[:].unsqueeze(1).broadcast_to([P, TT * TOPK, EXPERTS]),
                        ek[:].rearrange("p j k -> p (j k)").unsqueeze(2).broadcast_to([P, TT * TOPK, EXPERTS]),
                        ALU.is_equal))
                    nc.vector.tensor_tensor(member[:, 0:TT], onehot[:, :, 0, :], onehot[:, :, 1, :], ALU.add)\
                        .then_inc(member_done, 1)
                    assert links[0] == LINKS, links

                def router_place():
                    dve.wait_ge(rank_ps_done, i - 1)
                    place_link(nc.vector.tensor_tensor(rank[:], out_ps[:, 0, 0:TT * EXPERTS].rearrange("p (j e) -> p j e",
                                                                                                e=EXPERTS),
                                                 t.base[:].unsqueeze(1).broadcast_to([P, TT, EXPERTS]), ALU.add))
                    nc.vector.tensor_tensor(t.base[:], t.base[:], out_ps[:, 0, TT * EXPERTS:(TT + 1) * EXPERTS],
                                            ALU.add).then_inc(rank_read, 1)
                    for k in range(TOPK):
                        place_link(nc.vector.tensor_tensor(onehot[:, :, k, :], onehot[:, :, k, :], rank[:], ALU.mult))
                    place_link(nc.vector.tensor_reduce(rk[:], onehot[:], AXX, ALU.add))
                    place_link(nc.vector.scalar_tensor_tensor(out=rk[:], in0=ek[:], scalar=float(REGION), in1=rk[:],
                                                        op0=ALU.mult, op1=ALU.add))
                    nc.vector.tensor_copy(pos[:, par], rk[:])
                    nc.vector.tensor_copy(xrow[:, par, :, DIM:DIM + 2], wk[:, :, 0:1].broadcast_to([P, TT, 2]))
                    nc.vector.tensor_copy(xrow[:, par, :, DIM + 2], wk[:, :, 1])
                    dve.wait_ge(rank_read, i - 1)
                    place_link(nc.vector.tensor_copy(xrow[:, par, :, DIM + 3], t.token2[:]))
                    nc.vector.tensor_copy(xrow[:, par, :, DIM + 1], ek[:, :, 0])
                    nc.vector.tensor_scalar(t.token2[:], t.token2[:], float(TOPK * T), None, ALU.add)\
                        .then_inc(pos_done, 1)
                    dve.wait_ge(pos_done, i - 1)
                    assert placed[0] == PLACE_LINKS, placed

                for n in range(STATE):
                    if scans:
                        if not POOL_DBX[n]:
                            dbx(n)
                        recurrence(n)
                        if n >= 1 and not POOL_HC[n - 1]:
                            hc(n - 1)
                    if place and n == 3:
                        router_shift()
                    if front:
                        if 4 <= n <= 7:
                            for k in range(1, TAPS):
                                tap(n - 4, k)
                    if back and (n == 5 or n == 9):
                        for j in range(2) if n == 5 else range(2, TT):
                            residual(j)
                        for j in range(2) if n == 5 else range(2, TT):
                            moments(j)
                    if place and n == 8:
                        router_top()
                    if back:
                        if n == 10:
                            variance()
                    if place and n == 13:
                        router_place()
                    if front and n == 14:
                        step_sizes()
                if scans and not POOL_HC[STATE - 1]:
                    hc(STATE - 1)

            def tables():
                links = [0]

                def link(ins):
                    links[0] += 1
                    ins.then_inc(chain, 1)
                    dve.wait_ge(chain, links[0])

                dve.wait_ge(made, 4)
                dve.wait_ge(sum_done, STATE * BLOCKS)
                link(nc.vector.tensor_copy(tail_f[:], tail_i[:]))
                link(nc.vector.memset(tail_row[:], 0.0))
                link(nc.vector.memset(tail_row[:, DIM + 1:DIM + 2], -1.0))
                link(nc.vector.tensor_copy(tail_row[:, DIM + 3:DIM + 4], pad_i[:]))
                link(nc.vector.tensor_tensor(tail_f[:], tail_f[:], t.base[:], ALU.add))
                nc.vector.tensor_copy(t.tail_at[:], tail_f[:]).then_inc(tails_known, 1)
                link(nc.vector.tensor_copy(thresholds[:], thresholds_i[:]))
                link(nc.vector.tensor_copy(t.slot_f[:], slot_i[:]))
                link(nc.vector.tensor_tensor(over[:], t.base[:].unsqueeze(2).broadcast_to([P, EXPERTS, MAX_J]),
                                             thresholds[:].unsqueeze(1).broadcast_to([P, EXPERTS, MAX_J]), ALU.is_gt))
                link(nc.vector.tensor_reduce(n_slots[:], over[:], AXX, ALU.add))
                link(nc.vector.tensor_tensor_scan(ends[:], t.ones[:, 0:EXPERTS], n_slots[:], 0.0, ALU.mult, ALU.add))
                link(nc.vector.tensor_tensor(passed[:], t.slot_f[:].unsqueeze(2).broadcast_to([P, SLOTS, EXPERTS]),
                                             ends[:].unsqueeze(1).broadcast_to([P, SLOTS, EXPERTS]), ALU.is_ge))
                link(nc.vector.tensor_reduce(t.slot_e[:], passed[:], AXX, ALU.add))
                link(nc.vector.tensor_tensor(passed[:], passed[:],
                                             n_slots[:].unsqueeze(1).broadcast_to([P, SLOTS, EXPERTS]), ALU.mult))
                link(nc.vector.tensor_reduce(slot_start[:], passed[:], AXX, ALU.add))
                link(nc.vector.tensor_scalar(slot_valid[:], t.slot_e[:], float(EXPERTS), None, ALU.is_lt))
                link(nc.vector.tensor_tensor(slot_start[:], t.slot_f[:], slot_start[:], ALU.subtract))
                link(nc.vector.tensor_scalar(slot_start[:], slot_start[:], float(P), None, ALU.mult))
                link(nc.vector.scalar_tensor_tensor(out=slot_start[:], in0=t.slot_e[:], scalar=float(REGION),
                                                    in1=slot_start[:], op0=ALU.mult, op1=ALU.add))
                link(nc.vector.tensor_tensor(slot_start[:], slot_start[:], slot_valid[:], ALU.mult))
                link(nc.vector.tensor_scalar(t.slot_e[:], t.slot_e[:], float(EXPERTS - 1), None, ALU.min))
                link(nc.vector.tensor_scalar(slot_valid[:], slot_valid[:], -float(EXPERTS * REGION),
                                             float(EXPERTS * REGION), ALU.mult, ALU.add))
                link(nc.vector.tensor_tensor(slot_start[:], slot_start[:], slot_valid[:], ALU.add))
                link(nc.vector.tensor_scalar(t.slot_f[:], t.slot_f[:], float(P), None, ALU.mult))
                link(nc.vector.tensor_copy(t.slot_ei[:], t.slot_e[:]))
                link(nc.vector.tensor_scalar(t.ends_i[:], ends[:], 1.0, None, ALU.add))
                link(nc.vector.tensor_copy(t.slot_row[:], slot_start[:]))

            nc.vector.memset(member[:, TT, :], 0.0)
            for k in range(DA_RING):
                nc.vector.memset(decay[:, k, :, 0:1], 0.0).then_inc(cut_done, 1)
            dve.wait_ge(cut_done, DA_RING)
            steps(dve, step)
            tables()

        @block.gpsimd
        def _(pool):
            def step(i, half, scans, front, back, place):
                f, r, par, rp = i + 1, i - 1, half, 1 - half

                def dbx(n):
                    if n == POOL_DBX.index(1):
                        pool.wait_ge(u_done, i + 1)
                    wait_row(pool, b_loaded, i, n)
                    pool.wait_ge(carried_in, STATE * i + n + 1)
                    nc.gpsimd.tensor_tensor(scan[:, n % S_RING, :, 1:], u[:, par],
                                            b_row[:, n % B_RING:n % B_RING + 1, :].broadcast_to([P, EC, T]), ALU.mult)\
                        .then_inc(dbx_pool, 1)

                def hc(n):
                    wait_row(pool, c_loaded, i, n)
                    pool.wait_ge(scan_done, STATE * i + n + 1)
                    wait_past(pool, sum_done, STATE, *[(a, b + 1) for a, b in [slot_before(i, n, P_RING)]][0])
                    nc.gpsimd.tensor_tensor(prod[:, n % P_RING], scan[:, n % S_RING, :, 1:],
                                            c_row[:, n % C_RING:n % C_RING + 1, :].broadcast_to([P, EC, T]), ALU.mult)\
                        .then_inc(hc_pool, 1)

                def rstds():
                    pool.wait_ge(norm_chain, 2 * r + 2)
                    nc.gpsimd.tensor_tensor(rstd[:], var[:, 0:TT], t.minus_half[:], ALU.pow).then_inc(rstd_done, 1)
                    pool.wait_ge(rstd_done, 2 * r + 1)
                    nc.gpsimd.tensor_tensor(shift[:], var[:, TT:], rstd[:], ALU.mult).then_inc(rstd_done, 1)

                def low_part(a, n):
                    pool.wait_ge(high_done, PIECES * a + n + 1)
                    nc.gpsimd.tensor_tensor(parts[:, n % 2, 1].bitcast(F32R), raw[:, n % 2], parts[:, n % 2, 0],
                                            ALU.subtract).then_inc(low_done, 1)

                def send_rows(b, k, j):
                    if j == 0:
                        pool.wait_ge(pos_done, b + 1)
                        pool.wait_ge(x1_done, TT * (b + 1))
                        hold(pool, held_pool)
                    for c in range(TOPK):
                        pool.indirect_dma_start(
                            out=d.rows, out_offset=bass.IndirectOffsetOnAxis(ap=pos[:, k, j, c:c + 1], axis=0),
                            in_=xrow[:, k, j, :], in_offset=None)\
                            .then_inc((early_sent if j < TT // 2 else late_sent)[k], 16)

                def sent(sems, free):
                    pool.wait_ge(sems[rp], 4 * TT * TOPK * (i - 3 - rp) + 8 * TT * TOPK)
                    pool.sem_inc(free, 1)

                if isinstance(i, int) and i == BLOCKS + 1:
                    pool.wait_ge(sum_done, STATE * BLOCKS)
                    for out, pattern, base, channel in ((thresholds_i, [[P, MAX_J]], 0, 0), (slot_i, [[1, SLOTS]], 0, 0),
                                                        (tail_i, [[REGION, EXPERTS]], 0, 0), (pad_i, [[0, 1]], TRASH - 1, 1)):
                        nc.gpsimd.iota(out, pattern=pattern, base=base, channel_multiplier=channel).then_inc(made, 1)
                for n in range(STATE):
                    if scans:
                        if POOL_DBX[n]:
                            dbx(n)
                        if n >= 1 and POOL_HC[n - 1]:
                            hc(n - 1)
                    if (scans and n >= 1) or (n == 0 and back):
                        low_part(*earlier(i, n, 1))
                    if not isinstance(i, int) or i >= 3:
                        if n == 2:
                            sent(early_sent, early_free)
                        if n == 5:
                            send_rows(i - 3, rp, 2)
                        if n == 6:
                            send_rows(i - 3, rp, 3)
                        if n == 7:
                            sent(late_sent, late_free)
                    if back and n == 12:
                        rstds()
                    if place and n >= 14:
                        send_rows(i - 2, par, n - 14)
                if scans and POOL_HC[STATE - 1]:
                    hc(STATE - 1)

            pool.sem_inc(early_free, 2)
            pool.sem_inc(late_free, 2)
            steps(pool, step)
            for j in range(2, TT):
                for c in range(TOPK):
                    pool.indirect_dma_start(
                        out=d.rows, out_offset=bass.IndirectOffsetOnAxis(ap=pos[:, 1, j, c:c + 1], axis=0),
                        in_=xrow[:, 1, j, :], in_offset=None).then_inc(late_sent[1], 16)
            for k in range(2):
                pool.wait_ge(early_sent[k], 8 * TT * TOPK * BLOCKS // 2)
                pool.wait_ge(late_sent[k], 8 * TT * TOPK * BLOCKS // 2)


def experts(nc, d, t):
    with ExitStack() as ctx:
        def sb(name, shape, dt=F32):
            return ctx.enter_context(nc.sbuf_tensor(name, shape, dt))

        def ps(name, shape):
            return ctx.enter_context(nc.psum_tensor(name, shape, F32))

        def sem(name):
            return ctx.enter_context(nc.semaphore(name))

        b1 = sb("b1", [P, EXPERTS, FF])
        b2 = sb("b2", [P, EXPERTS, DIM])
        FC = FF // P
        tags = sb("tags", [P, Y_RING, 6])
        dest = sb("dest", [P, Y_RING], U32)
        xg = sb("xg", [P, X_RING, ROW])
        xg_t = sb("xg_t", [P, 2, 2, KC, P], F32R)
        h = sb("h", [P, FF])
        h_t = sb("h_t", [P, FC, P])
        h_parts = sb("h_parts", [P, 2, FC, P], F32R)
        y = sb("y", [P, Y_RING, DIM])

        xt_ps = ps("xt_ps", [P, T])
        h_ps = ps("h_ps", [P, 2, T])
        ht_ps = ps("ht_ps", [P, FC, P])
        y_ps2 = ps("y_ps2", [P, 2, T])

        w_r = t.w.bitcast(F32R)
        w_loaded = [sem(f"w_loaded{e}") for e in range(EXPERTS)]
        w_ready = sem("w_ready")
        x_loaded = [sem(f"x_loaded{k}") for k in range(X_RING)]
        xt_done = sem("xt_done")
        x_high = sem("x_high")
        x_low = sem("x_low")
        h_ps_done = sem("h_ps_done")
        h_done = sem("h_done")
        ht_ps_done = sem("ht_ps_done")
        gelu_done = sem("gelu_done")
        h_high = sem("h_high")
        h_low = sem("h_low")
        y_ps_done = sem("y_ps_done")
        y_biased = sem("y_biased")
        y_done = sem("y_done")
        tag_chain = sem("tag_chain")
        y_sent = [sem(f"y_sent{k}") for k in range(Y_RING)]
        y_free = sem("y_free")
        x1_loaded = sem("x1_loaded")
        held_sp, held_pool = sem("held_sp2"), sem("held_pool2")
        block = ctx.enter_context(nc.Block())
        HALF = FF // 2
        PRODUCTS = ((0, 0), (0, 1), (1, 0))

        def wait_x(eng, s, k):
            eng.wait_ge(x_loaded[k], (16 // X_RING) * (s - k) + 16)

        @block.sync
        def _(sp):
            def load_expert(e):
                sp.dma_start(b1[:, e], d.b1[e].partition_broadcast(P)).then_inc(w_loaded[e], 16)
                sp.dma_start(b2[:, e], d.b2[e].partition_broadcast(P)).then_inc(w_loaded[e], 16)
                loads = W_LOADS if e > 0 else 0
                for m in range(loads):
                    lo, hi = m * PIECES // W_LOADS, (m + 1) * PIECES // W_LOADS
                    sp.wait_ge(w_loaded[e], 16 * (m + 2))
                    sp.dma_start(t.w[:, e % W_RING, lo:hi].rearrange("p q h n -> p q (h n)"),
                                 d.parts[e, lo:hi].rearrange("q p h n -> p q (h n)")).then_inc(w_loaded[e], 16)
                sp.wait_ge(w_loaded[e], 16 * (loads + 2))
                sp.sem_inc(w_ready, 1)

            load_expert(0)
            for k in range(X_RING):
                sp.wait_ge(x_loaded[k], 16)
            for e in range(1, W_RING):
                load_expert(e)
            for b in range(BLOCKS):
                sp.dma_start(t.x1[:, b], d.x1[b]).then_inc(x1_loaded, 16)
                sp.wait_ge(x1_loaded, 16 * (b + 1))
            for e in range(W_RING, EXPERTS):
                end = sp.value_load(t.ends_i[0:1, e - W_RING:e - W_RING + 1], min_val=1, max_val=SLOTS + 1)
                sp.wait_ge(y_ps_done, end)
                hold(sp, held_sp)
                load_expert(e)

        @block.gpsimd
        def _(pool):
            pool.sem_inc(y_free, Y_RING)

            def load_x(s, k):
                if not isinstance(s, int) or s >= X_RING:
                    pool.wait_ge(xt_done, s - (X_RING - 1))
                    pool.wait_ge(tag_chain, 4 * (s - X_RING) + 4)
                    hold(pool, held_pool)
                row = pool.value_load(t.slot_row[0:1, bass.ds(s, 1)], min_val=0, max_val=EXPERTS * REGION)
                pool.dma_start(xg[:, k], d.rows[bass.ds(row, P), :]).then_inc(x_loaded[k], 16)

            for s in range(X_RING):
                load_x(s, s)

            def send(s, k):
                if not isinstance(s, int) or s >= Y_RING:
                    pool.wait_ge(y_sent[k], (16 // Y_RING) * (s - k))
                    pool.sem_inc(y_free, 1)
                pool.wait_ge(y_done, s + 1)
                hold(pool, held_pool)
                pool.indirect_dma_start(out=d.y, out_offset=bass.IndirectOffsetOnAxis(ap=dest[:, k:k + 1], axis=0),
                                        in_=y[:, k, :], in_offset=None).then_inc(y_sent[k], 16)

            for s in range(X_RING):
                send(s, s % Y_RING)
                load_x(s + X_RING, s)
            with nc.Fori(1, SLOTS // X_RING - 1, engines=(pool.engine,), hint_back_edge=True) as q:
                for m in range(X_RING):
                    send(X_RING * q + m, m % Y_RING)
                    load_x(X_RING * q + (m + X_RING), m)
            for s in range(X_RING * (SLOTS // X_RING - 1), SLOTS):
                send(s, s % Y_RING)
                if s + X_RING < SLOTS:
                    load_x(s + X_RING, s % X_RING)
            for k in range(Y_RING):
                pool.wait_ge(y_sent[k], 16 * len(range(k, SLOTS, Y_RING)))

        @block.scalar
        def _(act):
            def read_xt(s, k):
                act.wait_ge(xt_done, s + 1)
                if not isinstance(s, int) or s >= 2:
                    act.wait_ge(h_ps_done, 2 * (s - 1))
                nc.scalar.copy(xg_t[:, k, 0].rearrange("p k q -> p (k q)"), xt_ps[:, 0:KC * P]).then_inc(x_high, 1)

            def gelu(s):
                for g in range(2):
                    act.wait_ge(ht_ps_done, 2 * s + g + 1)
                    if g == 0 and (not isinstance(s, int) or s >= 1):
                        act.wait_ge(y_ps_done, s + 1)
                    lo, hi = g * FC // 2, (g + 1) * FC // 2
                    nc.scalar.activation(h_t[:, lo:hi, :], ht_ps[:, lo:hi, :], ACT.Gelu).then_inc(gelu_done, 1)
                    act.wait_ge(gelu_done, 2 * s + g + 1)
                    nc.scalar.copy(h_parts[:, 0, lo:hi, :], h_t[:, lo:hi, :]).then_inc(h_high, 1)

            read_xt(0, 0)
            read_xt(1, 1)
            gelu(0)
            read_xt(2, 0)
            with nc.Fori(0, SLOTS // 2 - 2, engines=(act.engine,), hint_back_edge=True) as q:
                gelu(2 * q + 1)
                read_xt(2 * q + 3, 1)
                gelu(2 * q + 2)
                read_xt(2 * q + 4, 0)
            for s in range(2 * (SLOTS // 2) - 3, SLOTS):
                gelu(s)
                if s + 2 < SLOTS:
                    read_xt(s + 2, s % 2)

        @block.tensor
        def _(pe):
            def turn_x(s, k):
                wait_x(pe, s, k)
                if not isinstance(s, int) or s >= 1:
                    pe.wait_ge(x_low, s)
                for c in range(KC):
                    last = nc.tensor.transpose(xt_ps[:, c * P:(c + 1) * P], xg[:, k, c * P:(c + 1) * P], t.ident[:])
                last.then_inc(xt_done, 1)

            def expert_of(s):
                return pe.value_load(t.slot_ei[0:1, bass.ds(s, 1)], min_val=0, max_val=EXPERTS - 1)

            def up(s, k, e, after=None):
                pe.wait_ge(w_ready, e + 1)
                pe.wait_ge(x_low, s + 1)
                e_after = None
                for g in range(2):
                    if not isinstance(s, int) or s >= 1:
                        pe.wait_ge(h_done, 2 * s - 1 + g)
                    for c in range(KC):
                        q = (c * FF + g * HALF) // PW
                        for m, (xp, wp) in enumerate(PRODUCTS):
                            last = nc.tensor.matmul(h_ps[:, g, :].rearrange("p (q n) -> p q n", n=PW),
                                                    xg_t[:, k % 2, xp, c, :],
                                                    w_r[:, bass.ds(e % W_RING, 1), q:q + HALF // PW, wp, :].squeeze(1),
                                                    start=(c == 0 and m == 0), stop=(c == KC - 1 and m == 2))
                    last.then_inc(h_ps_done, 1)
                    if g == 0 and after is not None:
                        e_after = expert_of(after)
                return e_after

            def turn_h(s):
                for g in range(2):
                    pe.wait_ge(h_done, 2 * s + g + 1)
                    if not isinstance(s, int) or s >= 1:
                        pe.wait_ge(gelu_done, 2 * s - 1 + g)
                    for j in range(g * FC // 2, (g + 1) * FC // 2):
                        last = nc.tensor.transpose(ht_ps[:, j, :], h[:, j * P:(j + 1) * P], t.ident[:])
                    last.then_inc(ht_ps_done, 1)

            def down(s, k, e):
                pe.wait_ge(y_biased, s)
                for j in range(FC):
                    if j % (FC // 2) == 0:
                        pe.wait_ge(h_low, 2 * s + 1 + j // (FC // 2))
                    for m, (hp, wp) in enumerate(PRODUCTS):
                        last = nc.tensor.matmul(y_ps2[:, k % 2, 0:DIM], h_parts[:, hp, j, :],
                                                w_r[:, bass.ds(e % W_RING, 1), PIECES // 2 + j, wp, :].squeeze(1),
                                                start=(j == 0 and m == 0), stop=(j == FC - 1 and m == 2))
                last.then_inc(y_ps_done, 1)

            def slot(s, k, e, e_next, turn=True, first=True, last=False):
                e_after = None
                turn_h(s)
                if turn:
                    turn_x(s + 2, (k + 2) % X_RING)
                if first:
                    e_after = up(s + 1, (k + 1) % X_RING, e_next, after=None if last else s + 2)
                down(s, k, e)
                return e_after

            pe.sem_inc(y_ps_done, 1)
            turn_x(0, 0)
            turn_x(1, 1)
            e = expert_of(0)
            e_next = up(0, 0, e, after=1)
            e, e_next = e_next, slot(0, 0, e, e_next)
            slot(1, 1, e, e_next, last=True)
            with nc.Fori(0, (SLOTS - 4) // X_RING, engines=(pe.engine,), hint_back_edge=True) as q:
                e, e_next = expert_of(X_RING * q + 2), expert_of(X_RING * q + 3)
                for m in range(X_RING):
                    e, e_next = e_next, slot(X_RING * q + (2 + m), (2 + m) % X_RING, e, e_next, last=(m == X_RING - 1))
            left = 2 + (SLOTS - 4) // X_RING * X_RING
            e, e_next = expert_of(left), expert_of(left + 1)
            for s in range(left, SLOTS):
                last = s + 2 >= SLOTS
                e, e_next = e_next, slot(s, s % X_RING, e, e_next, turn=not last, first=(s + 1 < SLOTS), last=last)

        @block.vector
        def _(dve):
            def tag(s, x):
                k = x % Y_RING
                wait_x(dve, s, x)
                dve.wait_ge(y_free, s + 1)
                e0 = xg[:, x, DIM + 1:DIM + 2]
                nc.vector.tensor_tensor(tags[:, k, 0:1], e0, t.slot_e[:, bass.ds(s, 1)], ALU.is_equal)
                nc.vector.tensor_tensor(tags[:, k, 1:2], e0, t.slot_e[:, bass.ds(s, 1)], ALU.not_equal)
                nc.vector.tensor_scalar(tags[:, k, 4:5], e0, 0.0, t.slot_f[:, bass.ds(s, 1)], ALU.is_lt, ALU.mult)\
                    .then_inc(tag_chain, 1)
                dve.wait_ge(tag_chain, 4 * s + 1)
                nc.vector.tensor_tensor(tags[:, k, 2:3], xg[:, x, DIM:DIM + 1], tags[:, k, 0:1], ALU.mult)
                nc.vector.tensor_tensor(tags[:, k, 5:6], xg[:, x, DIM + 3:DIM + 4], tags[:, k, 1:2], ALU.add)\
                    .then_inc(tag_chain, 1)
                dve.wait_ge(tag_chain, 4 * s + 2)
                nc.vector.tensor_tensor(dest[:, k:k + 1], tags[:, k, 5:6], tags[:, k, 4:5], ALU.add)\
                    .then_inc(tag_chain, 1)
                nc.vector.scalar_tensor_tensor(out=tags[:, k, 3:4], in0=xg[:, x, DIM + 2:DIM + 3],
                                               scalar=tags[:, k, 1:2], in1=tags[:, k, 2:3], op0=ALU.mult,
                                               op1=ALU.add).then_inc(tag_chain, 1)

            def expert_of(s):
                return dve.value_load(t.slot_ei[0:1, bass.ds(s, 1)], min_val=0, max_val=EXPERTS - 1)

            def bias_h(s, e):
                for g in range(2):
                    dve.wait_ge(h_ps_done, 2 * s + g + 1)
                    if not isinstance(s, int) or s >= 1:
                        dve.wait_ge(ht_ps_done, 2 * s - 1 + g)
                    nc.vector.tensor_tensor(h[:, g * HALF:(g + 1) * HALF], h_ps[:, g, :],
                                            b1[:, bass.ds(e, 1), g * HALF:(g + 1) * HALF].squeeze(1),
                                            ALU.add).then_inc(h_done, 1)

            def x_rest(s, k):
                dve.wait_ge(x_high, s + 1)
                nc.vector.tensor_tensor(xg_t[:, k, 1].rearrange("p k q -> p (k q)"), xt_ps[:, 0:KC * P],
                                        xg_t[:, k, 0].rearrange("p k q -> p (k q)").bitcast(F32), ALU.subtract)\
                    .then_inc(x_low, 1)

            def h_rest(s):
                for g in range(2):
                    dve.wait_ge(h_high, 2 * s + g + 1)
                    lo, hi = g * FC // 2, (g + 1) * FC // 2
                    nc.vector.tensor_tensor(h_parts[:, 1, lo:hi, :], h_t[:, lo:hi, :],
                                            h_parts[:, 0, lo:hi, :].bitcast(F32), ALU.subtract).then_inc(h_low, 1)

            def bias_y(s, k, e):
                dve.wait_ge(y_ps_done, s + 2)
                nc.vector.tensor_tensor(y[:, k, :], y_ps2[:, k % 2, 0:DIM], b2[:, bass.ds(e, 1), :].squeeze(1),
                                        ALU.add).then_inc(y_biased, 1)
                dve.wait_ge(y_biased, s + 2)
                dve.wait_ge(tag_chain, 4 * s + 4)
                nc.vector.tensor_scalar(y[:, k, :], y[:, k, :], tags[:, k, 3:4], None, ALU.mult)\
                    .then_inc(y_done, 1)

            dve.sem_inc(y_biased, 1)
            x_rest(0, 0)
            x_rest(1, 1)
            bias_h(0, expert_of(0))

            def slot(s, k, turn=True, first=True):
                e = expert_of(s)
                if first:
                    e_next = expert_of(s + 1)
                h_rest(s)
                if turn:
                    x_rest(s + 2, k % 2)
                tag(s, k)
                if first:
                    bias_h(s + 1, e_next)
                bias_y(s, k % Y_RING, e)

            slot(0, 0)
            slot(1, 1)
            with nc.Fori(0, (SLOTS - 4) // X_RING, engines=(dve.engine,), hint_back_edge=True) as q:
                for m in range(X_RING):
                    slot(X_RING * q + (2 + m), (2 + m) % X_RING)
            for s in range(2 + (SLOTS - 4) // X_RING * X_RING, SLOTS):
                slot(s, s % X_RING, turn=(s + 2 < SLOTS), first=(s + 1 < SLOTS))


def combine(nc, d, t):
    with ExitStack() as ctx:
        G = 2
        N = TOKENS // P // G
        B = 8
        ye = ctx.enter_context(nc.sbuf_tensor("c_y", [P, B, G, TOPK, DIM], F32))
        o = ctx.enter_context(nc.sbuf_tensor("c_o", [P, B, G, DIM], F32))
        stats = ctx.enter_context(nc.sbuf_tensor("c_stats", [P, G, 6], F32))
        mv = ctx.enter_context(nc.sbuf_tensor("c_mv", [P, G, 2], F32))
        var = ctx.enter_context(nc.sbuf_tensor("c_var", [P, B, 2, G], F32))
        rstd = ctx.enter_context(nc.sbuf_tensor("c_rstd", [P, B, 2, G], F32))
        sem = lambda name: ctx.enter_context(nc.semaphore(name))
        loaded = [sem(f"c_loaded{k}") for k in range(B)]
        stored = [sem(f"c_stored{k}") for k in range(B)]
        added = sem("c_added")
        chain = sem("c_chain")
        rstd_done = sem("c_rstd_done")
        o_done = sem("c_o_done")
        block = ctx.enter_context(nc.Block())
        y_v = d.y[0:TRASH, :].rearrange("(i p k) n -> p i k n", p=P, k=TOPK)
        o_v = d.out.rearrange("(i p) n -> p i n", p=P)

        @block.sync
        def _(sp):
            for m in range(N):
                if m >= B:
                    sp.wait_ge(added, m - B + 1)
                sp.dma_start(ye[:, m % B], y_v[:, G * m:G * m + G]).then_inc(loaded[m % B], 16)

        @block.gpsimd
        def _(pool):
            def add(m):
                pool.wait_ge(loaded[m % B], 16 * (m // B + 1))
                if m >= B:
                    pool.wait_ge(stored[m % B], 16 * (m // B))
                nc.gpsimd.tensor_tensor(o[:, m % B], ye[:, m % B, :, 0, :], ye[:, m % B, :, 1, :], ALU.add)\
                    .then_inc(added, 1)

            def rstds(m):
                b = m % B
                pool.wait_ge(chain, 5 * m + 5)
                nc.gpsimd.tensor_tensor(rstd[:, b, 0], var[:, b, 0], t.minus_half[:, 0:G], ALU.pow)\
                    .then_inc(rstd_done, 1)
                pool.wait_ge(rstd_done, 2 * m + 1)
                nc.gpsimd.tensor_tensor(rstd[:, b, 1], var[:, b, 1], rstd[:, b, 0], ALU.mult)\
                    .then_inc(rstd_done, 1)

            add(0)
            add(1)
            for m in range(N):
                if m + 2 < N:
                    add(m + 2)
                rstds(m)

        @block.vector
        def _(dve):
            for m in range(N):
                b = m % B
                links = [5 * m]

                def link(ins):
                    links[0] += 1
                    ins.then_inc(chain, 1)
                    dve.wait_ge(chain, links[0])

                dve.wait_ge(added, m + 1)
                blk, j = divmod(G * m, TT)
                link(nc.vector.tensor_tensor(o[:, b], o[:, b], t.x1[:, blk, j:j + G, :], ALU.add))
                for g in range(G):
                    last = nc.vector.bn_stats(stats[:, g, :], o[:, b, g, :])
                link(last)
                for g in range(G):
                    last = nc.vector.bn_aggr(mv[:, g, :], stats[:, g, :])
                link(last)
                if m >= B:
                    dve.wait_ge(rstd_done, 2 * (m - B) + 2)
                nc.vector.tensor_scalar(var[:, b, 1], mv[:, :, 0], -1.0, None, ALU.mult).then_inc(chain, 1)
                nc.vector.tensor_scalar(var[:, b, 0], mv[:, :, 1], EPS, None, ALU.add).then_inc(chain, 1)

        @block.scalar
        def _(act):
            for m in range(N):
                b = m % B
                act.wait_ge(rstd_done, 2 * m + 2)
                for g in range(G):
                    nc.scalar.activation(o[:, b, g, :], o[:, b, g, :], ACT.Identity, bias=rstd[:, b, 1, g:g + 1],
                                         scale=rstd[:, b, 0, g:g + 1]).then_inc(o_done, 1)
                act.wait_ge(o_done, 2 * m + 2)
                act.dma_start(o_v[:, G * m:G * m + G, :], o[:, b]).then_inc(stored[b], 16)
            for k in range(B):
                act.wait_ge(stored[k], 16 * len(range(k, N, B)))


class Names:
    pass


def build(nc, d):
    assert EXPERTS == BLOCKS and PIECES == STATE and PW == DIM
    d.bc = nc.dram_tensor("bc_rows", [BLOCKS, 2 * STATE, T], F32, kind="Internal").ap()
    d.parts = nc.dram_tensor("weight_parts", [EXPERTS, PIECES, P, 2, PW], F32, kind="Internal").ap()
    d.x1 = nc.dram_tensor("x1_rows", [BLOCKS, P, TT, DIM], F32, kind="Internal").ap()
    d.rows = nc.dram_tensor("expert_rows", [EXPERTS * REGION + P, ROW], F32, kind="Internal").ap()
    d.y = nc.dram_tensor("expert_out", [TRASH + SLOTS * P, DIM], F32, kind="Internal").ap()
    t = Names()
    with ExitStack() as ctx:
        def sb(name, shape, dt=F32):
            return ctx.enter_context(nc.sbuf_tensor(name, shape, dt))

        t.ident = sb("ident", [P, P])
        t.before = sb("before", [P, P])
        t.ones = sb("ones", [P, P])
        t.minus_half = sb("minus_half", [P, TT])
        t.iota_e = sb("iota_e", [P, EXPERTS], I32)
        t.iota_ef = sb("iota_ef", [P, EXPERTS])
        t.iota_t = sb("iota_t", [P, TT], I32)
        t.token2 = sb("token2", [P, TT])
        t.base = sb("base", [P, EXPERTS])
        t.slot_f = sb("slot_f", [P, SLOTS])
        t.slot_e = sb("slot_e", [P, SLOTS])
        t.slot_ei = sb("slot_ei", [P, SLOTS], I32)
        t.slot_row = sb("slot_row", [P, SLOTS], I32)
        t.ends_i = sb("ends_i", [P, EXPERTS], I32)
        t.tail_at = sb("tail_at", [P, EXPERTS], I32)
        weights = W_RING * PIECES * 2 * PW
        t.arena = sb("arena", [P, max(weights, (S_RING + DA_RING) * EC * (T + 1) + (P_RING * EC + B_RING + C_RING) * T
                                      + 6 * PW)])
        t.w = t.arena[:, 0:weights].rearrange("p (r q h n) -> p r q h n", r=W_RING, q=PIECES, h=2)
        with ExitStack() as phase:
            def sb(name, shape, dt=F32):
                return phase.enter_context(nc.sbuf_tensor(name, shape, dt))

            t.w_in = sb("w_in", [P, KC, 2 * INNER])
            t.conv_w = sb("conv_w", [P, EC, TAPS])
            t.conv_b = sb("conv_b", [P, EC])
            t.w_x = sb("w_x", [P, EC, 2 * STATE])
            t.w_dt = sb("w_dt", [P, EC])
            t.w_xdt = sb("w_xdt", [P, EC, P])
            t.dt_col = sb("dt_col", [P, EC])
            t.b_dt = sb("b_dt", [P, EC])
            t.neg_a = sb("neg_a", [P, STATE])
            t.d_col = sb("d_col", [P, EC])
            t.diag_d = sb("diag_d", [P, EC, P])
            t.w_out = sb("w_out", [P, EC, DIM])
            t.router = sb("router", [P, KC, EXPERTS])
            t.zeros = sb("zeros", [P, EC, TAPS])
            t.xp = sb("xp", [P, EC, T + TAPS - 1])
            setup(nc, d, t)
            mamba(nc, d, t)
        t.x1 = ctx.enter_context(nc.sbuf_tensor("x1", [P, BLOCKS, TT, DIM], F32))
        experts(nc, d, t)
        combine(nc, d, t)


def kernel(L0_attn_x, L0_attn_W_in, L0_attn_conv_w, L0_attn_conv_b, L0_attn_W_x, L0_attn_W_dt, L0_attn_b_dt,
           L0_attn_A_log, L0_attn_D, L0_attn_W_out, L0_ffn_router_w, L0_ffn_expert_w1, L0_ffn_expert_b1,
           L0_ffn_expert_w2, L0_ffn_expert_b2):
    import concourse.bacc as bacc
    from concourse.bass_utils import run_bass_kernel_spmd

    def lay(a):
        return np.ascontiguousarray(a)

    def columns(a):
        return lay(a.reshape(EC, P, -1).transpose(1, 0, 2))

    x = np.asarray(L0_attn_x)
    w_x = np.asarray(L0_attn_W_x)
    arrays = {
        "x_t": lay(x.reshape(BLOCKS, T, KC, P).transpose(0, 3, 2, 1)),
        "x_tok": lay(x.reshape(BLOCKS, TT, P, DIM).transpose(0, 2, 1, 3)),
        "w_in": lay(np.asarray(L0_attn_W_in).T),
        "conv_w": columns(np.asarray(L0_attn_conv_w)),
        "conv_b": columns(np.asarray(L0_attn_conv_b))[:, :, 0],
        "w_x": lay(w_x[:2 * STATE].T),
        "dt_col": columns(w_x[2 * STATE])[:, :, 0],
        "w_dt": columns(np.asarray(L0_attn_W_dt))[:, :, 0],
        "b_dt": columns(np.asarray(L0_attn_b_dt))[:, :, 0],
        "a_log": lay(np.asarray(L0_attn_A_log)),
        "d_skip": columns(np.asarray(L0_attn_D))[:, :, 0],
        "w_out": lay(np.asarray(L0_attn_W_out).T),
        "router": lay(np.asarray(L0_ffn_router_w).T),
        "pieces": lay(np.concatenate([
            np.asarray(L0_ffn_expert_w1).transpose(0, 2, 1).reshape(EXPERTS, KC, P, FF // PW, PW)
            .transpose(0, 1, 3, 2, 4).reshape(EXPERTS, -1, P, PW),
            np.asarray(L0_ffn_expert_w2).transpose(0, 2, 1).reshape(EXPERTS, FF // P, P, PW)], axis=1)),
        "b1": lay(np.asarray(L0_ffn_expert_b1)),
        "b2": lay(np.asarray(L0_ffn_expert_b2)),
    }
    arrays = {f"in_{n}": lay(a) for n, a in arrays.items()}
    nc = bacc.Bacc("TRN2", target_bir_lowering=False, num_devices=1)
    d = Names()
    d.x_t = nc.dram_tensor("in_x_t", arrays["in_x_t"].shape, F32, kind="ExternalInput").ap()
    d.x_tok = nc.dram_tensor("in_x_tok", arrays["in_x_tok"].shape, F32, kind="ExternalInput").ap()
    d.w_in = nc.dram_tensor("in_w_in", arrays["in_w_in"].shape, F32, kind="ExternalInput").ap()
    d.conv_w = nc.dram_tensor("in_conv_w", arrays["in_conv_w"].shape, F32, kind="ExternalInput").ap()
    d.conv_b = nc.dram_tensor("in_conv_b", arrays["in_conv_b"].shape, F32, kind="ExternalInput").ap()
    d.w_x = nc.dram_tensor("in_w_x", arrays["in_w_x"].shape, F32, kind="ExternalInput").ap()
    d.w_dt = nc.dram_tensor("in_w_dt", arrays["in_w_dt"].shape, F32, kind="ExternalInput").ap()
    d.dt_col = nc.dram_tensor("in_dt_col", arrays["in_dt_col"].shape, F32, kind="ExternalInput").ap()
    d.b_dt = nc.dram_tensor("in_b_dt", arrays["in_b_dt"].shape, F32, kind="ExternalInput").ap()
    d.a_log = nc.dram_tensor("in_a_log", arrays["in_a_log"].shape, F32, kind="ExternalInput").ap()
    d.d_skip = nc.dram_tensor("in_d_skip", arrays["in_d_skip"].shape, F32, kind="ExternalInput").ap()
    d.w_out = nc.dram_tensor("in_w_out", arrays["in_w_out"].shape, F32, kind="ExternalInput").ap()
    d.router = nc.dram_tensor("in_router", arrays["in_router"].shape, F32, kind="ExternalInput").ap()
    d.pieces = nc.dram_tensor("in_pieces", arrays["in_pieces"].shape, F32, kind="ExternalInput").ap()
    d.b1 = nc.dram_tensor("in_b1", arrays["in_b1"].shape, F32, kind="ExternalInput").ap()
    d.b2 = nc.dram_tensor("in_b2", arrays["in_b2"].shape, F32, kind="ExternalInput").ap()
    d.out = nc.dram_tensor("out_0", (TOKENS, DIM), F32, kind="ExternalOutput").ap()
    build(nc, d)
    got = run_bass_kernel_spmd(nc, [arrays], core_ids=[0])
    return got.results[0]["out_0"].reshape(SEQS, SEQ, DIM)
```
